# Optimizing a Trainium2 kernel written in Bass

```python
import numpy as np
import jax
import jax.numpy as jnp

def _softmax(x, axis=-1):
    return jax.nn.softmax(x, axis=axis)

def _gelu(x):
    return jax.nn.gelu(x, approximate=True)

def _silu(x):
    return jax.nn.silu(x)

def _sigmoid(x):
    return jax.nn.sigmoid(x)

def _layernorm(x, axis=-1, eps=1e-05):
    m = jnp.mean(x, axis=axis, keepdims=True)
    v = jnp.var(x, axis=axis, keepdims=True)
    return (x - m) / jnp.sqrt(v + eps)

def _scatter_add(tgt, idx, src, axis=0):
    return tgt.at[idx].add(src)

def _segment_sum(src, seg, n):
    return jax.ops.segment_sum(src, seg, n)
kernel_name = 'mk_adj_ffn_d2_adj_r2_ee7126'

def setup_inputs(seed: int=0):
    np.random.seed(seed)
    _w = jnp.asarray

    def _rec_inputs():
        import jax
        import jax.numpy as jnp
        _gk = jax.random.key(seed)
        x = -0.0001117 + 0.9999 * jax.random.normal(jax.random.fold_in(_gk, 1), (64, 128, 256), jnp.float32)
        _w = (1.0 + jnp.arange(128, dtype=jnp.float32)) ** (-0.5)
        _w = _w / _w.mean()
        _pij = jnp.clip(0.0625 * _w[:, None] * _w[None, :], 0.0, 1.0)
        _a = jax.random.uniform(jax.random.fold_in(_gk, 2), (128, 128)) < _pij
        adj = _a.astype(jnp.int32)
        return (x, adj)
    x, adj = _rec_inputs()

    def _L0_gnn_setup():
        import jax, jax.numpy as jnp
        import numpy as np
        B, N, F, F1 = (512, 75, 256, 128)
        NEG = -1000000000.0
        ALPHA = 0.2
        key = jax.random.key(seed)
        k1, k2, k3, k4 = jax.random.split(key, 4)
        X = jax.random.normal(k1, (B, N, F), dtype=jnp.float32)
        A = jax.random.randint(k2, (N, N), 0, 2, dtype=jnp.int32)
        W = jax.random.normal(k3, (F, F1), dtype=jnp.float32) * (1.0 / np.sqrt(F))
        a = jax.random.normal(k4, (2, F1, 1), dtype=jnp.float32) * (1.0 / np.sqrt(F1))
        return {'X': X, 'A': A, 'W': W, 'a': a}
    _L0_gnn_all = _L0_gnn_setup()
    _L0_gnn_in = {k: v for k, v in _L0_gnn_all.items() if k in ('W', 'a')}
    del _L0_gnn_all

    def _L0_ffn_setup():
        import jax, jax.numpy as jnp
        import numpy as np
        E, TOPK, H, DK, DV, D = (4, 2, 8, 64, 64, 256)
        B, L = (4, 512)
        VDIM = H * DV

        def _silu(x):
            return x * jax.nn.sigmoid(x)

        def _l2norm(x):
            return x * jax.lax.rsqrt(jnp.sum(x * x, axis=-1, keepdims=True) + 1e-06)

        def _forward(h, Wq, Wgate, Wk, Wv, Wb, Wa, A_log, dt_bias, Wg, o_norm_weight, Wo):
            Bs, Ls, _ = h.shape
            scores = jax.nn.softmax((h @ Wgate).astype(jnp.float32), axis=-1)
            rw, sel = jax.lax.top_k(scores, TOPK)
            rw = rw / jnp.sum(rw, axis=-1, keepdims=True)
            bi = jnp.arange(Bs)[:, None, None]
            li = jnp.arange(Ls)[None, :, None]
            w_full = jnp.zeros((Bs, Ls, E), jnp.float32).at[bi, li, sel].set(rw)
            m = jnp.transpose(w_full > 0, (2, 0, 1))
            q = _l2norm(_silu(h @ Wq).reshape(Bs, Ls, H, DK))
            k = _l2norm(_silu(h @ Wk).reshape(Bs, Ls, H, DK))
            v = _silu(h @ Wv).reshape(Bs, Ls, H, DV)
            beta = jax.nn.sigmoid(h @ Wb)
            g = -jnp.exp(A_log) * jax.nn.softplus((h @ Wa).astype(jnp.float32) + dt_bias)
            beta_e = beta[None] * m[..., None]
            g_e = jnp.where(m[..., None], g[None], 0.0)
            scale = DK ** (-0.5)
            xs = (jnp.moveaxis(q, 1, 0), jnp.moveaxis(k, 1, 0), jnp.moveaxis(v, 1, 0), jnp.moveaxis(beta_e, 2, 0), jnp.moveaxis(g_e, 2, 0))

            def step(S, x):
                qt, kt, vt, bt, gt = x
                S = S * jnp.exp(gt)[..., None, None]
                kv = jnp.einsum('bhk,ebhkv->ebhv', kt, S)
                delta = (vt[None] - kv) * bt[..., None]
                S = S + kt[None, :, :, :, None] * delta[..., None, :]
                ot = jnp.einsum('bhk,ebhkv->ebhv', qt * scale, S)
                return (S, ot)
            S0 = jnp.zeros((E, Bs, H, DK, DV), jnp.float32)
            _, o = jax.lax.scan(step, S0, xs)
            o = jnp.moveaxis(o, 0, 2)
            core = jnp.einsum('ble,eblhv->blhv', w_full, o)
            gate = _silu((h @ Wg).reshape(Bs, Ls, H, DV))
            core = core * jax.lax.rsqrt(jnp.mean(core * core, axis=-1, keepdims=True) + 1e-05)
            core = core * o_norm_weight * gate
            return core.reshape(Bs, Ls, VDIM) @ Wo
        key = jax.random.key(seed)
        ks = jax.random.split(key, 12)
        std = 0.02
        h = jax.random.normal(ks[0], (B, L, D), jnp.float32)
        Wq = jax.random.normal(ks[1], (D, H * DK), jnp.float32) * std
        Wgate = jax.random.normal(ks[2], (D, E), jnp.float32) * std
        Wk = jax.random.normal(ks[3], (D, H * DK), jnp.float32) * std
        Wv = jax.random.normal(ks[4], (D, VDIM), jnp.float32) * std
        Wb = jax.random.normal(ks[5], (D, H), jnp.float32) * std
        Wa = jax.random.normal(ks[6], (D, H), jnp.float32) * std
        Wg = jax.random.normal(ks[7], (D, VDIM), jnp.float32) * std
        Wo = jax.random.normal(ks[8], (VDIM, D), jnp.float32) * std
        A = jax.random.uniform(ks[9], (H,), jnp.float32, 0.0001, 16.0)
        A_log = jnp.log(A)
        dt = jnp.exp(jax.random.uniform(ks[10], (H,), jnp.float32) * (np.float32(np.log(0.1)) - np.float32(np.log(0.001))) + np.float32(np.log(0.001)))
        dt = jnp.maximum(dt, 0.0001)
        dt_bias = dt + jnp.log(-jnp.expm1(-dt))
        o_norm_weight = jnp.ones((DV,), jnp.float32)
        return {'hidden_states': h, 'Wq': Wq, 'Wgate': Wgate, 'Wk': Wk, 'Wv': Wv, 'Wb': Wb, 'Wa': Wa, 'A_log': A_log, 'dt_bias': dt_bias, 'Wg': Wg, 'o_norm_weight': o_norm_weight, 'Wo': Wo}
    _L0_ffn_all = _L0_ffn_setup()
    _L0_ffn_in = {k: v for k, v in _L0_ffn_all.items() if k in ('Wq', 'Wgate', 'Wk', 'Wv', 'Wb', 'Wa', 'A_log', 'dt_bias', 'Wg', 'o_norm_weight', 'Wo')}
    del _L0_ffn_all

    def _L1_gnn_setup():
        import jax, jax.numpy as jnp
        import numpy as np
        D_MODEL = 256
        NUM_HEADS = 8
        D_HEAD = D_MODEL // NUM_HEADS
        B, N = (4, 1024)
        key = jax.random.key(seed)
        ks = jax.random.split(key, 10)
        s = 1.0 / np.sqrt(D_MODEL)
        inp = {'h': jax.random.normal(ks[0], (B, N, D_MODEL), dtype=jnp.float32), 'adj': jax.random.randint(ks[1], (N, N), 0, 2, dtype=jnp.int32), 'Wq': jax.random.uniform(ks[2], (D_MODEL, D_MODEL), jnp.float32, -s, s), 'bq': jax.random.uniform(ks[3], (D_MODEL,), jnp.float32, -s, s), 'Wk': jax.random.uniform(ks[4], (D_MODEL, D_MODEL), jnp.float32, -s, s), 'bk': jax.random.uniform(ks[5], (D_MODEL,), jnp.float32, -s, s), 'Wv': jax.random.uniform(ks[6], (D_MODEL, D_MODEL), jnp.float32, -s, s), 'bv': jax.random.uniform(ks[7], (D_MODEL,), jnp.float32, -s, s), 'Wo': jax.random.uniform(ks[8], (D_MODEL, D_MODEL), jnp.float32, -s, s), 'bo': jax.random.uniform(ks[9], (D_MODEL,), jnp.float32, -s, s)}
        return inp
    _L1_gnn_all = _L1_gnn_setup()
    _L1_gnn_in = {k: v for k, v in _L1_gnn_all.items() if k in ('Wq', 'bq', 'Wk', 'bk', 'Wv', 'bv', 'Wo', 'bo')}
    del _L1_gnn_all

    def _L1_ffn_setup():
        import jax, jax.numpy as jnp
        import numpy as np
        TOP_K = 2
        key = jax.random.key(seed)
        k1, k2, k3, k4 = jax.random.split(key, 4)
        B, S, d = (4, 1024, 256)
        E, H = (32, 128)
        x = jax.random.normal(k1, (B, S, d), dtype=jnp.float32)
        expert_sel = jax.random.normal(k2, (E, d), dtype=jnp.float32) / np.sqrt(d).astype(np.float32)
        keys = jax.random.normal(k3, (E, d, H), dtype=jnp.float32) / np.sqrt(d).astype(np.float32)
        values = jax.random.normal(k4, (E, H, d), dtype=jnp.float32) / np.sqrt(E * H).astype(np.float32)
        return {'x': x, 'expert_sel': expert_sel, 'keys': keys, 'values': values}
    _L1_ffn_all = _L1_ffn_setup()
    _L1_ffn_in = {k: v for k, v in _L1_ffn_all.items() if k in ('expert_sel', 'keys', 'values')}
    del _L1_ffn_all
    return {'x': x, 'adj': adj, 'L0_gnn_W': _L0_gnn_in['W'], 'L0_gnn_a': _L0_gnn_in['a'], 'L0_ffn_Wq': _L0_ffn_in['Wq'], 'L0_ffn_Wgate': _L0_ffn_in['Wgate'], 'L0_ffn_Wk': _L0_ffn_in['Wk'], 'L0_ffn_Wv': _L0_ffn_in['Wv'], 'L0_ffn_Wb': _L0_ffn_in['Wb'], 'L0_ffn_Wa': _L0_ffn_in['Wa'], 'L0_ffn_A_log': _L0_ffn_in['A_log'], 'L0_ffn_dt_bias': _L0_ffn_in['dt_bias'], 'L0_ffn_Wg': _L0_ffn_in['Wg'], 'L0_ffn_o_norm_weight': _L0_ffn_in['o_norm_weight'], 'L0_ffn_Wo': _L0_ffn_in['Wo'], 'L1_gnn_Wq': _L1_gnn_in['Wq'], 'L1_gnn_bq': _L1_gnn_in['bq'], 'L1_gnn_Wk': _L1_gnn_in['Wk'], 'L1_gnn_bk': _L1_gnn_in['bk'], 'L1_gnn_Wv': _L1_gnn_in['Wv'], 'L1_gnn_bv': _L1_gnn_in['bv'], 'L1_gnn_Wo': _L1_gnn_in['Wo'], 'L1_gnn_bo': _L1_gnn_in['bo'], 'L1_ffn_expert_sel': _L1_ffn_in['expert_sel'], 'L1_ffn_keys': _L1_ffn_in['keys'], 'L1_ffn_values': _L1_ffn_in['values']}

def reference(x, adj, L0_gnn_W, L0_gnn_a, L0_ffn_Wq, L0_ffn_Wgate, L0_ffn_Wk, L0_ffn_Wv, L0_ffn_Wb, L0_ffn_Wa, L0_ffn_A_log, L0_ffn_dt_bias, L0_ffn_Wg, L0_ffn_o_norm_weight, L0_ffn_Wo, L1_gnn_Wq, L1_gnn_bq, L1_gnn_Wk, L1_gnn_bk, L1_gnn_Wv, L1_gnn_bv, L1_gnn_Wo, L1_gnn_bo, L1_ffn_expert_sel, L1_ffn_keys, L1_ffn_values):
    import jax
    import jax.numpy as jnp

    def _L0_gnn_ref(X, A, W, a):
        import jax, jax.numpy as jnp
        import numpy as np
        B, N, F, F1 = (512, 75, 256, 128)
        NEG = -1000000000.0
        ALPHA = 0.2
        h = jnp.einsum('bnf,fo->bno', X, W)
        att_self = jnp.einsum('bno,od->bnd', h, a[0])
        att_neigh = jnp.einsum('bno,od->bnd', h, a[1])
        e = att_self + jnp.swapaxes(att_neigh, 1, 2)
        e = jax.nn.leaky_relu(e, ALPHA)
        adj = A.astype(h.dtype)
        e = e + NEG * (1.0 - adj)[None, :, :]
        alpha = jax.nn.softmax(e, axis=-1)
        out = jnp.einsum('bij,bjo->bio', alpha, h)
        return jnp.concatenate([out, h], axis=-1)

    def _L0_ffn_ref(hidden_states, Wq, Wgate, Wk, Wv, Wb, Wa, A_log, dt_bias, Wg, o_norm_weight, Wo):
        import jax, jax.numpy as jnp
        import numpy as np
        E, TOPK, H, DK, DV, D = (4, 2, 8, 64, 64, 256)
        B, L = (4, 512)
        VDIM = H * DV

        def _silu(x):
            return x * jax.nn.sigmoid(x)

        def _l2norm(x):
            return x * jax.lax.rsqrt(jnp.sum(x * x, axis=-1, keepdims=True) + 1e-06)

        def _forward(h, Wq, Wgate, Wk, Wv, Wb, Wa, A_log, dt_bias, Wg, o_norm_weight, Wo):
            Bs, Ls, _ = h.shape
            scores = jax.nn.softmax((h @ Wgate).astype(jnp.float32), axis=-1)
            rw, sel = jax.lax.top_k(scores, TOPK)
            rw = rw / jnp.sum(rw, axis=-1, keepdims=True)
            bi = jnp.arange(Bs)[:, None, None]
            li = jnp.arange(Ls)[None, :, None]
            w_full = jnp.zeros((Bs, Ls, E), jnp.float32).at[bi, li, sel].set(rw)
            m = jnp.transpose(w_full > 0, (2, 0, 1))
            q = _l2norm(_silu(h @ Wq).reshape(Bs, Ls, H, DK))
            k = _l2norm(_silu(h @ Wk).reshape(Bs, Ls, H, DK))
            v = _silu(h @ Wv).reshape(Bs, Ls, H, DV)
            beta = jax.nn.sigmoid(h @ Wb)
            g = -jnp.exp(A_log) * jax.nn.softplus((h @ Wa).astype(jnp.float32) + dt_bias)
            beta_e = beta[None] * m[..., None]
            g_e = jnp.where(m[..., None], g[None], 0.0)
            scale = DK ** (-0.5)
            xs = (jnp.moveaxis(q, 1, 0), jnp.moveaxis(k, 1, 0), jnp.moveaxis(v, 1, 0), jnp.moveaxis(beta_e, 2, 0), jnp.moveaxis(g_e, 2, 0))

            def step(S, x):
                qt, kt, vt, bt, gt = x
                S = S * jnp.exp(gt)[..., None, None]
                kv = jnp.einsum('bhk,ebhkv->ebhv', kt, S)
                delta = (vt[None] - kv) * bt[..., None]
                S = S + kt[None, :, :, :, None] * delta[..., None, :]
                ot = jnp.einsum('bhk,ebhkv->ebhv', qt * scale, S)
                return (S, ot)
            S0 = jnp.zeros((E, Bs, H, DK, DV), jnp.float32)
            _, o = jax.lax.scan(step, S0, xs)
            o = jnp.moveaxis(o, 0, 2)
            core = jnp.einsum('ble,eblhv->blhv', w_full, o)
            gate = _silu((h @ Wg).reshape(Bs, Ls, H, DV))
            core = core * jax.lax.rsqrt(jnp.mean(core * core, axis=-1, keepdims=True) + 1e-05)
            core = core * o_norm_weight * gate
            return core.reshape(Bs, Ls, VDIM) @ Wo
        return _forward(hidden_states, Wq, Wgate, Wk, Wv, Wb, Wa, A_log, dt_bias, Wg, o_norm_weight, Wo)

    def _L1_gnn_ref(h, adj, Wq, bq, Wk, bk, Wv, bv, Wo, bo):
        import jax, jax.numpy as jnp
        import numpy as np
        D_MODEL = 256
        NUM_HEADS = 8
        D_HEAD = D_MODEL // NUM_HEADS
        B, N = (4, 1024)
        b, n, _ = h.shape

        def split_heads(x):
            return x.reshape(b, n, NUM_HEADS, D_HEAD).transpose(0, 2, 1, 3)
        q = split_heads(h @ Wq.T + bq)
        k = split_heads(h @ Wk.T + bk)
        v = split_heads(h @ Wv.T + bv)
        scale = 1.0 / np.sqrt(D_HEAD)
        scores = jnp.einsum('bhqd,bhkd->bhqk', q, k) * scale
        mask = (adj == 0)[None, None, :, :]
        scores = jnp.where(mask, -jnp.inf, scores)
        attn = jax.nn.softmax(scores, axis=-1)
        out = jnp.einsum('bhqk,bhkd->bhqd', attn, v)
        out = out.transpose(0, 2, 1, 3).reshape(b, n, D_MODEL)
        return out @ Wo.T + bo

    def _L1_ffn_ref(x, expert_sel, keys, values):
        import jax, jax.numpy as jnp
        import numpy as np
        TOP_K = 2
        B, S, d = x.shape
        E = keys.shape[0]
        xt = x.reshape(-1, d)
        T = xt.shape[0]
        sel = jax.nn.sigmoid(xt @ expert_sel.T)
        sel_val, sel_idx = jax.lax.top_k(sel, TOP_K)
        w = jnp.zeros((T, E), dtype=xt.dtype).at[jnp.arange(T)[:, None], sel_idx].add(sel_val)
        h = jax.nn.relu(jnp.einsum('td,edh->teh', xt, keys))
        out = jnp.einsum('teh,te,ehv->tv', h, w, values)
        return out.reshape(B, S, -1)
    x = x + _L0_gnn_ref(_layernorm(x, axis=-1), adj, L0_gnn_W, L0_gnn_a)
    x = x + _L0_ffn_ref(_layernorm(x, axis=-1), L0_ffn_Wq, L0_ffn_Wgate, L0_ffn_Wk, L0_ffn_Wv, L0_ffn_Wb, L0_ffn_Wa, L0_ffn_A_log, L0_ffn_dt_bias, L0_ffn_Wg, L0_ffn_o_norm_weight, L0_ffn_Wo)
    x = x + _L1_gnn_ref(_layernorm(x, axis=-1), adj, L1_gnn_Wq, L1_gnn_bq, L1_gnn_Wk, L1_gnn_bk, L1_gnn_Wv, L1_gnn_bv, L1_gnn_Wo, L1_gnn_bo)
    x = x + _L1_ffn_ref(_layernorm(x, axis=-1), L1_ffn_expert_sel, L1_ffn_keys, L1_ffn_values)
    return x

_drawn_inputs = setup_inputs


def setup_inputs(seed=0):
    import zlib

    import numpy as np

    out = dict(_drawn_inputs(seed))
    spreads = {'L0_ffn_o_norm_weight': (1.0, 0.6)}
    factors = {'L0_ffn_Wb': 5.065,
     'L0_ffn_Wa': 23.507,
     'L0_ffn_A_log': 3.871,
     'L0_ffn_dt_bias': 3.15,
     'L1_gnn_bq': 8.0,
     'L1_gnn_bk': 64.0}
    for name, (base, spread) in spreads.items():
        noise = np.random.default_rng([zlib.crc32(name.encode()), seed]).standard_normal(out[name].shape)
        drawn = base * np.exp(spread * noise) if base else spread * noise
        out[name] = jnp.asarray(drawn.astype(out[name].dtype))
    for name, factor in factors.items():
        out[name] = (out[name] * factor).astype(out[name].dtype)
    return out
```

```python
from contextlib import ExitStack

import numpy as np
import concourse.bass as bass
from concourse import mybir

ALU = mybir.AluOpType
ACT = mybir.ActivationFunctionType
AX = mybir.AxisListType
F32 = mybir.dt.float32
BF16 = mybir.dt.bfloat16
I32 = mybir.dt.int32
U32 = mybir.dt.uint32

P = 128
D = 256
F1 = 128
H = 8
DK = 64
HD = H * DK
E0 = 4
TOPK = 2
R = TOPK * P
BK = 32
NB_ = P // BK
D1 = 32
E1 = 32
H1 = 128
U = 2
SMALL = E0 + 2 * H
ROWV = 2 * H + 2 * E0
LN_EPS = 1e-5
BIG = 32768.0
NEG = -1.0e9
OFF = -1.0e30


class Count:

    def __init__(self, ctx, nc, name, per, unit=1, again=False):
        self.sem = ctx.enter_context(nc.semaphore(name))
        self.per, self.unit, self.first = per, unit, int(again)

    def at(self, turn, k):
        return turn * (self.per * self.unit) + (k * self.unit + self.first)


def start_at_one(engine, counts):
    for count in counts:
        if count.first:
            engine.sem_inc(count.sem, 1)


class Chain:

    def __init__(self, count, engine, turn):
        self.count, self.engine, self.turn, self.k = count, engine, turn, 0

    def done(self, instruction):
        self.k += 1
        instruction.then_inc(self.count.sem, 1)
        self.engine.wait_ge(self.count.sem, self.count.at(self.turn, self.k))

    def close(self):
        assert self.k == self.count.per, (self.k, self.count.per)


def carry(nc, c):
    nc.vector.memset(c["pad"][:], 0.0)


def constants(nc, ctx, dram):
    def sb(name, shape, dt=F32):
        return ctx.enter_context(nc.sbuf_tensor(name, shape, dt))

    c = {
        "ident": sb("ident", [P, P]),
        "big_ident": sb("big_ident", [P, P], BF16),
        "before": sb("before", [P, P], BF16),
        "ones_bf": sb("ones_bf", [P, P], BF16),
        "ones": sb("ones", [P, P]),
        "after": sb("after", [P, P]),
        "after_block": sb("after_block", [P, P]),
        "upto": sb("upto", [P, P]),
        "upto_block": sb("upto_block", [P, BK]),
        "col_block": sb("col_block", [P, P]),
        "my_block": sb("my_block", [P, 1]),
        "in_block": sb("in_block", [P, 1]),
        "causal": sb("causal", [P, R + P]),
        "row1": sb("row1", [P, R]),
        "row0": sb("row0", [P, R]),
        "rowid": sb("rowid", [P, 2]),
        "adj_neg": sb("adj_neg", [P, P]),
        "adj_off": sb("adj_off", [P, P]),
        "adj_i": sb("adj_i", [P, P], I32),
        "adj_f": sb("adj_f", [P, P]),
        "dt_bias": sb("dt_bias", [P, H]),
        "neg_a": sb("neg_a", [P, H]),
        "a_log": sb("a_log", [P, H]),
        "norm_w": sb("norm_w", [P, DK]),
        "norm_w0": sb("norm_w0", [P, DK]),
        "pad": sb("pad", [P, 1]),
        "minus_half": sb("minus_half", [P, 2 * U * 2 * H]),
    }
    made = c["made"] = ctx.enter_context(nc.semaphore("const_made"))
    zeroed = ctx.enter_context(nc.semaphore("const_zeroed"))
    params = ctx.enter_context(nc.semaphore("params_loaded"))
    steps = ctx.enter_context(nc.semaphore("const_steps"))
    acted = ctx.enter_context(nc.semaphore("const_exp"))

    with nc.Block() as block:
        @block.sync
        def _(sp):
            sp.dma_start(c["adj_i"][:], dram["adj"]).then_inc(params, 16)
            sp.dma_start(c["dt_bias"][:], dram["L0_ffn_dt_bias"].partition_broadcast(P)).then_inc(params, 16)
            sp.dma_start(c["a_log"][:], dram["L0_ffn_A_log"].partition_broadcast(P)).then_inc(params, 16)
            sp.dma_start(c["norm_w0"][:], dram["L0_ffn_o_norm_weight"].partition_broadcast(P)).then_inc(params, 16)

        @block.gpsimd
        def _(pool):
            g = nc.gpsimd
            for name, value in (("ident", 0.0), ("big_ident", 0.0), ("before", 1.0), ("ones_bf", 1.0), ("ones", 1.0),
                                ("after", 1.0), ("upto", 1.0),
                                ("causal", -1.0), ("minus_half", -0.5)):
                last = g.memset(c[name][:], value)
            last.then_inc(zeroed, 1)
            pool.wait_ge(zeroed, 1)

            def keep(ap, pattern, base, cm, fill, op=ALU.is_ge):
                return g.affine_select(out=ap, in_=ap, pattern=pattern, compare_op=op, fill=fill,
                                       base=base, channel_multiplier=cm)

            keep(c["ident"][:], [[-1, P]], 0, 1, 1.0, ALU.not_equal)
            keep(c["big_ident"][:], [[-1, P]], 0, 1, BIG, ALU.not_equal)
            keep(c["before"][:], [[1, P]], -1, -1, 0.0)
            keep(c["after"][:], [[-1, P]], -1, 1, 0.0)
            keep(c["upto"][:], [[1, P]], 0, -1, 0.0)
            g.iota(c["col_block"][:].rearrange("p (k i) -> p k i", i=BK), [[1, NB_], [0, BK]], base=0, channel_multiplier=0,
                   allow_small_or_imprecise_dtypes=True)
            keep(c["causal"][:, 0:R], [[1, R]], 0, -1, -2.0)
            keep(c["causal"][:, R:R + P], [[1, P]], 0, -1, -2.0)
            g.iota(c["row1"][:], [[1, R]], base=1, channel_multiplier=0, allow_small_or_imprecise_dtypes=True)
            g.iota(c["row0"][:], [[1, R]], base=0, channel_multiplier=0, allow_small_or_imprecise_dtypes=True)
            g.iota(c["rowid"][:], [[P, 2]], base=0, channel_multiplier=1,
                   allow_small_or_imprecise_dtypes=True).then_inc(made, 1)

        @block.scalar
        def _(act):
            act.wait_ge(params, 64)
            nc.scalar.activation(c["neg_a"][:], c["a_log"][:], ACT.Exp).then_inc(acted, 1)

        @block.vector
        def _(dve):
            v = nc.vector
            dve.wait_ge(params, 64)
            v.tensor_scalar(c["norm_w"][:], c["norm_w0"][:], 0.5, None, ALU.mult)
            v.tensor_copy(c["adj_f"][:], c["adj_i"][:]).then_inc(steps, 1)
            dve.wait_ge(steps, 1)
            v.tensor_scalar(c["adj_neg"][:], c["adj_f"][:], -NEG, NEG, ALU.mult, ALU.add)
            v.tensor_scalar(c["adj_off"][:], c["adj_f"][:], 0.0, OFF, ALU.is_equal, ALU.mult)
            dve.wait_ge(acted, 1)
            v.tensor_scalar(c["neg_a"][:], c["neg_a"][:], -1.0, None, ALU.mult).then_inc(steps, 1)
            dve.wait_ge(steps, 2)
            dve.wait_ge(made, 1)
            v.tensor_scalar(c["my_block"][:], c["rowid"][:, 0:1], float(BK), None, ALU.is_ge).then_inc(steps, 1)
            for k in range(2, NB_):
                dve.wait_ge(steps, k + 1)
                v.scalar_tensor_tensor(c["my_block"][:], c["rowid"][:, 0:1], float(BK * k), c["my_block"][:],
                                       ALU.is_ge, ALU.add).then_inc(steps, 1)
            dve.wait_ge(steps, 5)
            v.scalar_tensor_tensor(c["in_block"][:], c["my_block"][:], -float(BK), c["rowid"][:, 0:1], ALU.mult, ALU.add)
            v.scalar_tensor_tensor(c["after_block"][:], c["col_block"][:], c["my_block"][:], c["after"][:],
                                   ALU.is_equal, ALU.mult).then_inc(steps, 1)
            dve.wait_ge(steps, 6)
            v.tensor_scalar(c["upto_block"][:], c["row0"][:, 0:BK], c["in_block"][:], None, ALU.is_ge).then_inc(steps, 1)
            dve.wait_ge(steps, 7)
    return c

A_DVE_STEPS = 69
A_POOL_STEPS = 1
C_DVE_STEPS = 4
D_DVE_STEPS = 26


def phase_rows(nc, c, dram, NB):
    TURNS = NB // U
    ctx = ExitStack()
    counts = []

    def sb(name, shape, dt=F32):
        return ctx.enter_context(nc.sbuf_tensor(name, shape, dt))

    def count(name, per, unit=1, again=False):
        counts.append(Count(ctx, nc, "a_" + name, per, unit, again))
        return counts[-1]

    with ctx:
        w0 = sb("a_w0", [P, 2, F1])
        att = sb("a_att", [P, 2])
        att_b = sb("a_att_b", [P, 2, P])
        wqkvg = sb("a_wqkvg", [P, 4, 2, HD])
        wsmall = sb("a_wsmall", [P, 2, SMALL])
        x = sb("a_x", [P, U, D])
        stats = sb("a_stats", [P, U, 6])
        mv = sb("a_mv", [P, U, 2])
        var = sb("a_var", [P, U])
        rstd = sb("a_rstd", [P, U])
        xn = sb("a_xn", [P, U, D])
        xnT = sb("a_xnT", [P, U, 2, P])
        hh = sb("a_hh", [P, U, 2, P])
        e_low = sb("a_e_low", [P, U, P])
        e_act = sb("a_e_act", [P, U, P])
        e_masked = sb("a_e_masked", [P, U, P])
        e_max = sb("a_e_max", [P, U])
        e_neg_max = sb("a_e_neg_max", [P, U])
        probs = sb("a_probs", [P, U, P])
        probsT = sb("a_probsT", [P, U, P])
        p_sum = sb("a_p_sum", [P, U])
        p_rec = sb("a_p_rec", [P, U])
        x1 = sb("a_x1", [P, U, D])
        x1nT = sb("a_x1nT", [P, U, 2, P])
        tanh = sb("a_tanh", [P, U, 4, HD])
        qk = sb("a_qk", [P, U, 2, HD])
        qk_sq = sb("a_qk_sq", [P, U, 2 * H, DK])
        ss = sb("a_ss", [P, U, 2 * H])
        rnorm = sb("a_rnorm", [P, U, 2 * H])
        vv = sb("a_vv", [P, U, HD])
        gg = sb("a_gg", [P, U, HD])
        gate = sb("a_gate", [P, U, HD])
        lmax = sb("a_lmax", [P, U])
        ez = sb("a_ez", [P, U, SMALL])
        zz = sb("a_zz", [P, U, H])
        ex = sb("a_ex", [P, U, SMALL])
        den = sb("a_den", [P, U, 2 * H + 1])
        rec = sb("a_rec", [P, U, 2 * H + 1])
        s1 = sb("a_s1", [P, U, H])
        s2 = sb("a_s2", [P, U, H])
        poly = sb("a_poly", [P, U, H])
        scores = sb("a_scores", [P, U, 8])
        top = sb("a_top", [P, U, 8])
        top_i = sb("a_top_i", [P, U, 8], U32)
        top_f = sb("a_top_f", [P, U, 8])
        sel = sb("a_sel", [P, U, E0])
        sel_bf = sb("a_sel_bf", [P, U, 2, E0], BF16)
        wun = sb("a_wun", [P, U, E0])
        wsum = sb("a_wsum", [P, U])
        wrec = sb("a_wrec", [P, U])
        tokv = sb("a_tokv", [P, U, ROWV])
        place = sb("a_place", [P, U, 2, E0])
        place1 = sb("a_place1", [P, U, E0])
        pT = sb("a_pT", [P, U, R])
        pP = sb("a_pP", [P, U, 2, P])
        eid = sb("a_eid", [P, U, R])
        from_e = sb("a_from_e", [P, U, 2, E0 + 1])
        eid_row = sb("a_eid_row", [P, U, 2])
        onehot = sb("a_onehot", [P, U, 2, E0])
        rv = sb("a_rv", [P, U, 2, ROWV])
        picked = sb("a_picked", [P, U, 2, 2, E0])
        w_act = sb("a_w_act", [P, U, 2, 2])
        rowg = sb("a_rowg", [P, U, 2, H])
        rowb = sb("a_rowb", [P, U, 2, H])
        roww = sb("a_roww", [P, U, 2])
        mask = sb("a_mask", [P, U, R + P], BF16)
        mask_c = sb("a_mask_c", [P, U, 2, BK], BF16)
        kqT = sb("a_kqT", [P, U, 2, 4, R])
        vp = sb("a_vp", [P, U, 2, HD])
        gdecay = sb("a_gdecay", [P, U, 2, H, BK])
        decay = sb("a_decay", [P, U, 2, H, BK])
        acomp = sb("a_acomp", [P, U, 2, H, BK])

        ps = ctx.enter_context(nc.psum_tensor("a_ps", [P, U, 3, 512], F32))
        ps_small = ctx.enter_context(nc.psum_tensor("a_ps_small", [P, 512], F32))
        ps_perm = ctx.enter_context(nc.psum_tensor("a_ps_perm", [P, U, 2, P], F32))
        sm_proj = ps_small[:, 0:U * SMALL].rearrange("p (u s) -> p u s", u=U)
        sm_place = ps_small[:, 64:64 + U * 2 * E0].rearrange("p (u a e) -> p u a e", u=U, a=2)
        sm_row = ps_small[:, 128:128 + U * 2 * ROWV].rearrange("p (u t s) -> p u t s", u=U, t=2)

        w_in = ctx.enter_context(nc.semaphore("a_w_in"))
        att_ready = ctx.enter_context(nc.semaphore("a_att_ready"))
        x_in = count("x_in", U, 16)
        xn_ready = count("xn_ready", 2 * U)
        var_ready = count("var_ready", 2)
        rstd_ready = count("rstd_ready", 2)
        xnT_ps = count("xnT_ps", U)
        xnT_sb = count("xnT_sb", U)
        h_ps = count("h_ps", U)
        h_sb = count("h_sb", U)
        e_ps = count("e_ps", U)
        e_ready = count("e_ready", U)
        probs_ready = count("probs_ready", U)
        pT_ps = count("probsT_ps", U)
        pT_sb = count("probsT_sb", U)
        o_ps = count("o_ps", U)
        x1_ready = count("x1_ready", U, again=True)
        x1nT_ps = count("x1nT_ps", U)
        x1nT_sb = count("x1nT_sb", U)
        small_ps = count("small_ps", U)
        ez_ready = count("ez_ready", 1)
        ex_ready = count("ex_ready", 1)
        proj_ps = count("proj_ps", 4 * U)
        tanh_ready = count("tanh_ready", 4 * U)
        proj_sb = count("proj_sb", 4 * U)
        sq_ready = count("sq_ready", U)
        ss_ready = count("ss_ready", 1)
        rnorm_ready = count("rnorm_ready", 1)
        qk_ready = count("qk_ready", U)
        gate_ready = count("gate_ready", U)
        sel_ready = count("sel_ready", 1)
        place_ps = count("place_ps", 1)
        perm_ready = count("perm_ready", U)
        rows_ps = count("rows_ps", U)
        P_sb = count("P_sb", 1)
        mask_ready = count("mask_ready", U)
        mask_c_ready = count("mask_c_ready", U)
        rowv_ready = count("rowv_ready", 1)
        perm_ps = count("perm_ps", 6 * U)
        perm_sb = count("perm_sb", 6 * U)
        gdecay_ready = count("gdecay_ready", U)
        compact_ps = count("compact_ps", U)
        decay_ready = count("decay_ready", U)
        acomp_ready = count("acomp_ready", U, again=True)
        x1_out = count("x1_out", U, 16, again=True)
        out = count("out", 9 * U, 16, again=True)
        dve_step = count("dve_step", A_DVE_STEPS)
        pool_step = count("pool_step", A_POOL_STEPS)

        with nc.Block() as block:
            @block.sync
            def _(sp):
                start_at_one(sp, counts)
                sp.dma_start(w0[:], dram["L0_gnn_W"].rearrange("(k p) f -> p k f", p=P)).then_inc(w_in, 16)
                sp.dma_start(att[:], dram["L0_gnn_a"].rearrange("a o d -> o (a d)"),
                             allow_slow_non_contiguous=True).then_inc(w_in, 16)
                for n, name in enumerate(("Wq", "Wk", "Wv", "Wg")):
                    sp.dma_start(wqkvg[:, n], dram["L0_ffn_" + name].rearrange("(k p) f -> p k f", p=P)).then_inc(w_in, 16)
                at = 0
                for name, width in (("Wgate", E0), ("Wb", H), ("Wa", H)):
                    sp.dma_start(wsmall[:, :, at:at + width],
                                 dram["L0_ffn_" + name].rearrange("(k p) f -> p k f", p=P),
                                 allow_slow_non_contiguous=True).then_inc(w_in, 16)
                    at += width
                with sp.Fori(0, TURNS) as it:
                    for u in range(U):
                        sp.wait_ge(x1_ready.sem, x1_ready.at(it, 0))
                        sp.dma_start(x[:, u], dram["x"][it * U + u]).then_inc(x_in.sem, 16)
                    for u in range(U):
                        sp.wait_ge(x1_ready.sem, x1_ready.at(it, u + 1))
                        sp.dma_start(dram["x1"][it * U + u], x1[:, u]).then_inc(x1_out.sem, 16)
                    for u in range(U):
                        b = it * U + u
                        sp.wait_ge(gate_ready.sem, gate_ready.at(it, u + 1))
                        sp.dma_start(dram["gate"][b], gate[:, u]).then_inc(out.sem, 16)
                        sp.wait_ge(mask_ready.sem, mask_ready.at(it, u + 1))
                        sp.dma_start(dram["mask"][b], mask[:, u]).then_inc(out.sem, 16)
                    sp.wait_ge(P_sb.sem, P_sb.at(it, 1))
                    sp.wait_ge(rowv_ready.sem, rowv_ready.at(it, 1))
                    for u in range(U):
                        b = it * U + u
                        sp.dma_start(dram["perm"][b], pP[:, u]).then_inc(out.sem, 16)
                        sp.dma_start(dram["rowg"][b], rowg[:, u]).then_inc(out.sem, 16)
                        sp.dma_start(dram["rowb"][b], rowb[:, u]).then_inc(out.sem, 16)
                        sp.dma_start(dram["roww"][b], roww[:, u]).then_inc(out.sem, 16)
                    sp.wait_ge(perm_sb.sem, perm_sb.at(it, 6 * U))
                    for u in range(U):
                        b = it * U + u
                        sp.dma_start(dram["vp"][b], vp[:, u]).then_inc(out.sem, 16)
                        sp.dma_start(dram["kqT"][b], kqT[:, u]).then_inc(out.sem, 16)
                    for u in range(U):
                        sp.wait_ge(acomp_ready.sem, acomp_ready.at(it, u + 1))
                        sp.dma_start(dram["acomp"][it * U + u], acomp[:, u]).then_inc(out.sem, 16)
                sp.wait_ge(x1_out.sem, x1_out.at(TURNS, 0))
                sp.wait_ge(out.sem, out.at(TURNS, 0))

            @block.tensor
            def _(pe):
                mm, tr = nc.tensor.matmul, nc.tensor.transpose
                pe.wait_ge(w_in, 16 * 9)
                pe.wait_ge(att_ready, 1)
                with pe.Fori(0, TURNS) as it:
                    for u in range(U):
                        pe.wait_ge(acomp_ready.sem, acomp_ready.at(it, 0))
                        pe.wait_ge(xn_ready.sem, xn_ready.at(it, u + 1))
                        for k in range(2):
                            last = tr(ps[:, u, 0, P * k:P * k + P], xn[:, u, P * k:P * k + P], c["ident"][:])
                        last.then_inc(xnT_ps.sem, 1)
                    for u in range(U):
                        pe.wait_ge(xnT_sb.sem, xnT_sb.at(it, u + 1))
                        for k in range(2):
                            mm(ps[:, u, 1, 0:P], xnT[:, u, k], w0[:, k], start=k == 0, stop=k == 1)
                        for k in range(2):
                            last = mm(ps[:, u, 1, P:2 * P], w0[:, k], xnT[:, u, k], start=k == 0, stop=k == 1)
                        last.then_inc(h_ps.sem, 1)
                    for u in range(U):
                        pe.wait_ge(h_sb.sem, h_sb.at(it, u + 1))
                        mm(ps[:, u, 2, 0:P], hh[:, u, 1], att_b[:, 0], start=True, stop=False)
                        mm(ps[:, u, 2, 0:P], att_b[:, 1], hh[:, u, 1], start=False, stop=True).then_inc(e_ps.sem, 1)
                    for u in range(U):
                        pe.wait_ge(probs_ready.sem, probs_ready.at(it, u + 1))
                        tr(ps[:, u, 2, P:2 * P], probs[:, u], c["ident"][:]).then_inc(pT_ps.sem, 1)
                    for u in range(U):
                        pe.wait_ge(pT_sb.sem, pT_sb.at(it, u + 1))
                        mm(ps[:, u, 2, 2 * P:3 * P], probsT[:, u], hh[:, u, 0], start=True, stop=True).then_inc(o_ps.sem, 1)
                    for u in range(U):
                        pe.wait_ge(xn_ready.sem, xn_ready.at(it, U + u + 1))
                        for k in range(2):
                            last = tr(ps[:, u, 0, 2 * P + P * k:3 * P + P * k], xn[:, u, P * k:P * k + P], c["ident"][:])
                        last.then_inc(x1nT_ps.sem, 1)
                    for u in range(U):
                        pe.wait_ge(x1nT_sb.sem, x1nT_sb.at(it, u + 1))
                        for k in range(2):
                            last = mm(sm_proj[:, u], x1nT[:, u, k], wsmall[:, k], start=k == 0, stop=k == 1)
                        last.then_inc(small_ps.sem, 1)
                    for n, bank in enumerate((1, 2, 0, 1)):
                        for u in range(U):
                            if n == 3:
                                pe.wait_ge(proj_sb.sem, proj_sb.at(it, u + 1))
                            for k in range(2):
                                last = mm(ps[:, u, bank], x1nT[:, u, k], wqkvg[:, n, k], start=k == 0, stop=k == 1)
                            last.then_inc(proj_ps.sem, 1)
                    pe.wait_ge(sel_ready.sem, sel_ready.at(it, 1))
                    for u in range(U):
                        mm(sm_place[:, u, 0], c["before"][:], sel_bf[:, u, 0], start=True, stop=False)
                        mm(sm_place[:, u, 0], c["ones_bf"][:], sel_bf[:, u, 1], start=False, stop=True)
                        last = mm(sm_place[:, u, 1], c["ones_bf"][:], sel_bf[:, u, 1], start=True, stop=True)
                    last.then_inc(place_ps.sem, 1)
                    for u in range(U):
                        pe.wait_ge(perm_ready.sem, perm_ready.at(it, u + 1))
                        for t in range(2):
                            rows = slice(P * t, P * t + P)
                            tr(ps_perm[:, u, t], pT[:, u, rows], c["ident"][:])
                            last = mm(sm_row[:, u, t], pT[:, u, rows], tokv[:, u], start=True, stop=True)
                        last.then_inc(rows_ps.sem, 1)
                    pe.wait_ge(proj_sb.sem, proj_sb.at(it, 4 * U))
                    for n in range(6):
                        for u in range(U):
                            if n == 2:
                                pe.wait_ge(qk_ready.sem, qk_ready.at(it, u + 1))
                            if n >= 3:
                                pe.wait_ge(perm_sb.sem, perm_sb.at(it, (n - 3) * U + u + 1))
                            if n < 2:
                                last = mm(ps[:, u, n], pT[:, u, P * n:P * n + P], vv[:, u], start=True, stop=True)
                            else:
                                which, half = (1, n - 2) if n < 4 else (0, n - 4)
                                for q in range(2):
                                    pair = 2 * half + q
                                    last = mm(ps[:, u, n % 3, R * q:R * q + R], qk[:, u, which, P * pair:P * pair + P],
                                              pT[:, u], start=True, stop=True)
                            last.then_inc(perm_ps.sem, 1)
                    for u in range(U):
                        pe.wait_ge(perm_sb.sem, perm_sb.at(it, 5 * U + u + 1))
                        pe.wait_ge(gdecay_ready.sem, gdecay_ready.at(it, u + 1))
                        pe.wait_ge(mask_c_ready.sem, mask_c_ready.at(it, u + 1))
                        for t in range(2):
                            dst = ps[:, u, 2, H * BK * t:H * BK * (t + 1)].rearrange("p (h i) -> p h i", h=H)
                            mm(dst, c["after_block"][:], gdecay[:, u, t], start=True, stop=False)
                            mm(dst, c["big_ident"][:], mask_c[:, u, t].unsqueeze(1).to_broadcast([P, H, BK]),
                               start=False, stop=True)
                        for t in range(2):
                            for h in range(H):
                                part = slice(DK * (h % 2), DK * (h % 2) + DK)
                                for k in range(NB_):
                                    kT = kqT[part, u, 0, h // 2, P * t + BK * k:P * t + BK * k + BK]
                                    at = (t * 4 + h // 2) * BK
                                    last = mm(ps[BK * k:BK * k + BK, u, h % 2, at:at + BK], kT, kT, start=True, stop=True)
                        last.then_inc(compact_ps.sem, 1)

            @block.scalar
            def _(act):
                a = nc.scalar
                with act.Fori(0, TURNS) as it:
                    for u in range(U):
                        act.wait_ge(xnT_ps.sem, xnT_ps.at(it, u + 1))
                        a.activation(xnT[:, u], ps[:, u, 0, 0:2 * P], ACT.Copy).then_inc(xnT_sb.sem, 1)
                    for u in range(U):
                        act.wait_ge(h_ps.sem, h_ps.at(it, u + 1))
                        a.activation(hh[:, u], ps[:, u, 1, 0:2 * P], ACT.Copy).then_inc(h_sb.sem, 1)
                    for u in range(U):
                        act.wait_ge(e_ready.sem, e_ready.at(it, u + 1))
                        a.activation(probs[:, u], e_masked[:, u], ACT.Exp, bias=e_neg_max[:, u:u + 1],
                                     accum_out=p_sum[:, u:u + 1]).then_inc(probs_ready.sem, 1)
                    for u in range(U):
                        act.wait_ge(pT_ps.sem, pT_ps.at(it, u + 1))
                        a.activation(probsT[:, u], ps[:, u, 2, P:2 * P], ACT.Copy).then_inc(pT_sb.sem, 1)
                    for u in range(U):
                        act.wait_ge(x1nT_ps.sem, x1nT_ps.at(it, u + 1))
                        a.activation(x1nT[:, u], ps[:, u, 0, 2 * P:4 * P], ACT.Copy).then_inc(x1nT_sb.sem, 1)
                    act.wait_ge(ez_ready.sem, ez_ready.at(it, 1))
                    a.activation(ex[:], ez[:], ACT.Exp).then_inc(ex_ready.sem, 1)
                    for n, bank in enumerate((1, 2, 0, 1)):
                        for u in range(U):
                            act.wait_ge(proj_ps.sem, proj_ps.at(it, n * U + u + 1))
                            a.activation(tanh[:, u, n], ps[:, u, bank], ACT.Tanh, scale=0.5).then_inc(tanh_ready.sem, 1)
                    act.wait_ge(out.sem, out.at(it, 0))
                    act.wait_ge(rows_ps.sem, rows_ps.at(it, U))
                    a.activation(pP[:], ps_perm[:], ACT.Copy).then_inc(P_sb.sem, 1)
                    for n in range(6):
                        for u in range(U):
                            act.wait_ge(perm_ps.sem, perm_ps.at(it, n * U + u + 1))
                            if n < 2:
                                dst = vp[:, u, n]
                            else:
                                which, half = (0, n - 2) if n < 4 else (1, n - 4)
                                dst = kqT[:, u, which, 2 * half:2 * half + 2]
                            a.activation(dst, ps[:, u, n % 3], ACT.Copy).then_inc(perm_sb.sem, 1)
                    for u in range(U):
                        act.wait_ge(compact_ps.sem, compact_ps.at(it, u + 1))
                        a.activation(decay[:, u], ps[:, u, 2], ACT.Exp).then_inc(decay_ready.sem, 1)

            @block.gpsimd
            def _(pool):
                g = nc.gpsimd
                with pool.Fori(0, TURNS) as it:
                    chain = Chain(pool_step, pool, it)
                    for n in range(2):
                        pool.wait_ge(var_ready.sem, var_ready.at(it, n + 1))
                        g.tensor_tensor(rstd[:], var[:], c["minus_half"][:, 0:U], ALU.pow).then_inc(rstd_ready.sem, 1)
                    for u in range(U):
                        pool.wait_ge(proj_sb.sem, proj_sb.at(it, U + u + 1))
                        y = qk[:, u].rearrange("p a (h d) -> p (a h) d", d=DK)
                        g.tensor_tensor(qk_sq[:, u], y, y, ALU.mult).then_inc(sq_ready.sem, 1)
                    pool.wait_ge(ss_ready.sem, ss_ready.at(it, 1))
                    chain.done(g.tensor_tensor(rnorm[:].rearrange("p u h -> p (u h)"), ss[:].rearrange("p u h -> p (u h)"),
                                               c["minus_half"][:, 0:U * 2 * H], ALU.pow))
                    for u in range(U):
                        y = qk[:, u].rearrange("p a (h d) -> p (a h) d", d=DK)
                        g.tensor_tensor(y, y, rnorm[:, u].unsqueeze(2).to_broadcast([P, 2 * H, DK]),
                                        ALU.mult).then_inc(qk_ready.sem, 1)
                    pool.wait_ge(out.sem, out.at(it, 0))
                    for u in range(U):
                        pool.wait_ge(proj_sb.sem, proj_sb.at(it, 3 * U + u + 1))
                        g.tensor_tensor(gate[:, u].rearrange("p (h d) -> p h d", d=DK), gg[:, u].rearrange("p (h d) -> p h d", d=DK),
                                        c["norm_w"][:].unsqueeze(1).to_broadcast([P, H, DK]), ALU.mult).then_inc(gate_ready.sem, 1)
                    pool.wait_ge(rowv_ready.sem, rowv_ready.at(it, 1))
                    for u in range(U):
                        for t in range(2):
                            last = g.tensor_tensor(gdecay[:, u, t], c["upto_block"][:].unsqueeze(1).to_broadcast([P, H, BK]),
                                                   rowg[:, u, t].unsqueeze(2).to_broadcast([P, H, BK]), ALU.mult)
                        last.then_inc(gdecay_ready.sem, 1)
                    chain.close()

            @block.vector
            def _(dve):
                v = nc.vector
                dve.wait_ge(w_in, 16 * 9)
                v.tensor_scalar(att_b[:, 0], c["ones"][:], att[:, 0:1], None, ALU.mult)
                v.memset(scores[:], -1.0)
                v.memset(from_e[:], 0.0)
                v.memset(sel_bf[:], 0.0)
                v.tensor_scalar(att_b[:, 1], c["ones"][:], att[:, 1:2], None, ALU.mult).then_inc(att_ready, 1)
                dve.wait_ge(att_ready, 1)
                with dve.Fori(0, TURNS) as it:
                    chain = Chain(dve_step, dve, it)

                    def layernorm(src, n):
                        for u in range(U):
                            if n == 0:
                                dve.wait_ge(x_in.sem, x_in.at(it, U))
                            chain.done(v.bn_stats(stats[:, u], src[:, u]))
                            carry(nc, c)
                            chain.done(v.bn_aggr(mv[:, u], stats[:, u]))
                        v.tensor_scalar(var[:], mv[:, :, 1], LN_EPS, None, ALU.add).then_inc(var_ready.sem, 1)
                        dve.wait_ge(rstd_ready.sem, rstd_ready.at(it, n + 1))
                        for u in range(U):
                            v.tensor_scalar(xn[:, u], src[:, u], mv[:, u, 0:1], rstd[:, u:u + 1],
                                            ALU.subtract, ALU.mult).then_inc(xn_ready.sem, 1)

                    layernorm(x, 0)
                    for u in range(U):
                        dve.wait_ge(e_ps.sem, e_ps.at(it, u + 1))
                        chain.done(v.tensor_scalar(e_low[:, u], ps[:, u, 2, 0:P], 0.2, None, ALU.mult))
                        chain.done(v.tensor_tensor(e_act[:, u], e_low[:, u], ps[:, u, 2, 0:P], ALU.max))
                        chain.done(v.tensor_tensor(e_masked[:, u], e_act[:, u], c["adj_neg"][:], ALU.add))
                        chain.done(v.tensor_reduce(e_max[:, u:u + 1], e_masked[:, u], AX.X, ALU.max))
                        v.tensor_scalar(e_neg_max[:, u:u + 1], e_max[:, u:u + 1], -1.0, None, ALU.mult).then_inc(e_ready.sem, 1)
                    dve.wait_ge(x1_out.sem, x1_out.at(it, 0))
                    for u in range(U):
                        dve.wait_ge(o_ps.sem, o_ps.at(it, u + 1))
                        chain.done(v.reciprocal(p_rec[:, u:u + 1], p_sum[:, u:u + 1]))
                        v.scalar_tensor_tensor(x1[:, u, 0:F1], ps[:, u, 2, 2 * P:3 * P], p_rec[:, u:u + 1], x[:, u, 0:F1],
                                               ALU.mult, ALU.add)
                        v.tensor_tensor(x1[:, u, F1:D], hh[:, u, 0], x[:, u, F1:D], ALU.add).then_inc(x1_ready.sem, 1)
                        dve.wait_ge(x1_ready.sem, x1_ready.at(it, u + 1))
                    layernorm(x1, 1)
                    dve.wait_ge(small_ps.sem, small_ps.at(it, U))
                    v.tensor_reduce(lmax[:], sm_proj[:, :, 0:E0], AX.X, ALU.max)
                    v.tensor_scalar(ez[:, :, E0:E0 + H], sm_proj[:, :, E0:E0 + H], -1.0, None, ALU.mult)
                    chain.done(v.tensor_tensor(zz[:], sm_proj[:, :, E0 + H:SMALL],
                                               c["dt_bias"][:].unsqueeze(1).to_broadcast([P, U, H]), ALU.add))
                    v.tensor_tensor(ez[:, :, 0:E0], sm_proj[:, :, 0:E0], lmax[:].unsqueeze(2).to_broadcast([P, U, E0]),
                                    ALU.subtract)
                    v.scalar_tensor_tensor(ez[:, :, E0 + H:SMALL], zz[:], -1.0, zz[:], ALU.mult, ALU.min).then_inc(ez_ready.sem, 1)
                    dve.wait_ge(ex_ready.sem, ex_ready.at(it, 1))
                    v.tensor_scalar(den[:, :, 0:H], ex[:, :, E0:E0 + H], 1.0, None, ALU.add)
                    v.tensor_scalar(den[:, :, H:2 * H], ex[:, :, E0 + H:SMALL], 2.0, None, ALU.add)
                    chain.done(v.tensor_reduce(den[:, :, 2 * H:2 * H + 1], ex[:, :, 0:E0], AX.X, ALU.add))
                    chain.done(v.reciprocal(rec[:], den[:]))
                    v.tensor_tensor(scores[:, :, 0:E0], ex[:, :, 0:E0], rec[:, :, 2 * H:2 * H + 1].to_broadcast([P, U, E0]), ALU.mult)
                    chain.done(v.tensor_tensor(s1[:], ex[:, :, E0 + H:SMALL], rec[:, :, H:2 * H], ALU.mult))
                    chain.done(v.tensor_tensor(s2[:], s1[:], s1[:], ALU.mult))
                    chain.done(v.tensor_scalar(poly[:], s2[:], 2.0 / 17.0, None, ALU.mult))
                    for m in range(7, 0, -1):
                        chain.done(v.scalar_tensor_tensor(poly[:], poly[:], 2.0 / (2 * m + 1), s2[:], ALU.add, ALU.mult))
                    chain.done(v.scalar_tensor_tensor(poly[:], poly[:], 2.0, s1[:], ALU.add, ALU.mult))
                    chain.done(v.scalar_tensor_tensor(poly[:], zz[:], 0.0, poly[:], ALU.max, ALU.add))
                    chain.done(v.tensor_tensor(poly[:], poly[:], c["neg_a"][:].unsqueeze(1).to_broadcast([P, U, H]), ALU.mult))
                    v.tensor_scalar(tokv[:, :, 2 * E0 + H:ROWV], poly[:], -1000.0, None, ALU.max)
                    v.tensor_copy(tokv[:, :, 2 * E0:2 * E0 + H], rec[:, :, 0:H])
                    for u in range(U):
                        carry(nc, c)
                        chain.done(v.max(top[:, u], scores[:, u]))
                        carry(nc, c)
                        chain.done(v.max_index(top_i[:, u], top[:, u], scores[:, u]))
                    chain.done(v.tensor_copy(top_f[:], top_i[:]))
                    for u in range(U):
                        chain.done(v.tensor_scalar(sel[:, u], c["row0"][:, 0:E0], top_f[:, u, 0:1], None, ALU.is_equal))
                        chain.done(v.scalar_tensor_tensor(sel[:, u], c["row0"][:, 0:E0], top_f[:, u, 1:2], sel[:, u],
                                                          ALU.is_equal, ALU.add))
                    v.tensor_copy(sel_bf[:, :, 0], sel[:])
                    v.tensor_copy(sel_bf[:, :, 1, 1:2], sel[:, :, 0:1])
                    chain.done(v.tensor_tensor(sel_bf[:, :, 1, 2:3], sel[:, :, 0:1], sel[:, :, 1:2], ALU.add))
                    v.tensor_tensor(sel_bf[:, :, 1, 3:4], sel_bf[:, :, 1, 2:3], sel[:, :, 2:3], ALU.add).then_inc(sel_ready.sem, 1)
                    chain.done(v.tensor_tensor(wun[:], scores[:, :, 0:E0], sel[:], ALU.mult))
                    chain.done(v.tensor_tensor(wsum[:].unsqueeze(2), top[:, :, 0:1], top[:, :, 1:2], ALU.add))
                    chain.done(v.reciprocal(wrec[:], wsum[:]))
                    chain.done(v.tensor_tensor(wun[:], wun[:], wrec[:].unsqueeze(2).to_broadcast([P, U, E0]), ALU.mult))
                    v.tensor_scalar(tokv[:, :, 0:E0], wun[:], 0.5 * DK ** -0.5, None, ALU.mult)
                    chain.done(v.tensor_scalar(tokv[:, :, E0:2 * E0], wun[:], 0.0, None, ALU.is_gt))
                    for n, bank in enumerate((1, 2, 0, 1)):
                        for u in range(U):
                            dve.wait_ge(tanh_ready.sem, tanh_ready.at(it, n * U + u + 1))
                            dst = (qk[:, u, 0], qk[:, u, 1], vv[:, u], gg[:, u])[n]
                            v.scalar_tensor_tensor(dst, tanh[:, u, n], 1.0, ps[:, u, bank], ALU.add,
                                                   ALU.mult).then_inc(proj_sb.sem, 1)
                    dve.wait_ge(place_ps.sem, place_ps.at(it, 1))
                    chain.done(v.tensor_copy(place[:], sm_place))
                    chain.done(v.scalar_tensor_tensor(place1[:], place[:, :, 0], 1.0, sel[:], ALU.add, ALU.mult))
                    for u in range(U):
                        chain.done(v.tensor_scalar(pT[:, u], c["row1"][:], place1[:, u, 0:1], None, ALU.is_equal))
                        for e in range(1, E0):
                            last = v.scalar_tensor_tensor(pT[:, u], c["row1"][:], place1[:, u, e:e + 1], pT[:, u],
                                                          ALU.is_equal, ALU.add)
                            if e < E0 - 1:
                                chain.done(last)
                        last.then_inc(perm_ready.sem, 1)
                    for u in range(U):
                        for t in range(2):
                            v.tensor_scalar(from_e[:, u, t, 0:E0], place[:, u, 1], c["rowid"][:, t:t + 1], None, ALU.is_le)
                        chain.done(v.tensor_scalar(eid[:, u], c["row0"][:], place[:, u, 1, 1:2], None, ALU.is_ge))
                        for e in range(2, E0):
                            chain.done(v.scalar_tensor_tensor(eid[:, u], c["row0"][:], place[:, u, 1, e:e + 1], eid[:, u],
                                                              ALU.is_ge, ALU.add))
                    chain.done(v.tensor_reduce(eid_row[:].rearrange("p u t -> p (u t)"),
                                               from_e[:, :, :, 1:E0].rearrange("p u t e -> p (u t) e"), AX.X, ALU.add))
                    dve.wait_ge(out.sem, out.at(it, 0))
                    for u in range(U):
                        v.scalar_tensor_tensor(mask[:, u, 0:R], eid[:, u], eid_row[:, u, 0:1], c["causal"][:, 0:R],
                                               ALU.is_equal, ALU.add)
                        v.scalar_tensor_tensor(mask[:, u, R:R + P], eid[:, u, P:R], eid_row[:, u, 1:2], c["causal"][:, R:R + P],
                                               ALU.is_equal, ALU.add).then_inc(mask_ready.sem, 1)
                    for u in range(U):
                        dve.wait_ge(mask_ready.sem, mask_ready.at(it, u + 1))
                        for k in range(NB_):
                            rows = slice(BK * k, BK * k + BK)
                            both = mask[rows, u, :].rearrange("p (a b) -> p a b", b=P)[:, 0:3:2, rows]
                            last = v.tensor_copy(mask_c[rows, u], both)
                        last.then_inc(mask_c_ready.sem, 1)
                    dve.wait_ge(rows_ps.sem, rows_ps.at(it, U))
                    v.tensor_copy(rv[:], sm_row)
                    chain.done(v.tensor_tensor(onehot[:], from_e[:, :, :, 0:E0], from_e[:, :, :, 1:E0 + 1], ALU.subtract))
                    for a in range(2):
                        last = v.tensor_tensor(picked[:, :, :, a], rv[:, :, :, E0 * a:E0 * a + E0], onehot[:], ALU.mult)
                    chain.done(last)
                    chain.done(v.tensor_reduce(w_act[:].rearrange("p u t a -> p (u t a)"),
                                               picked[:].rearrange("p u t a e -> p (u t a) e"), AX.X, ALU.add))
                    v.tensor_copy(roww[:], w_act[:, :, :, 0])
                    active = w_act[:, :, :, 1:2].to_broadcast([P, U, 2, H])
                    v.tensor_tensor(rowb[:], rv[:, :, :, 2 * E0:2 * E0 + H], active, ALU.mult)
                    v.tensor_tensor(rowg[:], rv[:, :, :, 2 * E0 + H:ROWV], active, ALU.mult).then_inc(rowv_ready.sem, 1)
                    for u in range(U):
                        dve.wait_ge(sq_ready.sem, sq_ready.at(it, u + 1))
                        chain.done(v.tensor_reduce(ss[:, u], qk_sq[:, u], AX.X, ALU.add))
                    v.tensor_scalar(ss[:], ss[:], 4e-6, None, ALU.add).then_inc(ss_ready.sem, 1)
                    for u in range(U):
                        dve.wait_ge(decay_ready.sem, decay_ready.at(it, u + 1))
                        for odd in range(2):
                            last = v.tensor_tensor(acomp[:, u, :, odd:H:2], ps[:, u, odd, 0:256].rearrange("p (t h i) -> p t h i", t=2, h=4),
                                                   decay[:, u, :, odd:H:2], ALU.mult)
                        last.then_inc(acomp_ready.sem, 1)
                    chain.close()


def phase_invert(nc, c, dram, NB):
    GROUP = P // (2 * H)
    TURNS = NB // GROUP
    SY = 2 * H
    ctx = ExitStack()
    counts = []

    def sb(name, shape, dt=F32):
        return ctx.enter_context(nc.sbuf_tensor(name, shape, dt))

    def count(name, per, unit=1, again=False):
        counts.append(Count(ctx, nc, "b_" + name, per, unit, again))
        return counts[-1]

    with ctx:
        a_in = sb("b_a_in", [P, GROUP, SY, BK])
        beta_in = sb("b_beta_in", [P, GROUP, SY])
        betaT = sb("b_betaT", [P, P])
        a_sys = sb("b_a_sys", [P, BK, NB_, BK])
        x_sys = sb("b_x_sys", [P, BK, NB_, BK])
        eyes = sb("b_eyes", [P, BK, NB_, BK])
        prod_d = sb("b_prod_d", [P, BK * NB_ * BK // 4])
        prod_p = sb("b_prod_p", [P, BK * BK // 4 + BK])
        inv = sb("b_inv", [P, P, BK])
        ps = ctx.enter_context(nc.psum_tensor("b_ps", [P, 4, 4, P], F32))
        ps_beta = ctx.enter_context(nc.psum_tensor("b_ps_beta", [P, P], F32))
        ps_back = ctx.enter_context(nc.psum_tensor("b_ps_back", [P, 3, 4, P], F32))

        zeroed = ctx.enter_context(nc.semaphore("b_zeroed"))
        loaded = count("loaded", 2, 16)
        beta_ps = count("beta_ps", 1)
        beta_sb = count("beta_sb", 1, again=True)
        sys_ps = count("sys_ps", 8, again=True)
        sys_sb = count("sys_sb", 8, again=True)
        eye = count("eye", 1)
        solved = count("solved", 1)
        pool_step = count("pool_step", 2 * (BK - 1))
        dve_step = count("dve_step", 2 * (BK - 1))
        scaled = count("scaled", 1, again=True)
        back_ps = count("back_ps", 8, again=True)
        back_sb = count("back_sb", 8, again=True)
        stored = count("stored", 1, 16, again=True)

        def update(engine, lo, hi, prod, chain, last_sem):
            for s in range(BK - 1):
                rows, cols = BK - 1 - s, s + 1
                p = prod[:, 0:rows * (hi - lo) * cols].rearrange("p (r k c) -> p r k c", r=rows, k=hi - lo)
                factor = a_sys[:, s + 1:BK, lo:hi, s:s + 1].to_broadcast([P, rows, hi - lo, cols])
                row = x_sys[:, s:s + 1, lo:hi, 0:cols].to_broadcast([P, rows, hi - lo, cols])
                below = x_sys[:, s + 1:BK, lo:hi, 0:cols]
                chain.done(engine.tensor_tensor(p, factor, row, ALU.mult))
                last = engine.tensor_tensor(below, below, p, ALU.subtract)
                chain.done(last)
            chain.close()

        with nc.Block() as block:
            @block.sync
            def _(sp):
                start_at_one(sp, counts)
                with sp.Fori(0, TURNS) as it:
                    sp.wait_ge(sys_ps.sem, sys_ps.at(it, 0))
                    sp.dma_start(a_in[:], dram["acomp"][bass.ds(it * GROUP, GROUP)].rearrange("b p t h i -> p b (t h) i")).then_inc(loaded.sem, 16)
                    sp.dma_start(beta_in[:], dram["rowb"][bass.ds(it * GROUP, GROUP)].rearrange("b p t h -> p b (t h)"),
                                 allow_slow_non_contiguous=True).then_inc(loaded.sem, 16)
                    sp.wait_ge(back_sb.sem, back_sb.at(it, 8))
                    sp.dma_start(dram["inv"][bass.ds(it * GROUP, GROUP)].rearrange("b p t h i -> p b (t h i)"),
                                 inv[:].rearrange("p (b s) i -> p b (s i)", b=GROUP)).then_inc(stored.sem, 16)
                sp.wait_ge(stored.sem, stored.at(TURNS, 0))

            @block.tensor
            def _(pe):
                tr = nc.tensor.transpose
                a_flat = a_in[:].rearrange("p b s i -> p (b s) i")
                with pe.Fori(0, TURNS) as it:
                    pe.wait_ge(loaded.sem, loaded.at(it, 2))
                    pe.wait_ge(beta_sb.sem, beta_sb.at(it, 0))
                    tr(ps_beta[:], beta_in[:].rearrange("p b s -> p (b s)"), c["ident"][:]).then_inc(beta_ps.sem, 1)
                    for n in range(8):
                        if n >= 4:
                            pe.wait_ge(sys_sb.sem, sys_sb.at(it, n - 3))
                        else:
                            pe.wait_ge(sys_sb.sem, sys_sb.at(it, 0))
                        for q in range(4):
                            last = tr(ps[:, n % 4, q], a_flat[:, :, 4 * n + q], c["ident"][:])
                        last.then_inc(sys_ps.sem, 1)
                    pe.wait_ge(scaled.sem, scaled.at(it, 1))
                    for n in range(8):
                        if n >= 3:
                            pe.wait_ge(back_sb.sem, back_sb.at(it, n - 2))
                        else:
                            pe.wait_ge(back_sb.sem, back_sb.at(it, 0))
                        for q in range(4):
                            last = tr(ps_back[:, n % 3, q], x_sys[:, 4 * n + q].rearrange("p k c -> p (k c)"), c["ident"][:])
                        last.then_inc(back_ps.sem, 1)

            @block.scalar
            def _(act):
                with act.Fori(0, TURNS) as it:
                    act.wait_ge(beta_ps.sem, beta_ps.at(it, 1))
                    act.wait_ge(scaled.sem, scaled.at(it, 0))
                    nc.scalar.activation(betaT[:], ps_beta[:], ACT.Copy).then_inc(beta_sb.sem, 1)
                    act.wait_ge(stored.sem, stored.at(it, 0))
                    for n in range(8):
                        act.wait_ge(back_ps.sem, back_ps.at(it, n + 1))
                        nc.scalar.activation(inv[:].rearrange("p s i -> p i s")[:, 4 * n:4 * n + 4], ps_back[:, n % 3],
                                             ACT.Copy).then_inc(back_sb.sem, 1)

            @block.gpsimd
            def _(pool):
                g = nc.gpsimd
                g.memset(eyes[:], 0.0).then_inc(zeroed, 1)
                pool.wait_ge(zeroed, 1)
                g.affine_select(out=eyes[:], in_=eyes[:], pattern=[[1, BK], [0, NB_], [-1, BK]],
                                compare_op=ALU.not_equal, fill=1.0, base=0, channel_multiplier=0).then_inc(zeroed, 1)
                pool.wait_ge(zeroed, 2)
                with pool.Fori(0, TURNS) as it:
                    pool.wait_ge(back_ps.sem, back_ps.at(it, 0))
                    g.tensor_tensor(x_sys[:], eyes[:], eyes[:], ALU.mult).then_inc(eye.sem, 1)
                    pool.wait_ge(eye.sem, eye.at(it, 1))
                    pool.wait_ge(sys_sb.sem, sys_sb.at(it, 8))
                    update(g, NB_ - 1, NB_, prod_p, Chain(pool_step, pool, it), None)
                    pool.wait_ge(dve_step.sem, dve_step.at(it + 1, 0))
                    g.tensor_tensor(x_sys[:], x_sys[:], betaT[:].rearrange("p (k r) -> p r k", k=NB_).unsqueeze(3).to_broadcast([P, BK, NB_, BK]),
                                    ALU.mult).then_inc(scaled.sem, 1)

            @block.vector
            def _(dve):
                v = nc.vector
                with dve.Fori(0, TURNS) as it:
                    dve.wait_ge(beta_sb.sem, beta_sb.at(it, 1))
                    dve.wait_ge(scaled.sem, scaled.at(it, 0))
                    for n in range(8):
                        dve.wait_ge(sys_ps.sem, sys_ps.at(it, n + 1))
                        v.tensor_tensor(a_sys[:, 4 * n:4 * n + 4].rearrange("p i k c -> p i (k c)"), ps[:, n % 4],
                                        betaT[:].unsqueeze(1).to_broadcast([P, 4, P]), ALU.mult).then_inc(sys_sb.sem, 1)
                    dve.wait_ge(eye.sem, eye.at(it, 1))
                    dve.wait_ge(sys_sb.sem, sys_sb.at(it, 8))
                    update(v, 0, NB_ - 1, prod_d, Chain(dve_step, dve, it), None)


def phase_mix(nc, c, dram, NB):
    TURNS = NB // U
    ctx = ExitStack()
    counts = []

    def sb(name, shape, dt=F32):
        return ctx.enter_context(nc.sbuf_tensor(name, shape, dt))

    def count(name, per, unit=1, again=False):
        counts.append(Count(ctx, nc, "c_" + name, per, unit, again))
        return counts[-1]

    DECAYS = [(0, 0, 0), (0, 0, 1), (0, 1, 0), (0, 1, 1), (1, 1, 0), (1, 1, 1)]
    PRODUCTS = [(0, (h,)) for h in range(H)] + [(1, (h, h + 2)) for h in (0, 1, 4, 5)]
    ND, NP = len(DECAYS), len(PRODUCTS)

    with ctx:
        wo = sb("c_wo", [P, 4, D])
        kqT = sb("c_kqT", [P, U, 2, 4, R])
        vp = sb("c_vp", [P, U, 2, HD])
        mask = sb("c_mask", [P, U, R + P], BF16)
        perm = sb("c_perm", [P, U, 2, P])
        inv = sb("c_inv", [P, U, 2, H, BK])
        rowg = sb("c_rowg", [P, U, 2, H])
        roww = sb("c_roww", [P, U, 2])
        gate = sb("c_gate", [P, U, HD])
        x1 = sb("c_x1", [P, U, D])
        gsum = sb("c_gsum", [P, U, 2, H, P])
        decay0 = sb("c_decay0", [P, U, H, R])
        decay1 = sb("c_decay1", [P, U, H, P])
        mix0 = sb("c_mix0", [P, U, H, 2, R])
        mix1 = sb("c_mix1", [P, U, H, 2, P])
        rest = sb("c_rest", [P, U, HD])
        base1 = sb("c_base1", [P, U, HD])
        uu = sb("c_uu", [P, U, 2, HD])
        oo = sb("c_oo", [P, U, 2, HD])
        core_sq = sb("c_core_sq", [P, U, HD])
        ms = sb("c_ms", [P, U, H])
        rms = sb("c_rms", [P, U, H])
        y = sb("c_y", [P, U, HD])
        yT = sb("c_yT", [P, U, 4, P])
        x2 = sb("c_x2", [P, U, D])
        ps = ctx.enter_context(nc.psum_tensor("c_ps", [P, U, 4, 512], F32))

        w_in = ctx.enter_context(nc.semaphore("c_w_in"))
        g_in = count("g_in", 2 * U, 16)
        kq_in = count("kq_in", U, 16)
        v_in = count("v_in", 3 * U, 16)
        tail_in = count("tail_in", 3 * U, 16)
        gsum_ready = count("gsum_ready", U)
        decay_ps = count("decay_ps", ND * U, again=True)
        decay_sb = count("decay_sb", ND * U)
        prod_ps = count("prod_ps", NP * U, again=True)
        mix_ready = count("mix_ready", NP * U, again=True)
        solve_ps = count("solve_ps", 2 * NB_ * U)
        uu_ready = count("uu_ready", 2 * NB_ * U)
        rest_ps = count("rest_ps", 2 * (NB_ - 1) * U)
        rest_ready = count("rest_ready", 2 * (NB_ - 1) * U)
        cross_ps = count("cross_ps", U)
        base1_ready = count("base1_ready", U)
        o_ps = count("o_ps", 2 * U)
        oo_ready = count("oo_ready", 2 * U, again=True)
        core_ps = count("core_ps", U)
        sq_ready = count("sq_ready", U)
        ms_ready = count("ms_ready", 1)
        rms_ready = count("rms_ready", 1)
        y_ready = count("y_ready", U)
        yT_ps = count("yT_ps", U)
        yT_ready = count("yT_ready", U)
        out_ps = count("out_ps", U)
        x2_ready = count("x2_ready", U, again=True)
        stored = count("stored", U, 16, again=True)
        dve_step = count("dve_step", C_DVE_STEPS)

        with nc.Block() as block:
            @block.sync
            def _(sp):
                start_at_one(sp, counts)
                sp.dma_start(wo[:], dram["L0_ffn_Wo"].rearrange("(k p) f -> p k f", p=P)).then_inc(w_in, 16)
                with sp.Fori(0, TURNS) as it:
                    for u in range(U):
                        b = it * U + u
                        sp.wait_ge(decay_ps.sem, decay_ps.at(it, 0))
                        sp.dma_start(rowg[:, u], dram["rowg"][b]).then_inc(g_in.sem, 16)
                        sp.dma_start(mask[:, u], dram["mask"][b]).then_inc(g_in.sem, 16)
                    for u in range(U):
                        sp.wait_ge(prod_ps.sem, prod_ps.at(it, 0))
                        sp.dma_start(kqT[:, u], dram["kqT"][it * U + u]).then_inc(kq_in.sem, 16)
                    for u in range(U):
                        b = it * U + u
                        sp.wait_ge(oo_ready.sem, oo_ready.at(it, 0))
                        sp.dma_start(vp[:, u], dram["vp"][b]).then_inc(v_in.sem, 16)
                        sp.dma_start(inv[:, u], dram["inv"][b]).then_inc(v_in.sem, 16)
                        sp.dma_start(roww[:, u], dram["roww"][b]).then_inc(v_in.sem, 16)
                    for u in range(U):
                        b = it * U + u
                        sp.wait_ge(x2_ready.sem, x2_ready.at(it, 0))
                        sp.dma_start(perm[:, u], dram["perm"][b]).then_inc(tail_in.sem, 16)
                        sp.dma_start(gate[:, u], dram["gate"][b]).then_inc(tail_in.sem, 16)
                        sp.dma_start(x1[:, u], dram["x1"][b]).then_inc(tail_in.sem, 16)
                    for u in range(U):
                        sp.wait_ge(x2_ready.sem, x2_ready.at(it, u + 1))
                        sp.dma_start(dram["x2"][it * U + u], x2[:, u]).then_inc(stored.sem, 16)
                sp.wait_ge(stored.sem, stored.at(TURNS, 0))

            @block.tensor
            def _(pe):
                mm, tr = nc.tensor.matmul, nc.tensor.transpose

                def carrier(u):
                    mm(ps[:, u, 1, 0:1], c["ones_bf"][:], c["ones_bf"][:, 0:1], start=True, stop=True)

                pe.wait_ge(w_in, 16)
                with pe.Fori(0, TURNS) as it:
                    pe.wait_ge(x2_ready.sem, x2_ready.at(it, 0))
                    pe.wait_ge(g_in.sem, g_in.at(it, 2 * U))
                    for n, (tj, ti, half) in enumerate(DECAYS):
                        for u in range(U):
                            if n == 0:
                                pe.wait_ge(gsum_ready.sem, gsum_ready.at(it, u + 1))
                            if n >= 4:
                                pe.wait_ge(decay_sb.sem, decay_sb.at(it, (n - 4) * U + u + 1))
                            heads = slice(4 * half, 4 * half + 4)
                            dst = ps[:, u, n % 4].rearrange("p (h i) -> p h i", h=4)
                            if tj == ti:
                                mm(dst, c["after"][:], gsum[:, u, tj, heads], start=True, stop=False)
                            else:
                                mm(dst, c["after"][:], rowg[:, u, 0, heads].unsqueeze(2).to_broadcast([P, 4, P]),
                                   start=True, stop=False)
                                mm(dst, c["ones"][:], gsum[:, u, 1, heads], start=False, stop=False)
                            at = P * (tj + ti)
                            mm(dst, c["big_ident"][:], mask[:, u, at:at + P].unsqueeze(1).to_broadcast([P, 4, P]),
                               start=False, stop=True).then_inc(decay_ps.sem, 1)
                    for n, (t, heads) in enumerate(PRODUCTS):
                        for u in range(U):
                            if n == 0:
                                pe.wait_ge(kq_in.sem, kq_in.at(it, U))
                            if n < 4:
                                m = max(k for k in range(ND) if k % 4 == (ND + n) % 4)
                                pe.wait_ge(decay_sb.sem, decay_sb.at(it, m * U + u + 1))
                            else:
                                pe.wait_ge(mix_ready.sem, mix_ready.at(it, (n - 4) * U + u + 1))
                            width = R if t == 0 else P
                            for m, h in enumerate(heads):
                                part = slice(DK * (h % 2), DK * (h % 2) + DK)
                                dst = ps[:, u, (ND + n) % 4, 2 * P * m:2 * P * m + 2 * width].rearrange("p (a i) -> p a i", a=2)
                                last = mm(dst, kqT[part, u, 0, h // 2, P * t:P * t + P],
                                          kqT[part, u, :, h // 2, R - width:R], start=True, stop=True)
                            last.then_inc(prod_ps.sem, 1)
                    pe.wait_ge(mix_ready.sem, mix_ready.at(it, NP * U))
                    pe.wait_ge(v_in.sem, v_in.at(it, 3 * U))
                    for t in range(2):
                        if t == 1:
                            for u in range(U):
                                pe.wait_ge(uu_ready.sem, uu_ready.at(it, (NB_ - 1) * U + u + 1))
                                for h in range(H):
                                    last = mm(ps[:, u, 2, DK * h:DK * h + DK], mix0[:, u, h, 0, P:R],
                                              uu[:, u, 0, DK * h:DK * h + DK], start=True, stop=True)
                                last.then_inc(cross_ps.sem, 1)
                        for k in range(NB_):
                            rows = slice(BK * k, BK * k + BK)
                            if k:
                                for u in range(U):
                                    pe.wait_ge(uu_ready.sem, uu_ready.at(it, (t * NB_ + k - 1) * U + u + 1))
                                    carrier(u)
                                    for h in range(H):
                                        m = mix0 if t == 0 else mix1
                                        last = mm(ps[rows, u, 2, DK * h:DK * h + DK], m[0:BK * k, u, h, 0, rows],
                                                  uu[0:BK * k, u, t, DK * h:DK * h + DK], start=True, stop=True)
                                    last.then_inc(rest_ps.sem, 1)
                            for u in range(U):
                                if k:
                                    pe.wait_ge(rest_ready.sem, rest_ready.at(it, (t * (NB_ - 1) + k - 1) * U + u + 1))
                                elif t:
                                    pe.wait_ge(base1_ready.sem, base1_ready.at(it, u + 1))
                                if k:
                                    pe.wait_ge(uu_ready.sem, uu_ready.at(it, (t * NB_ + k - 1) * U + u + 1))
                                carrier(u)
                                src = rest[:, u] if k else (base1[:, u] if t else vp[:, u, 0])
                                for h in range(H):
                                    last = mm(ps[rows, u, 3, DK * h:DK * h + DK], inv[rows, u, t, h],
                                              src[rows, DK * h:DK * h + DK], start=True, stop=True)
                                last.then_inc(solve_ps.sem, 1)
                    for t in range(2):
                        for u in range(U):
                            pe.wait_ge(uu_ready.sem, uu_ready.at(it, (2 * NB_ - 1) * U + u + 1))
                            for h in range(H):
                                cols = slice(DK * h, DK * h + DK)
                                last = mm(ps[:, u, t, cols], mix0[:, u, h, 1, P * t:P * t + P], uu[:, u, 0, cols],
                                          start=True, stop=t == 0)
                                if t:
                                    last = mm(ps[:, u, t, cols], mix1[:, u, h, 1], uu[:, u, 1, cols], start=False, stop=True)
                            last.then_inc(o_ps.sem, 1)
                    pe.wait_ge(tail_in.sem, tail_in.at(it, 3 * U))
                    for u in range(U):
                        pe.wait_ge(oo_ready.sem, oo_ready.at(it, U + u + 1))
                        for t in range(2):
                            last = mm(ps[:, u, 2], perm[:, u, t], oo[:, u, t], start=t == 0, stop=t == 1)
                        last.then_inc(core_ps.sem, 1)
                    for u in range(U):
                        pe.wait_ge(y_ready.sem, y_ready.at(it, u + 1))
                        for k in range(4):
                            last = tr(ps[:, u, 3, P * k:P * k + P], y[:, u, P * k:P * k + P], c["ident"][:])
                        last.then_inc(yT_ps.sem, 1)
                    for u in range(U):
                        pe.wait_ge(yT_ready.sem, yT_ready.at(it, u + 1))
                        for k in range(4):
                            last = mm(ps[:, u, 0, 0:D], yT[:, u, k], wo[:, k], start=k == 0, stop=k == 3)
                        last.then_inc(out_ps.sem, 1)

            @block.scalar
            def _(act):
                a = nc.scalar
                with act.Fori(0, TURNS) as it:
                    for n, (tj, ti, half) in enumerate(DECAYS):
                        for u in range(U):
                            act.wait_ge(decay_ps.sem, decay_ps.at(it, n * U + u + 1))
                            if n == 0:
                                act.wait_ge(mix_ready.sem, mix_ready.at(it, 0))
                            heads = slice(4 * half, 4 * half + 4)
                            dst = decay1[:, u, heads] if tj else decay0[:, u, heads, P * ti:P * ti + P]
                            a.activation(dst, ps[:, u, n % 4].rearrange("p (h i) -> p h i", h=4), ACT.Exp).then_inc(decay_sb.sem, 1)
                    for t in range(2):
                        for k in range(NB_):
                            rows = slice(BK * k, BK * k + BK)
                            for u in range(U):
                                act.wait_ge(solve_ps.sem, solve_ps.at(it, (t * NB_ + k) * U + u + 1))
                                a.activation(uu[rows, u, t], ps[rows, u, 3], ACT.Copy).then_inc(uu_ready.sem, 1)
                    for t in range(2):
                        for u in range(U):
                            act.wait_ge(o_ps.sem, o_ps.at(it, t * U + u + 1))
                            a.activation(oo[:, u, t], ps[:, u, t], ACT.Copy, scale=roww[:, u, t:t + 1]).then_inc(oo_ready.sem, 1)
                    for u in range(U):
                        act.wait_ge(core_ps.sem, core_ps.at(it, u + 1))
                        a.activation(core_sq[:, u], ps[:, u, 2], ACT.Square).then_inc(sq_ready.sem, 1)
                    for u in range(U):
                        act.wait_ge(yT_ps.sem, yT_ps.at(it, u + 1))
                        a.activation(yT[:, u], ps[:, u, 3], ACT.Copy).then_inc(yT_ready.sem, 1)

            @block.gpsimd
            def _(pool):
                g = nc.gpsimd
                with pool.Fori(0, TURNS) as it:
                    pool.wait_ge(g_in.sem, g_in.at(it, 2 * U))
                    pool.wait_ge(decay_ps.sem, decay_ps.at(it, 0))
                    for u in range(U):
                        for t in range(2):
                            last = g.tensor_tensor(gsum[:, u, t], c["upto"][:].unsqueeze(1).to_broadcast([P, H, P]),
                                                   rowg[:, u, t].unsqueeze(2).to_broadcast([P, H, P]), ALU.mult)
                        last.then_inc(gsum_ready.sem, 1)
                    pool.wait_ge(ms_ready.sem, ms_ready.at(it, 1))
                    g.tensor_tensor(rms[:].rearrange("p u h -> p (u h)"), ms[:].rearrange("p u h -> p (u h)"),
                                    c["minus_half"][:, 0:U * H], ALU.pow).then_inc(rms_ready.sem, 1)

            @block.vector
            def _(dve):
                v = nc.vector
                with dve.Fori(0, TURNS) as it:
                    chain = Chain(dve_step, dve, it)
                    dve.wait_ge(decay_sb.sem, decay_sb.at(it, ND * U))
                    for n, (t, heads) in enumerate(PRODUCTS):
                        for u in range(U):
                            dve.wait_ge(prod_ps.sem, prod_ps.at(it, n * U + u + 1))
                            src = ps[:, u, (ND + n) % 4]
                            if t == 0:
                                h = heads[0]
                                v.tensor_tensor(mix0[:, u, h], src.rearrange("p (a i) -> p a i", a=2),
                                                decay0[:, u, h].unsqueeze(1).to_broadcast([P, 2, R]), ALU.mult).then_inc(mix_ready.sem, 1)
                            else:
                                pair = slice(heads[0], heads[1] + 1, 2)
                                v.tensor_tensor(mix1[:, u, pair], src.rearrange("p (h a i) -> p h a i", h=2, a=2),
                                                decay1[:, u, pair].unsqueeze(2).to_broadcast([P, 2, 2, P]), ALU.mult).then_inc(mix_ready.sem, 1)
                    dve.wait_ge(v_in.sem, v_in.at(it, 3 * U))
                    for t in range(2):
                        if t == 1:
                            for u in range(U):
                                dve.wait_ge(cross_ps.sem, cross_ps.at(it, u + 1))
                                v.tensor_tensor(base1[:, u], vp[:, u, 1], ps[:, u, 2], ALU.subtract).then_inc(base1_ready.sem, 1)
                            dve.wait_ge(base1_ready.sem, base1_ready.at(it, U))
                        for k in range(1, NB_):
                            rows = slice(BK * k, BK * k + BK)
                            for u in range(U):
                                dve.wait_ge(rest_ps.sem, rest_ps.at(it, (t * (NB_ - 1) + k - 1) * U + u + 1))
                                src = base1[:, u] if t else vp[:, u, 0]
                                v.tensor_tensor(rest[rows, u], src[rows], ps[rows, u, 2], ALU.subtract).then_inc(rest_ready.sem, 1)
                    dve.wait_ge(tail_in.sem, tail_in.at(it, 3 * U))
                    for u in range(U):
                        dve.wait_ge(sq_ready.sem, sq_ready.at(it, u + 1))
                        chain.done(v.tensor_reduce(ms[:, u], core_sq[:, u].rearrange("p (h d) -> p h d", d=DK), AX.X, ALU.add))
                    v.tensor_scalar(ms[:], ms[:], 1.0 / DK, LN_EPS, ALU.mult, ALU.add).then_inc(ms_ready.sem, 1)
                    dve.wait_ge(rms_ready.sem, rms_ready.at(it, 1))
                    for u in range(U):
                        yh = y[:, u].rearrange("p (h d) -> p h d", d=DK)
                        chain.done(v.tensor_tensor(yh, ps[:, u, 2].rearrange("p (h d) -> p h d", d=DK),
                                                   rms[:, u].unsqueeze(2).to_broadcast([P, H, DK]), ALU.mult))
                        v.tensor_tensor(y[:, u], y[:, u], gate[:, u], ALU.mult).then_inc(y_ready.sem, 1)
                    dve.wait_ge(stored.sem, stored.at(it, 0))
                    for u in range(U):
                        dve.wait_ge(out_ps.sem, out_ps.at(it, u + 1))
                        v.tensor_tensor(x2[:, u], ps[:, u, 0, 0:D], x1[:, u], ALU.add).then_inc(x2_ready.sem, 1)
                    chain.close()


def phase_experts(nc, c, dram, NB):
    TURNS = NB // U
    G4 = 4
    TOKENS = G4 * P
    SLOTS = 2
    PAIRS, GROUPS = E1 // SLOTS, NB // G4
    SCALE = float(D1) ** -0.5
    ctx = ExitStack()
    counts = []

    def count(name, per, unit=1, again=False):
        counts.append(Count(ctx, nc, "e_" + name, per, unit, again))
        return counts[-1]

    def sb_in(stack):
        return lambda name, shape, dt=F32: stack.enter_context(nc.sbuf_tensor(name, shape, dt))

    with ctx:
        sb = sb_in(ctx)
        acc = sb("e_acc", [P, NB, D])
        xT_all = sb("e_xT_all", [P, 2, NB * P])
        w_all = sb("e_w_all", [P, NB, E1])

        with ExitStack() as attention:
            sb = sb_in(attention)
            wqkv = sb("d_wqkv", [P, 3, 2, D])
            wo = sb("d_wo", [P, 2, D])
            wsel = sb("d_wsel", [P, 2, E1])
            bqk = sb("d_bqk", [P, 2, 2])
            bv = sb("d_bv", [P, D])
            bo = sb("d_bo", [P, D])
            x = sb("d_x", [P, U, D])
            stats = sb("d_stats", [P, U, 6])
            mv = sb("d_mv", [P, U, 2])
            var = sb("d_var", [P, U])
            rstd = sb("d_rstd", [P, U])
            xn = sb("d_xn", [P, U, D])
            xnT = sb("d_xnT", [P, U, 2, P])
            qkT = sb("d_qkT", [P, U, 2, 2, P])
            vals = sb("d_vals", [P, U, D])
            s = sb("d_s", [P, U, H, P])
            neg_max = sb("d_neg_max", [P, U, H])
            probs = sb("d_probs", [P, U, H, P])
            psum = sb("d_psum", [P, U, H])
            prec = sb("d_prec", [P, U, H])
            probsT = sb("d_probsT", [P, U, H, P])
            ao = sb("d_ao", [P, U, D])
            aoT = sb("d_aoT", [P, U, 2, P])
            xb = sb("d_xb", [P, U, D])
            x3 = sb("d_x3", [P, U, D])
            x3nT = sb("d_x3nT", [P, U, 2, P])
            sig_e = sb("d_sig_e", [P, U, E1])
            sig_d = sb("d_sig_d", [P, U, E1])
            sig = sb("d_sig", [P, U, E1])
            top = sb("d_top", [P, U, 8])
            top_i = sb("d_top_i", [P, U, 8], U32)
            top_f = sb("d_top_f", [P, U, 8])
            w1 = sb("d_w1", [P, U, E1])
            w2 = sb("d_w2", [P, U, E1])
            ps = attention.enter_context(nc.psum_tensor("d_ps", [P, U, 4, 512], F32))

            w_in = attention.enter_context(nc.semaphore("d_w_in"))
            x_in = count("x_in", U, 16)
            var_ready = count("var_ready", 2)
            rstd_ready = count("rstd_ready", 2)
            xn_ready = count("xn_ready", 2 * U)
            xnT_ps = count("xnT_ps", U)
            xnT_sb = count("xnT_sb", U)
            qk_ps = count("qk_ps", U)
            v_ps = count("v_ps", U)
            qk_sb = count("qk_sb", U)
            v_sb = count("v_sb", U)
            s_ps = count("s_ps", U)
            s_ready = count("s_ready", U)
            probs_ready = count("probs_ready", U)
            probsT_ps = count("probsT_ps", 2 * U)
            probsT_sb = count("probsT_sb", 2 * U)
            pv_ps = count("pv_ps", U)
            ao_ready = count("ao_ready", U)
            aoT_ps = count("aoT_ps", U)
            aoT_sb = count("aoT_sb", U)
            out_ps = count("out_ps", U, again=True)
            xb_ready = count("xb_ready", U, again=True)
            x3nT_ps = count("x3nT_ps", U)
            x3nT_sb = count("x3nT_sb", U)
            sel_ps = count("sel_ps", U)
            sig_ready = count("sig_ready", U)
            routed = count("routed", U, again=True)
            dve_step = count("dve_step", D_DVE_STEPS)

            with nc.Block() as block:
                @block.sync
                def _(sp):
                    start_at_one(sp, counts)
                    for n, name in enumerate(("Wq", "Wk", "Wv")):
                        sp.dma_start(wqkv[:, n], dram["L1_gnn_" + name].rearrange("(k p) f -> p k f", p=P)).then_inc(w_in, 16)
                    sp.dma_start(wo[:], dram["L1_gnn_Wo"].rearrange("(k p) f -> p k f", p=P)).then_inc(w_in, 16)
                    sp.dma_start(wsel[:], dram["L1_ffn_expert_sel"].rearrange("(k p) f -> p k f", p=P),
                                 allow_slow_non_contiguous=True).then_inc(w_in, 16)
                    for n, name in enumerate(("bq", "bk")):
                        sp.dma_start(bqk[:, n], dram["L1_gnn_" + name].rearrange("(k p) -> p k", p=P),
                                     allow_slow_non_contiguous=True).then_inc(w_in, 16)
                    sp.dma_start(bv[:], dram["L1_gnn_bv"].partition_broadcast(P)).then_inc(w_in, 16)
                    sp.dma_start(bo[:], dram["L1_gnn_bo"].partition_broadcast(P)).then_inc(w_in, 16)
                    with sp.Fori(0, TURNS) as it:
                        for u in range(U):
                            sp.wait_ge(xb_ready.sem, xb_ready.at(it, 0))
                            sp.dma_start(x[:, u], dram["x2"][it * U + u]).then_inc(x_in.sem, 16)

                @block.tensor
                def _(pe):
                    mm, tr = nc.tensor.matmul, nc.tensor.transpose
                    pe.wait_ge(w_in, 16 * 9)
                    with pe.Fori(0, TURNS) as it:
                        for u in range(U):
                            pe.wait_ge(routed.sem, routed.at(it, 0))
                            pe.wait_ge(xn_ready.sem, xn_ready.at(it, u + 1))
                            for k in range(2):
                                last = tr(ps[:, u, 0, P * k:P * k + P], xn[:, u, P * k:P * k + P], c["ident"][:])
                            last.then_inc(xnT_ps.sem, 1)
                        for u in range(U):
                            pe.wait_ge(xnT_sb.sem, xnT_sb.at(it, u + 1))
                            for n in range(2):
                                for m in range(2):
                                    for k in range(2):
                                        at = 2 * P * n + P * m
                                        last = mm(ps[:, u, 1, at:at + P], wqkv[:, n, k, P * m:P * m + P], xnT[:, u, k],
                                                  start=k == 0, stop=k == 1)
                            last.then_inc(qk_ps.sem, 1)
                            for k in range(2):
                                last = mm(ps[:, u, 2, 0:D], xnT[:, u, k], wqkv[:, 2, k], start=k == 0, stop=k == 1)
                            last.then_inc(v_ps.sem, 1)
                        for u in range(U):
                            pe.wait_ge(qk_sb.sem, qk_sb.at(it, u + 1))
                            pe.wait_ge(v_sb.sem, v_sb.at(it, u + 1))
                            for h in range(H):
                                part = slice(D1 * (h % 4), D1 * (h % 4) + D1)
                                at = P * (h // 4)
                                last = mm(ps[:, u, h % 4, at:at + P], qkT[part, u, 0, h // 4], qkT[part, u, 1, h // 4],
                                          start=True, stop=True)
                            last.then_inc(s_ps.sem, 1)
                        for u in range(U):
                            pe.wait_ge(probs_ready.sem, probs_ready.at(it, u + 1))
                            for half in range(2):
                                for q in range(4):
                                    last = tr(ps[:, u, half, P * q:P * q + P], probs[:, u, 4 * half + q], c["ident"][:])
                                last.then_inc(probsT_ps.sem, 1)
                        for u in range(U):
                            pe.wait_ge(probsT_sb.sem, probsT_sb.at(it, 2 * u + 2))
                            for h in range(H):
                                cols = slice(D1 * h, D1 * h + D1)
                                last = mm(ps[:, u, 2, cols], probsT[:, u, h], vals[:, u, cols], start=True, stop=True)
                            last.then_inc(pv_ps.sem, 1)
                        for u in range(U):
                            pe.wait_ge(ao_ready.sem, ao_ready.at(it, u + 1))
                            for k in range(2):
                                last = tr(ps[:, u, 3, P * k:P * k + P], ao[:, u, P * k:P * k + P], c["ident"][:])
                            last.then_inc(aoT_ps.sem, 1)
                        for u in range(U):
                            pe.wait_ge(aoT_sb.sem, aoT_sb.at(it, u + 1))
                            for k in range(2):
                                last = mm(ps[:, u, 2, D:2 * D], aoT[:, u, k], wo[:, k], start=k == 0, stop=k == 1)
                            last.then_inc(out_ps.sem, 1)
                        for u in range(U):
                            pe.wait_ge(xn_ready.sem, xn_ready.at(it, U + u + 1))
                            for k in range(2):
                                last = tr(ps[:, u, 0, P * k:P * k + P], xn[:, u, P * k:P * k + P], c["ident"][:])
                            last.then_inc(x3nT_ps.sem, 1)
                        for u in range(U):
                            pe.wait_ge(x3nT_sb.sem, x3nT_sb.at(it, u + 1))
                            for k in range(2):
                                last = mm(ps[:, u, 1, 0:E1], x3nT[:, u, k], wsel[:, k], start=k == 0, stop=k == 1)
                            last.then_inc(sel_ps.sem, 1)

                @block.scalar
                def _(act):
                    a = nc.scalar
                    act.wait_ge(w_in, 16 * 9)
                    with act.Fori(0, TURNS) as it:
                        for u in range(U):
                            act.wait_ge(xnT_ps.sem, xnT_ps.at(it, u + 1))
                            a.activation(xnT[:, u], ps[:, u, 0, 0:2 * P], ACT.Copy).then_inc(xnT_sb.sem, 1)
                        for u in range(U):
                            act.wait_ge(qk_ps.sem, qk_ps.at(it, u + 1))
                            for n in range(2):
                                for m in range(2):
                                    at = 2 * P * n + P * m
                                    last = a.activation(qkT[:, u, n, m], ps[:, u, 1, at:at + P], ACT.Identity,
                                                        bias=bqk[:, n, m:m + 1])
                            last.then_inc(qk_sb.sem, 1)
                        for u in range(U):
                            act.wait_ge(s_ready.sem, s_ready.at(it, u + 1))
                            for h in range(H):
                                last = a.activation(probs[:, u, h], s[:, u, h], ACT.Exp, bias=neg_max[:, u, h:h + 1],
                                                    accum_out=psum[:, u, h:h + 1])
                            last.then_inc(probs_ready.sem, 1)
                        for u in range(U):
                            for half in range(2):
                                act.wait_ge(probsT_ps.sem, probsT_ps.at(it, 2 * u + half + 1))
                                a.activation(probsT[:, u, 4 * half:4 * half + 4], ps[:, u, half], ACT.Copy).then_inc(probsT_sb.sem, 1)
                        for u in range(U):
                            act.wait_ge(aoT_ps.sem, aoT_ps.at(it, u + 1))
                            a.activation(aoT[:, u], ps[:, u, 3, 0:2 * P], ACT.Copy).then_inc(aoT_sb.sem, 1)
                        for u in range(U):
                            act.wait_ge(x3nT_ps.sem, x3nT_ps.at(it, u + 1))
                            src = ps[:, u, 0, 0:2 * P].rearrange("p (k t) -> p k t", k=2)
                            a.activation(xT_all[:, :, bass.ds((it * U + u) * P, P)], src, ACT.Copy)
                            a.activation(x3nT[:, u], src, ACT.Copy).then_inc(x3nT_sb.sem, 1)
                        for u in range(U):
                            act.wait_ge(sel_ps.sem, sel_ps.at(it, u + 1))
                            a.activation(sig_e[:, u], ps[:, u, 1, 0:E1], ACT.Exp, scale=-1.0).then_inc(sig_ready.sem, 1)

                @block.gpsimd
                def _(pool):
                    g = nc.gpsimd
                    pool.wait_ge(w_in, 16 * 9)
                    with pool.Fori(0, TURNS) as it:
                        for n in range(2):
                            pool.wait_ge(var_ready.sem, var_ready.at(it, n + 1))
                            g.tensor_tensor(rstd[:], var[:], c["minus_half"][:, 0:U], ALU.pow).then_inc(rstd_ready.sem, 1)
                            if n == 0:
                                pool.wait_ge(routed.sem, routed.at(it, 0))
                                pool.wait_ge(xn_ready.sem, xn_ready.at(it, U))
                                for u in range(U):
                                    g.tensor_tensor(xb[:, u], x[:, u], bo[:], ALU.add).then_inc(xb_ready.sem, 1)

                @block.vector
                def _(dve):
                    v = nc.vector
                    dve.wait_ge(w_in, 16 * 9)
                    with dve.Fori(0, TURNS) as it:
                        chain = Chain(dve_step, dve, it)

                        def layernorm(src, n):
                            for u in range(U):
                                if n == 0:
                                    dve.wait_ge(x_in.sem, x_in.at(it, U))
                                chain.done(v.bn_stats(stats[:, u], src[:, u]))
                                carry(nc, c)
                                chain.done(v.bn_aggr(mv[:, u], stats[:, u]))
                            v.tensor_scalar(var[:], mv[:, :, 1], LN_EPS, None, ALU.add).then_inc(var_ready.sem, 1)
                            dve.wait_ge(rstd_ready.sem, rstd_ready.at(it, n + 1))
                            for u in range(U):
                                v.tensor_scalar(xn[:, u], src[:, u], mv[:, u, 0:1], rstd[:, u:u + 1],
                                                ALU.subtract, ALU.mult).then_inc(xn_ready.sem, 1)

                        layernorm(x, 0)
                        for u in range(U):
                            dve.wait_ge(v_ps.sem, v_ps.at(it, u + 1))
                            v.tensor_tensor(vals[:, u], ps[:, u, 2, 0:D], bv[:], ALU.add).then_inc(v_sb.sem, 1)
                        for u in range(U):
                            dve.wait_ge(s_ps.sem, s_ps.at(it, u + 1))
                            for r in range(4):
                                last = v.scalar_tensor_tensor(s[:, u, r:H:4], ps[:, u, r, 0:2 * P].rearrange("p (h k) -> p h k", h=2),
                                                              SCALE, c["adj_off"][:].unsqueeze(1).to_broadcast([P, 2, P]),
                                                              ALU.mult, ALU.add)
                            chain.done(last)
                            v.tensor_reduce(neg_max[:, u], s[:, u], AX.X, ALU.max, negate=True).then_inc(s_ready.sem, 1)
                        for u in range(U):
                            dve.wait_ge(pv_ps.sem, pv_ps.at(it, u + 1))
                            chain.done(v.reciprocal(prec[:, u], psum[:, u]))
                            v.tensor_tensor(ao[:, u].rearrange("p (h d) -> p h d", d=D1), ps[:, u, 2, 0:D].rearrange("p (h d) -> p h d", d=D1),
                                            prec[:, u].unsqueeze(2).to_broadcast([P, H, D1]), ALU.mult).then_inc(ao_ready.sem, 1)
                        dve.wait_ge(xb_ready.sem, xb_ready.at(it, U))
                        for u in range(U):
                            dve.wait_ge(out_ps.sem, out_ps.at(it, u + 1))
                            v.tensor_tensor(acc[:, bass.ds(it * U + u, 1)].rearrange("p a d -> p (a d)"), ps[:, u, 2, D:2 * D], xb[:, u], ALU.add)
                            chain.done(v.tensor_tensor(x3[:, u], ps[:, u, 2, D:2 * D], xb[:, u], ALU.add))
                        layernorm(x3, 1)
                        for u in range(U):
                            dve.wait_ge(sig_ready.sem, sig_ready.at(it, u + 1))
                            chain.done(v.tensor_scalar(sig_d[:, u], sig_e[:, u], 1.0, None, ALU.add))
                            chain.done(v.reciprocal(sig[:, u], sig_d[:, u]))
                            carry(nc, c)
                            chain.done(v.max(top[:, u], sig[:, u]))
                            carry(nc, c)
                            chain.done(v.max_index(top_i[:, u], top[:, u], sig[:, u]))
                            chain.done(v.tensor_copy(top_f[:, u], top_i[:, u]))
                            v.tensor_scalar(w1[:, u], c["row0"][:, 0:E1], top_f[:, u, 0:1], top[:, u, 0:1], ALU.is_equal, ALU.mult)
                            chain.done(v.tensor_scalar(w2[:, u], c["row0"][:, 0:E1], top_f[:, u, 1:2], top[:, u, 1:2],
                                                       ALU.is_equal, ALU.mult))
                            v.tensor_tensor(w_all[:, bass.ds(it * U + u, 1)].rearrange("p a e -> p (a e)"), w1[:, u], w2[:, u],
                                            ALU.add).then_inc(routed.sem, 1)
                        chain.close()
                    dve.wait_ge(routed.sem, routed.at(TURNS, 0))

        sb = sb_in(ctx)
        keys = sb("e_keys", [P, SLOTS * 2, H1])
        values = sb("e_values", [P, SLOTS, D])
        hidden = sb("e_hidden", [P, SLOTS, TOKENS])
        ps_h = ctx.enter_context(nc.psum_tensor("e_ps_h", [P, SLOTS, TOKENS], F32))
        ps_o = ctx.enter_context(nc.psum_tensor("e_ps_o", [P, SLOTS, G4, D], F32))
        attention_counts = len(counts)
        weights_in = count("weights_in", 2, 16)
        hidden_ps = count("hidden_ps", SLOTS)
        hidden_ready = count("hidden_ready", SLOTS, again=True)
        out_ps = count("expert_ps", SLOTS, again=True)
        added = count("added", SLOTS, again=True)
        stored = count("stored", NB, 16)
        expert_counts = counts[attention_counts:]

        with nc.Block() as block:
            @block.sync
            def _(sp):
                start_at_one(sp, expert_counts)
                with sp.Fori(0, PAIRS) as pair:
                    sp.wait_ge(out_ps.sem, out_ps.at(pair * GROUPS, 0))
                    two = bass.ds(pair * SLOTS, SLOTS)
                    sp.dma_start(keys[:], dram["L1_ffn_keys"][two].rearrange("n (k p) f -> p (n k) f", p=P)).then_inc(weights_in.sem, 16)
                    sp.dma_start(values[:], dram["L1_ffn_values"][two].rearrange("n p f -> p n f")).then_inc(weights_in.sem, 16)
                sp.wait_ge(added.sem, added.at(PAIRS * GROUPS, 0))
                with sp.Fori(0, NB) as b:
                    sp.dma_start(dram["out"][b], acc[:, bass.ds(b, 1)].rearrange("p a d -> p (a d)")).then_inc(stored.sem, 16)
                sp.wait_ge(stored.sem, stored.at(1, 0))

            @block.tensor
            def _(pe):
                mm = nc.tensor.matmul
                with pe.Fori(0, PAIRS) as pair:
                    with pe.Fori(0, GROUPS) as group:
                        turn = pair * GROUPS + group
                        pe.wait_ge(weights_in.sem, weights_in.at(pair, 2))
                        for n in range(SLOTS):
                            pe.wait_ge(hidden_ready.sem, hidden_ready.at(turn, 0))
                            for k in range(2):
                                last = mm(ps_h[:, n], keys[:, 2 * n + k], xT_all[:, k, bass.ds(group * TOKENS, TOKENS)],
                                          start=k == 0, stop=k == 1)
                            last.then_inc(hidden_ps.sem, 1)
                        for n in range(SLOTS):
                            pe.wait_ge(hidden_ready.sem, hidden_ready.at(turn, n + 1))
                            pe.wait_ge(added.sem, added.at(turn, 0))
                            for q in range(G4):
                                last = mm(ps_o[:, n, q], hidden[:, n, P * q:P * q + P], values[:, n], start=True, stop=True)
                            last.then_inc(out_ps.sem, 1)

            @block.scalar
            def _(act):
                with act.Fori(0, PAIRS * GROUPS) as turn:
                    for n in range(SLOTS):
                        act.wait_ge(out_ps.sem, out_ps.at(turn, 0))
                        act.wait_ge(hidden_ps.sem, hidden_ps.at(turn, n + 1))
                        nc.scalar.activation(hidden[:, n], ps_h[:, n], ACT.Relu).then_inc(hidden_ready.sem, 1)

            @block.vector
            def _(dve):
                v = nc.vector
                with dve.Fori(0, PAIRS) as pair:
                    with dve.Fori(0, GROUPS) as group:
                        turn = pair * GROUPS + group
                        for n in range(SLOTS):
                            dve.wait_ge(out_ps.sem, out_ps.at(turn, n + 1))
                            dve.wait_ge(added.sem, added.at(turn, n))
                            for q in range(G4):
                                b = group * G4 + q
                                y = acc[:, bass.ds(b, 1)].rearrange("p a d -> p (a d)")
                                w = w_all[:, bass.ds(b, 1), bass.ds(pair * SLOTS + n, 1)].rearrange("p a e -> p (a e)")
                                last = v.scalar_tensor_tensor(y, ps_o[:, n, q], w, y, ALU.mult, ALU.add)
                            last.then_inc(added.sem, 1)


def program(nc, ins, out, upto="E"):
    dram = dict(ins)
    NB = ins["x"].shape[0]
    dram["out"] = out

    def scratch(name, shape, dt=F32):
        dram[name] = nc.dram_tensor("scratch_" + name, [NB] + shape, dt, kind="Internal").ap()

    scratch("x1", [P, D])
    scratch("gate", [P, HD])
    scratch("mask", [P, R + P], BF16)
    scratch("perm", [P, 2, P])
    scratch("rowg", [P, 2, H])
    scratch("rowb", [P, 2, H])
    scratch("roww", [P, 2])
    scratch("vp", [P, 2, HD])
    scratch("kqT", [P, 2, 4, R])
    scratch("acomp", [P, 2, H, BK])
    scratch("x2", [P, D])
    scratch("inv", [P, 2, H, BK])
    with ExitStack() as ctx:
        c = constants(nc, ctx, dram)
        phase_rows(nc, c, dram, NB)
        if upto >= "B":
            phase_invert(nc, c, dram, NB)
        if upto >= "C":
            phase_mix(nc, c, dram, NB)
        if upto >= "E":
            phase_experts(nc, c, dram, NB)


TRANSPOSED = ("L1_gnn_Wq", "L1_gnn_Wk", "L1_gnn_Wv", "L1_gnn_Wo", "L1_ffn_expert_sel")


def kernel(**inputs):
    import concourse.bacc as bacc
    from concourse.bass_utils import run_bass_kernel_spmd

    nc = bacc.Bacc("TRN2", target_bir_lowering=False, num_devices=1)
    arrays, ins = {}, {}
    for name, a in inputs.items():
        a = np.asarray(a)
        a = np.ascontiguousarray(a.T if name in TRANSPOSED else a)
        arrays["in_" + name] = a
        ins[name] = nc.dram_tensor("in_" + name, a.shape, mybir.dt.from_np(a.dtype), kind="ExternalInput").ap()
    out = nc.dram_tensor("out", inputs["x"].shape, F32, kind="ExternalOutput").ap()
    program(nc, ins, out)
    r = run_bass_kernel_spmd(nc, [arrays], core_ids=[0])
    return r.results[0]["out"]
```

```python
from contextlib import ExitStack

import numpy as np
import concourse.bass as bass
from concourse import mybir

ALU = mybir.AluOpType
ACT = mybir.ActivationFunctionType
AX = mybir.AxisListType
F32 = mybir.dt.float32
BF16 = mybir.dt.bfloat16
I32 = mybir.dt.int32
U32 = mybir.dt.uint32

P = 128
D = 256
F1 = 128
H = 8
DK = 64
HD = H * DK
E0 = 4
TOPK = 2
R = TOPK * P
BK = 32
NB_ = P // BK
D1 = 32
E1 = 32
H1 = 128
U = 2
SMALL = E0 + 2 * H
ROWV = 2 * H + 2 * E0
LN_EPS = 1e-5
BIG = 32768.0
NEG = -1.0e9
OFF = -1.0e30


class Count:

    def __init__(self, ctx, nc, name, per, unit=1, again=False):
        self.sem = ctx.enter_context(nc.semaphore(name))
        self.per, self.unit, self.first = per, unit, int(again)

    def at(self, turn, k):
        assert k or self.first or (isinstance(turn, int) and turn)
        return turn * (self.per * self.unit) + (k * self.unit + self.first)


def start_at_one(engine, counts):
    for count in counts:
        if count.first:
            engine.sem_inc(count.sem, 1)


class Chain:

    def __init__(self, count, engine, turn):
        self.count, self.engine, self.turn, self.k = count, engine, turn, 0

    def done(self, instruction):
        self.k += 1
        instruction.then_inc(self.count.sem, 1)
        self.engine.wait_ge(self.count.sem, self.count.at(self.turn, self.k))

    def close(self):
        assert self.k == self.count.per, (self.k, self.count.per)


def carry(nc, c):
    nc.vector.memset(c["pad"][:], 0.0)


def hold(engine):
    engine.nop(nofuse=True)


def constants(nc, ctx, dram):
    def sb(name, shape, dt=F32):
        return ctx.enter_context(nc.sbuf_tensor(name, shape, dt))

    c = {
        "ident": sb("ident", [P, P]),
        "big_ident": sb("big_ident", [P, P], BF16),
        "before": sb("before", [P, P], BF16),
        "ones_bf": sb("ones_bf", [P, P], BF16),
        "ones": sb("ones", [P, P]),
        "after": sb("after", [P, P]),
        "after_block": sb("after_block", [P, P]),
        "upto": sb("upto", [P, P]),
        "upto_block": sb("upto_block", [P, BK]),
        "col_block": sb("col_block", [P, P]),
        "my_block": sb("my_block", [P, 1]),
        "in_block": sb("in_block", [P, 1]),
        "causal": sb("causal", [P, P]),
        "row1": sb("row1", [P, R]),
        "row0": sb("row0", [P, R]),
        "rowid": sb("rowid", [P, 2]),
        "adj_neg": sb("adj_neg", [P, P]),
        "adj_off": sb("adj_off", [P, P]),
        "adj_i": sb("adj_i", [P, P], I32),
        "adj_f": sb("adj_f", [P, P]),
        "dt_bias": sb("dt_bias", [P, H]),
        "neg_a": sb("neg_a", [P, H]),
        "a_log": sb("a_log", [P, H]),
        "norm_w": sb("norm_w", [P, DK]),
        "norm_w0": sb("norm_w0", [P, DK]),
        "pad": sb("pad", [P, 1]),
        "minus_half": sb("minus_half", [P, 2 * U * 2 * H]),
    }
    made = c["made"] = ctx.enter_context(nc.semaphore("const_made"))
    zeroed = ctx.enter_context(nc.semaphore("const_zeroed"))
    params = ctx.enter_context(nc.semaphore("params_loaded"))
    steps = ctx.enter_context(nc.semaphore("const_steps"))
    acted = ctx.enter_context(nc.semaphore("const_exp"))

    with nc.Block() as block:
        @block.sync
        def _(sp):
            sp.dma_start(c["adj_i"][:], dram["adj"]).then_inc(params, 16)
            sp.dma_start(c["dt_bias"][:], dram["L0_ffn_dt_bias"].partition_broadcast(P)).then_inc(params, 16)
            sp.dma_start(c["a_log"][:], dram["L0_ffn_A_log"].partition_broadcast(P)).then_inc(params, 16)
            sp.dma_start(c["norm_w0"][:], dram["L0_ffn_o_norm_weight"].partition_broadcast(P)).then_inc(params, 16)

        @block.gpsimd
        def _(pool):
            g = nc.gpsimd
            for name, value in (("ident", 0.0), ("big_ident", 0.0), ("before", 1.0), ("ones_bf", 1.0), ("ones", 1.0),
                                ("after", 1.0), ("upto", 1.0),
                                ("causal", -1.0), ("minus_half", -0.5)):
                last = g.memset(c[name][:], value)
            last.then_inc(zeroed, 1)
            pool.wait_ge(zeroed, 1)

            def keep(ap, pattern, base, cm, fill, op=ALU.is_ge):
                return g.affine_select(out=ap, in_=ap, pattern=pattern, compare_op=op, fill=fill,
                                       base=base, channel_multiplier=cm)

            keep(c["ident"][:], [[-1, P]], 0, 1, 1.0, ALU.not_equal)
            keep(c["big_ident"][:], [[-1, P]], 0, 1, BIG, ALU.not_equal)
            keep(c["before"][:], [[1, P]], -1, -1, 0.0)
            keep(c["after"][:], [[-1, P]], -1, 1, 0.0)
            keep(c["upto"][:], [[1, P]], 0, -1, 0.0)
            g.iota(c["col_block"][:].rearrange("p (k i) -> p k i", i=BK), [[1, NB_], [0, BK]], base=0, channel_multiplier=0,
                   allow_small_or_imprecise_dtypes=True)
            keep(c["causal"][:], [[1, P]], 0, -1, -2.0)
            g.iota(c["row1"][:], [[1, R]], base=1, channel_multiplier=0, allow_small_or_imprecise_dtypes=True)
            g.iota(c["row0"][:], [[1, R]], base=0, channel_multiplier=0, allow_small_or_imprecise_dtypes=True)
            g.iota(c["rowid"][:], [[P, 2]], base=0, channel_multiplier=1,
                   allow_small_or_imprecise_dtypes=True).then_inc(made, 1)

        @block.scalar
        def _(act):
            act.wait_ge(params, 64)
            nc.scalar.activation(c["neg_a"][:], c["a_log"][:], ACT.Exp).then_inc(acted, 1)

        @block.vector
        def _(dve):
            v = nc.vector
            dve.wait_ge(params, 64)
            v.tensor_scalar(c["norm_w"][:], c["norm_w0"][:], 0.5, None, ALU.mult)
            v.tensor_copy(c["adj_f"][:], c["adj_i"][:]).then_inc(steps, 1)
            dve.wait_ge(steps, 1)
            v.tensor_scalar(c["adj_neg"][:], c["adj_f"][:], -NEG, NEG, ALU.mult, ALU.add)
            v.tensor_scalar(c["adj_off"][:], c["adj_f"][:], 0.0, OFF, ALU.is_equal, ALU.mult)
            dve.wait_ge(acted, 1)
            v.tensor_scalar(c["neg_a"][:], c["neg_a"][:], -1.0, None, ALU.mult).then_inc(steps, 1)
            dve.wait_ge(steps, 2)
            dve.wait_ge(made, 1)
            v.tensor_scalar(c["my_block"][:], c["rowid"][:, 0:1], float(BK), None, ALU.is_ge).then_inc(steps, 1)
            for k in range(2, NB_):
                dve.wait_ge(steps, k + 1)
                v.scalar_tensor_tensor(c["my_block"][:], c["rowid"][:, 0:1], float(BK * k), c["my_block"][:],
                                       ALU.is_ge, ALU.add).then_inc(steps, 1)
            dve.wait_ge(steps, 5)
            v.scalar_tensor_tensor(c["in_block"][:], c["my_block"][:], -float(BK), c["rowid"][:, 0:1], ALU.mult, ALU.add)
            v.scalar_tensor_tensor(c["after_block"][:], c["col_block"][:], c["my_block"][:], c["after"][:],
                                   ALU.is_equal, ALU.mult).then_inc(steps, 1)
            dve.wait_ge(steps, 6)
            v.tensor_scalar(c["upto_block"][:], c["row0"][:, 0:BK], c["in_block"][:], None, ALU.is_ge).then_inc(steps, 1)
            dve.wait_ge(steps, 7)
    return c

A_DVE_STEPS = 61
A_POOL_STEPS = 1
C_DVE_STEPS = 7
D_DVE_STEPS = 16


def phase_rows(nc, c, dram, NB):
    TURNS = NB // U
    ctx = ExitStack()
    counts = []

    def sb(name, shape, dt=F32):
        return ctx.enter_context(nc.sbuf_tensor(name, shape, dt))

    def count(name, per, unit=1, again=False):
        counts.append(Count(ctx, nc, "a_" + name, per, unit, again))
        return counts[-1]

    with ctx:
        w0 = sb("a_w0", [P, 2, F1])
        att = sb("a_att", [P, 2])
        att_b = sb("a_att_b", [P, 2, P])
        wqkvg = sb("a_wqkvg", [P, 4, 2, HD])
        wsmall = sb("a_wsmall", [P, 2, SMALL])
        x = sb("a_x", [P, U, D])
        stats = sb("a_stats", [P, U, 6])
        mv = sb("a_mv", [P, U, 2])
        var = sb("a_var", [P, U])
        rstd = sb("a_rstd", [P, U])
        xn = sb("a_xn", [P, U, D])
        xnT = sb("a_xnT", [P, U, 2, P])
        hh = sb("a_hh", [P, U, 2, P])
        e_low = sb("a_e_low", [P, U, P])
        e_act = sb("a_e_act", [P, U, P])
        e_masked = sb("a_e_masked", [P, U, P])
        e_max = sb("a_e_max", [P, U])
        e_neg_max = sb("a_e_neg_max", [P, U])
        probs = sb("a_probs", [P, U, P])
        probsT = sb("a_probsT", [P, U, P])
        p_sum = sb("a_p_sum", [P, U])
        p_rec = sb("a_p_rec", [P, U])
        x1 = sb("a_x1", [P, U, D])
        x1nT = sb("a_x1nT", [P, U, 2, P])
        tanh = sb("a_tanh", [P, U, 4, HD])
        qk = sb("a_qk", [P, U, 2, HD])
        qk_sq = sb("a_qk_sq", [P, U, 2 * H, DK])
        ss = sb("a_ss", [P, U, 2 * H])
        rnorm = sb("a_rnorm", [P, U, 2 * H])
        vv = sb("a_vv", [P, U, HD])
        gg = sb("a_gg", [P, U, HD])
        gate = sb("a_gate", [P, U, HD])
        lmax = sb("a_lmax", [P, U])
        ez = sb("a_ez", [P, U, SMALL])
        zz = sb("a_zz", [P, U, H])
        ex = sb("a_ex", [P, U, SMALL])
        den = sb("a_den", [P, U, 2 * H + 1])
        rec = sb("a_rec", [P, U, 2 * H + 1])
        s1 = sb("a_s1", [P, U, H])
        s2 = sb("a_s2", [P, U, H])
        poly = sb("a_poly", [P, U, H])
        scores = sb("a_scores", [P, U, 8])
        top = sb("a_top", [P, U, 8])
        top_i = sb("a_top_i", [P, U, 8], U32)
        top_f = sb("a_top_f", [P, U, 8])
        sel = sb("a_sel", [P, U, E0])
        sel_bf = sb("a_sel_bf", [P, U, 2, E0], BF16)
        wun = sb("a_wun", [P, U, E0])
        wsum = sb("a_wsum", [P, U])
        wrec = sb("a_wrec", [P, U])
        tokv = sb("a_tokv", [P, U, ROWV])
        place = sb("a_place", [P, U, 2, E0])
        place1 = sb("a_place1", [P, U, E0])
        pT = sb("a_pT", [P, U, R])
        pP = sb("a_pP", [P, U, 2, P])
        eid = sb("a_eid", [P, U, R])
        from_e = sb("a_from_e", [P, U, 2, E0 + 1])
        eid_row = sb("a_eid_row", [P, U, 2])
        onehot = sb("a_onehot", [P, U, 2, E0])
        rv = sb("a_rv", [P, U, 2, ROWV])
        picked = sb("a_picked", [P, U, 2, 2, E0])
        w_act = sb("a_w_act", [P, U, 2, 2])
        rowg = sb("a_rowg", [P, U, 2, H])
        rowb = sb("a_rowb", [P, U, 2, H])
        roww = sb("a_roww", [P, U, 2])
        mask = sb("a_mask", [P, U, 2, P], BF16)
        mask_c = sb("a_mask_c", [P, U, 2, BK], BF16)
        straddle = sb("a_straddle", [P, U, 2])
        edge_e = sb("a_edge_e", [P, U, 2, H])
        edge = sb("a_edge", [P, U, 2, H])
        kqT = sb("a_kqT", [P, U, 2, 4, R])
        krow = sb("a_krow", [P, U, HD])
        vp = sb("a_vp", [P, U, 2, HD])
        gdecay = sb("a_gdecay", [P, U, 2, H, BK])
        decay = sb("a_decay", [P, U, 2, H, BK])
        acomp = sb("a_acomp", [P, U, 2, H, BK])

        ps = ctx.enter_context(nc.psum_tensor("a_ps", [P, U, 3, 512], F32))
        ps_small = ctx.enter_context(nc.psum_tensor("a_ps_small", [P, 512], F32))
        ps_perm = ctx.enter_context(nc.psum_tensor("a_ps_perm", [P, U, 2, P], F32))
        sm_proj = ps_small[:, 0:U * SMALL].rearrange("p (u s) -> p u s", u=U)
        sm_place = ps_small[:, 64:64 + U * 2 * E0].rearrange("p (u a e) -> p u a e", u=U, a=2)
        sm_row = ps_small[:, 128:128 + U * 2 * ROWV].rearrange("p (u t s) -> p u t s", u=U, t=2)

        sm_edge = ps[:, :, 0, 256:256 + 2 * H].rearrange("p u (t h) -> p u t h", t=2)

        w_in = ctx.enter_context(nc.semaphore("a_w_in"))
        att_ready = ctx.enter_context(nc.semaphore("a_att_ready"))
        x_in = count("x_in", U, 16)
        xn_ready = count("xn_ready", 2 * U)
        var_ready = count("var_ready", 2)
        rstd_ready = count("rstd_ready", 2)
        xnT_ps = count("xnT_ps", U)
        xnT_sb = count("xnT_sb", U)
        h_ps = count("h_ps", U)
        h_sb = count("h_sb", U)
        e_ps = count("e_ps", U)
        e_ready = count("e_ready", U)
        probs_ready = count("probs_ready", U)
        pT_ps = count("probsT_ps", U)
        pT_sb = count("probsT_sb", U)
        o_ps = count("o_ps", U)
        x1_ready = count("x1_ready", U, again=True)
        x1nT_ps = count("x1nT_ps", U, again=True)
        x1nT_sb = count("x1nT_sb", U)
        small_ps = count("small_ps", U)
        ez_ready = count("ez_ready", 1)
        ex_ready = count("ex_ready", 1)
        proj_ps = count("proj_ps", 4 * U)
        tanh_ready = count("tanh_ready", 4 * U)
        proj_sb = count("proj_sb", 4 * U)
        sq_ready = count("sq_ready", U)
        ss_ready = count("ss_ready", 1)
        rnorm_ready = count("rnorm_ready", 1)
        qk_ready = count("qk_ready", U)
        gate_ready = count("gate_ready", U)
        sel_ready = count("sel_ready", 1)
        place_ps = count("place_ps", 1)
        perm_ready = count("perm_ready", U)
        rows_ps = count("rows_ps", U)
        P_sb = count("P_sb", 1)
        mask_ready = count("mask_ready", U)
        mask_c_ready = count("mask_c_ready", U)
        rowv_ready = count("rowv_ready", 1)
        perm_ps = count("perm_ps", 7 * U)
        perm_sb = count("perm_sb", 7 * U)
        gdecay_ready = count("gdecay_ready", U)
        compact_ps = count("compact_ps", U)
        decay_ready = count("decay_ready", U)
        acomp_ready = count("acomp_ready", U, again=True)
        x1_out = count("x1_out", U, 16, again=True)
        out = count("out", 11 * U, 16, again=True)
        ln_first = count("ln_first", 2 * U)
        ln_second = count("ln_second", 2 * U)
        dve_step = count("dve_step", A_DVE_STEPS)
        pool_step = count("pool_step", A_POOL_STEPS)

        with nc.Block() as block:
            @block.sync
            def _(sp):
                start_at_one(sp, counts)
                sp.dma_start(w0[:], dram["L0_gnn_W"].rearrange("(k p) f -> p k f", p=P)).then_inc(w_in, 16)
                sp.dma_start(att[:], dram["L0_gnn_a"].rearrange("a o d -> o (a d)"),
                             allow_slow_non_contiguous=True).then_inc(w_in, 16)
                for n, name in enumerate(("Wq", "Wk", "Wv", "Wg")):
                    sp.dma_start(wqkvg[:, n], dram["L0_ffn_" + name].rearrange("(k p) f -> p k f", p=P)).then_inc(w_in, 16)
                at = 0
                for name, width in (("Wgate", E0), ("Wb", H), ("Wa", H)):
                    sp.dma_start(wsmall[:, :, at:at + width],
                                 dram["L0_ffn_" + name].rearrange("(k p) f -> p k f", p=P),
                                 allow_slow_non_contiguous=True).then_inc(w_in, 16)
                    at += width

                def load(it):
                    for u in range(U):
                        b = it * U + u
                        sp.wait_ge(x1_ready.sem, x1_ready.at(it, 0))
                        hold(sp)
                        sp.dma_start(x[:, u], dram["x"][b]).then_inc(x_in.sem, 16)

                def turn(it, following):
                    for u in range(U):
                        b = it * U + u
                        sp.wait_ge(x1_ready.sem, x1_ready.at(it, u + 1))
                        hold(sp)
                        sp.dma_start(dram["x1"][b], x1[:, u]).then_inc(x1_out.sem, 16)
                    if following is not None:
                        load(following)
                    for u in range(U):
                        b = it * U + u
                        sp.wait_ge(gate_ready.sem, gate_ready.at(it, u + 1))
                        hold(sp)
                        sp.dma_start(dram["gate"][b], gate[:, u]).then_inc(out.sem, 16)
                        sp.wait_ge(mask_ready.sem, mask_ready.at(it, u + 1))
                        hold(sp)
                        sp.dma_start(dram["mask"][b], mask[:, u]).then_inc(out.sem, 16)
                    sp.wait_ge(P_sb.sem, P_sb.at(it, 1))
                    hold(sp)
                    sp.wait_ge(rowv_ready.sem, rowv_ready.at(it, 1))
                    hold(sp)
                    for u in range(U):
                        b = it * U + u
                        sp.dma_start(dram["perm"][b], pP[:, u]).then_inc(out.sem, 16)
                        sp.dma_start(dram["rowg"][b], rowg[:, u]).then_inc(out.sem, 16)
                        sp.dma_start(dram["rowb"][b], rowb[:, u]).then_inc(out.sem, 16)
                        sp.dma_start(dram["roww"][b], roww[:, u]).then_inc(out.sem, 16)
                    sp.wait_ge(perm_sb.sem, perm_sb.at(it, 7 * U))
                    hold(sp)
                    for u in range(U):
                        b = it * U + u
                        sp.dma_start(dram["vp"][b], vp[:, u]).then_inc(out.sem, 16)
                        sp.dma_start(dram["krow"][b], krow[:, u]).then_inc(out.sem, 16)
                        sp.dma_start(dram["kqT"][b], kqT[:, u]).then_inc(out.sem, 16)
                    for u in range(U):
                        b = it * U + u
                        sp.wait_ge(acomp_ready.sem, acomp_ready.at(it, u + 1))
                        hold(sp)
                        sp.dma_start(dram["acomp"][b], acomp[:, u]).then_inc(out.sem, 16)
                        sp.dma_start(dram["edge"][b], edge[:, u]).then_inc(out.sem, 16)

                load(0)
                with sp.Fori(0, TURNS - 1) as it:
                    turn(it, it + 1)
                turn(TURNS - 1, None)
                sp.wait_ge(x1_out.sem, x1_out.at(TURNS, 0))
                sp.wait_ge(out.sem, out.at(TURNS, 0))

            @block.tensor
            def _(pe):
                mm, tr = nc.tensor.matmul, nc.tensor.transpose

                def places(it):
                    pe.wait_ge(sel_ready.sem, sel_ready.at(it, 1))
                    for u in range(U):
                        mm(sm_place[:, u, 0], c["before"][:], sel_bf[:, u, 0], start=True, stop=False)
                        mm(sm_place[:, u, 0], c["ones_bf"][:], sel_bf[:, u, 1], start=False, stop=True)
                        last = mm(sm_place[:, u, 1], c["ones_bf"][:], sel_bf[:, u, 1], start=True, stop=True)
                    last.then_inc(place_ps.sem, 1)

                pe.wait_ge(w_in, 16 * 9)
                pe.wait_ge(att_ready, 1)
                with pe.Fori(0, TURNS) as it:
                    for u in range(U):
                        pe.wait_ge(acomp_ready.sem, acomp_ready.at(it, 0))
                        pe.wait_ge(xn_ready.sem, xn_ready.at(it, u + 1))
                        for k in range(2):
                            last = tr(ps[:, u, 0, P * k:P * k + P], xn[:, u, P * k:P * k + P], c["ident"][:])
                        last.then_inc(xnT_ps.sem, 1)
                    for u in range(U):
                        pe.wait_ge(xnT_sb.sem, xnT_sb.at(it, u + 1))
                        for k in range(2):
                            mm(ps[:, u, 1, 0:P], xnT[:, u, k], w0[:, k], start=k == 0, stop=k == 1)
                        for k in range(2):
                            last = mm(ps[:, u, 1, P:2 * P], w0[:, k], xnT[:, u, k], start=k == 0, stop=k == 1)
                        last.then_inc(h_ps.sem, 1)
                    for u in range(U):
                        pe.wait_ge(h_sb.sem, h_sb.at(it, u + 1))
                        mm(ps[:, u, 2, 0:P], hh[:, u, 1], att_b[:, 0], start=True, stop=False)
                        mm(ps[:, u, 2, 0:P], att_b[:, 1], hh[:, u, 1], start=False, stop=True).then_inc(e_ps.sem, 1)
                    for u in range(U):
                        pe.wait_ge(probs_ready.sem, probs_ready.at(it, u + 1))
                        tr(ps[:, u, 2, P:2 * P], probs[:, u], c["ident"][:]).then_inc(pT_ps.sem, 1)
                    for u in range(U):
                        pe.wait_ge(pT_sb.sem, pT_sb.at(it, u + 1))
                        mm(ps[:, u, 2, 2 * P:3 * P], probsT[:, u], hh[:, u, 0], start=True, stop=True).then_inc(o_ps.sem, 1)
                    for u in range(U):
                        pe.wait_ge(xn_ready.sem, xn_ready.at(it, U + u + 1))
                        for k in range(2):
                            last = tr(ps[:, u, 0, 2 * P + P * k:3 * P + P * k], xn[:, u, P * k:P * k + P], c["ident"][:])
                        last.then_inc(x1nT_ps.sem, 1)
                    for u in range(U):
                        pe.wait_ge(x1nT_sb.sem, x1nT_sb.at(it, u + 1))
                        for k in range(2):
                            last = mm(sm_proj[:, u], x1nT[:, u, k], wsmall[:, k], start=k == 0, stop=k == 1)
                        last.then_inc(small_ps.sem, 1)
                    for n, bank in enumerate((1, 2, 0, 1)):
                        if n == 2:
                            places(it)
                        for u in range(U):
                            if n == 3:
                                pe.wait_ge(proj_sb.sem, proj_sb.at(it, u + 1))
                            for k in range(2):
                                last = mm(ps[:, u, bank], x1nT[:, u, k], wqkvg[:, n, k], start=k == 0, stop=k == 1)
                            last.then_inc(proj_ps.sem, 1)
                    for u in range(U):
                        pe.wait_ge(perm_ready.sem, perm_ready.at(it, u + 1))
                        for t in range(2):
                            rows = slice(P * t, P * t + P)
                            tr(ps_perm[:, u, t], pT[:, u, rows], c["ident"][:])
                            last = mm(sm_row[:, u, t], pT[:, u, rows], tokv[:, u], start=True, stop=True)
                        last.then_inc(rows_ps.sem, 1)
                    pe.wait_ge(proj_sb.sem, proj_sb.at(it, 4 * U))
                    for n in range(7):
                        for u in range(U):
                            if n == 2:
                                pe.wait_ge(qk_ready.sem, qk_ready.at(it, u + 1))
                            if n >= 3:
                                pe.wait_ge(perm_sb.sem, perm_sb.at(it, (n - 3) * U + u + 1))
                            if n < 2:
                                last = mm(ps[:, u, n], pT[:, u, P * n:P * n + P], vv[:, u], start=True, stop=True)
                            elif n == 6:
                                last = mm(ps[:, u, 0], pT[:, u, 0:P], qk[:, u, 1], start=True, stop=True)
                            else:
                                which, half = (1, n - 2) if n < 4 else (0, n - 4)
                                for q in range(2):
                                    pair = 2 * half + q
                                    last = mm(ps[:, u, n % 3, R * q:R * q + R], qk[:, u, which, P * pair:P * pair + P],
                                              pT[:, u], start=True, stop=True)
                            last.then_inc(perm_ps.sem, 1)
                    for u in range(U):
                        pe.wait_ge(perm_sb.sem, perm_sb.at(it, 6 * U + u + 1))
                        pe.wait_ge(gdecay_ready.sem, gdecay_ready.at(it, u + 1))
                        pe.wait_ge(mask_c_ready.sem, mask_c_ready.at(it, u + 1))
                        mm(sm_edge[:, u, 0], c["after"][:], rowg[:, u, 0], start=True, stop=True)
                        mm(sm_edge[:, u, 1], c["upto"][:], rowg[:, u, 1], start=True, stop=True)
                        for t in range(2):
                            dst = ps[:, u, 2, H * BK * t:H * BK * (t + 1)].rearrange("p (h i) -> p h i", h=H)
                            mm(dst, c["after_block"][:], gdecay[:, u, t], start=True, stop=False)
                            mm(dst, c["big_ident"][:], mask_c[:, u, t].unsqueeze(1).to_broadcast([P, H, BK]),
                               start=False, stop=True)
                        for t in range(2):
                            for h in range(H):
                                part = slice(DK * (h % 2), DK * (h % 2) + DK)
                                for k in range(NB_):
                                    kT = kqT[part, u, 0, h // 2, P * t + BK * k:P * t + BK * k + BK]
                                    at = (t * 4 + h // 2) * BK
                                    last = mm(ps[BK * k:BK * k + BK, u, h % 2, at:at + BK], kT, kT, start=True, stop=True)
                        last.then_inc(compact_ps.sem, 1)

            @block.scalar
            def _(act):
                a = nc.scalar
                with act.Fori(0, TURNS) as it:
                    for u in range(U):
                        act.wait_ge(xnT_ps.sem, xnT_ps.at(it, u + 1))
                        a.activation(xnT[:, u], ps[:, u, 0, 0:2 * P], ACT.Copy).then_inc(xnT_sb.sem, 1)
                    for u in range(U):
                        act.wait_ge(h_ps.sem, h_ps.at(it, u + 1))
                        a.activation(hh[:, u], ps[:, u, 1, 0:2 * P], ACT.Copy).then_inc(h_sb.sem, 1)
                    for u in range(U):
                        act.wait_ge(e_ready.sem, e_ready.at(it, u + 1))
                        a.activation(probs[:, u], e_masked[:, u], ACT.Exp, bias=e_neg_max[:, u:u + 1],
                                     accum_out=p_sum[:, u:u + 1]).then_inc(probs_ready.sem, 1)
                    for u in range(U):
                        act.wait_ge(pT_ps.sem, pT_ps.at(it, u + 1))
                        a.activation(probsT[:, u], ps[:, u, 2, P:2 * P], ACT.Copy).then_inc(pT_sb.sem, 1)
                    for u in range(U):
                        act.wait_ge(x1nT_ps.sem, x1nT_ps.at(it, u + 1))
                        a.activation(x1nT[:, u], ps[:, u, 0, 2 * P:4 * P], ACT.Copy).then_inc(x1nT_sb.sem, 1)
                    act.wait_ge(ez_ready.sem, ez_ready.at(it, 1))
                    a.activation(ex[:], ez[:], ACT.Exp).then_inc(ex_ready.sem, 1)
                    for n, bank in enumerate((1, 2, 0, 1)):
                        for u in range(U):
                            act.wait_ge(proj_ps.sem, proj_ps.at(it, n * U + u + 1))
                            a.activation(tanh[:, u, n], ps[:, u, bank], ACT.Tanh, scale=0.5).then_inc(tanh_ready.sem, 1)
                    act.wait_ge(out.sem, out.at(it, 0))
                    act.wait_ge(rows_ps.sem, rows_ps.at(it, U))
                    a.activation(pP[:], ps_perm[:], ACT.Copy).then_inc(P_sb.sem, 1)
                    for n in range(7):
                        for u in range(U):
                            act.wait_ge(perm_ps.sem, perm_ps.at(it, n * U + u + 1))
                            if n < 2:
                                dst = vp[:, u, n]
                            elif n == 6:
                                dst = krow[:, u]
                            else:
                                which, half = (0, n - 2) if n < 4 else (1, n - 4)
                                dst = kqT[:, u, which, 2 * half:2 * half + 2]
                            a.activation(dst, ps[:, u, n % 3], ACT.Copy).then_inc(perm_sb.sem, 1)
                    for u in range(U):
                        act.wait_ge(compact_ps.sem, compact_ps.at(it, u + 1))
                        a.activation(edge_e[:, u], sm_edge[:, u], ACT.Exp)
                        a.activation(decay[:, u], ps[:, u, 2], ACT.Exp).then_inc(decay_ready.sem, 1)

            @block.gpsimd
            def _(pool):
                g = nc.gpsimd

                def deviations(it, n):
                    pool.wait_ge(var_ready.sem, var_ready.at(it, n + 1))
                    g.tensor_tensor(rstd[:], var[:], c["minus_half"][:, 0:U], ALU.pow).then_inc(rstd_ready.sem, 1)

                def turn(it, following):
                    chain = Chain(pool_step, pool, it)
                    deviations(it, 1)
                    for u in range(U):
                        pool.wait_ge(proj_sb.sem, proj_sb.at(it, U + u + 1))
                        y = qk[:, u].rearrange("p a (h d) -> p (a h) d", d=DK)
                        g.tensor_tensor(qk_sq[:, u], y, y, ALU.mult).then_inc(sq_ready.sem, 1)
                    pool.wait_ge(ss_ready.sem, ss_ready.at(it, 1))
                    chain.done(g.tensor_tensor(rnorm[:].rearrange("p u h -> p (u h)"), ss[:].rearrange("p u h -> p (u h)"),
                                               c["minus_half"][:, 0:U * 2 * H], ALU.pow))
                    for u in range(U):
                        y = qk[:, u].rearrange("p a (h d) -> p (a h) d", d=DK)
                        g.tensor_tensor(y, y, rnorm[:, u].unsqueeze(2).to_broadcast([P, 2 * H, DK]),
                                        ALU.mult).then_inc(qk_ready.sem, 1)
                    pool.wait_ge(out.sem, out.at(it, 0))
                    for u in range(U):
                        pool.wait_ge(proj_sb.sem, proj_sb.at(it, 3 * U + u + 1))
                        g.tensor_tensor(gate[:, u].rearrange("p (h d) -> p h d", d=DK), gg[:, u].rearrange("p (h d) -> p h d", d=DK),
                                        c["norm_w"][:].unsqueeze(1).to_broadcast([P, H, DK]), ALU.mult).then_inc(gate_ready.sem, 1)
                    pool.wait_ge(rowv_ready.sem, rowv_ready.at(it, 1))
                    for u in range(U):
                        for t in range(2):
                            last = g.tensor_tensor(gdecay[:, u, t], c["upto_block"][:].unsqueeze(1).to_broadcast([P, H, BK]),
                                                   rowg[:, u, t].unsqueeze(2).to_broadcast([P, H, BK]), ALU.mult)
                        last.then_inc(gdecay_ready.sem, 1)
                    chain.close()
                    if following is not None:
                        deviations(following, 0)

                deviations(0, 0)
                with pool.Fori(0, TURNS - 1) as it:
                    turn(it, it + 1)
                turn(TURNS - 1, None)

            @block.vector
            def _(dve):
                v = nc.vector
                dve.wait_ge(w_in, 16 * 9)
                v.tensor_scalar(att_b[:, 0], c["ones"][:], att[:, 0:1], None, ALU.mult)
                v.memset(scores[:], -1.0)
                v.memset(from_e[:], 0.0)
                v.memset(sel_bf[:], 0.0)
                v.tensor_scalar(att_b[:, 1], c["ones"][:], att[:, 1:2], None, ALU.mult).then_inc(att_ready, 1)
                dve.wait_ge(att_ready, 1)
                def layernorm(src, it, n):
                    steps = Chain((ln_first, ln_second)[n], dve, it)
                    for u in range(U):
                        if n == 0:
                            dve.wait_ge(x_in.sem, x_in.at(it, U))
                        steps.done(v.bn_stats(stats[:, u], src[:, u]))
                        carry(nc, c)
                        steps.done(v.bn_aggr(mv[:, u], stats[:, u]))
                    v.tensor_scalar(var[:], mv[:, :, 1], LN_EPS, None, ALU.add).then_inc(var_ready.sem, 1)
                    dve.wait_ge(rstd_ready.sem, rstd_ready.at(it, n + 1))
                    if n == 0:
                        dve.wait_ge(x1nT_ps.sem, x1nT_ps.at(it, 0))
                    for u in range(U):
                        v.tensor_scalar(xn[:, u], src[:, u], mv[:, u, 0:1], rstd[:, u:u + 1],
                                        ALU.subtract, ALU.mult).then_inc(xn_ready.sem, 1)
                    steps.close()

                def turn(it, following):
                    chain = Chain(dve_step, dve, it)

                    def project(first, last):
                        for n in range(first, last):
                            for u in range(U):
                                dve.wait_ge(tanh_ready.sem, tanh_ready.at(it, n * U + u + 1))
                                dst = (qk[:, u, 0], qk[:, u, 1], vv[:, u], gg[:, u])[n]
                                v.scalar_tensor_tensor(dst, tanh[:, u, n], 1.0, ps[:, u, (1, 2, 0, 1)[n]], ALU.add,
                                                       ALU.mult).then_inc(proj_sb.sem, 1)


                    for u in range(U):
                        dve.wait_ge(e_ps.sem, e_ps.at(it, u + 1))
                        chain.done(v.tensor_scalar(e_low[:, u], ps[:, u, 2, 0:P], 0.2, None, ALU.mult))
                        chain.done(v.tensor_tensor(e_act[:, u], e_low[:, u], ps[:, u, 2, 0:P], ALU.max))
                        chain.done(v.tensor_tensor(e_masked[:, u], e_act[:, u], c["adj_neg"][:], ALU.add))
                        chain.done(v.tensor_reduce(e_max[:, u:u + 1], e_masked[:, u], AX.X, ALU.max))
                        v.tensor_scalar(e_neg_max[:, u:u + 1], e_max[:, u:u + 1], -1.0, None, ALU.mult).then_inc(e_ready.sem, 1)
                    dve.wait_ge(x1_out.sem, x1_out.at(it, 0))
                    for u in range(U):
                        dve.wait_ge(o_ps.sem, o_ps.at(it, u + 1))
                        chain.done(v.reciprocal(p_rec[:, u:u + 1], p_sum[:, u:u + 1]))
                        v.scalar_tensor_tensor(x1[:, u, 0:F1], ps[:, u, 2, 2 * P:3 * P], p_rec[:, u:u + 1], x[:, u, 0:F1],
                                               ALU.mult, ALU.add)
                        v.tensor_tensor(x1[:, u, F1:D], hh[:, u, 0], x[:, u, F1:D], ALU.add).then_inc(x1_ready.sem, 1)
                        dve.wait_ge(x1_ready.sem, x1_ready.at(it, u + 1))
                    layernorm(x1, it, 1)
                    dve.wait_ge(small_ps.sem, small_ps.at(it, U))
                    v.tensor_reduce(lmax[:], sm_proj[:, :, 0:E0], AX.X, ALU.max)
                    v.tensor_scalar(ez[:, :, E0:E0 + H], sm_proj[:, :, E0:E0 + H], -1.0, None, ALU.mult)
                    chain.done(v.tensor_tensor(zz[:], sm_proj[:, :, E0 + H:SMALL],
                                               c["dt_bias"][:].unsqueeze(1).to_broadcast([P, U, H]), ALU.add))
                    v.tensor_tensor(ez[:, :, 0:E0], sm_proj[:, :, 0:E0], lmax[:].unsqueeze(2).to_broadcast([P, U, E0]),
                                    ALU.subtract)
                    v.scalar_tensor_tensor(ez[:, :, E0 + H:SMALL], zz[:], -1.0, zz[:], ALU.mult, ALU.min).then_inc(ez_ready.sem, 1)
                    dve.wait_ge(ex_ready.sem, ex_ready.at(it, 1))
                    v.tensor_scalar(den[:, :, 0:H], ex[:, :, E0:E0 + H], 1.0, None, ALU.add)
                    v.tensor_scalar(den[:, :, H:2 * H], ex[:, :, E0 + H:SMALL], 2.0, None, ALU.add)
                    chain.done(v.tensor_reduce(den[:, :, 2 * H:2 * H + 1], ex[:, :, 0:E0], AX.X, ALU.add))
                    chain.done(v.reciprocal(rec[:], den[:]))
                    v.tensor_tensor(scores[:, :, 0:E0], ex[:, :, 0:E0], rec[:, :, 2 * H:2 * H + 1].to_broadcast([P, U, E0]), ALU.mult)
                    chain.done(v.tensor_tensor(s1[:], ex[:, :, E0 + H:SMALL], rec[:, :, H:2 * H], ALU.mult))
                    chain.done(v.tensor_tensor(s2[:], s1[:], s1[:], ALU.mult))
                    chain.done(v.tensor_scalar(poly[:], s2[:], 2.0 / 17.0, None, ALU.mult))
                    for m in range(7, 0, -1):
                        chain.done(v.scalar_tensor_tensor(poly[:], poly[:], 2.0 / (2 * m + 1), s2[:], ALU.add, ALU.mult))
                    chain.done(v.scalar_tensor_tensor(poly[:], poly[:], 2.0, s1[:], ALU.add, ALU.mult))
                    chain.done(v.scalar_tensor_tensor(poly[:], zz[:], 0.0, poly[:], ALU.max, ALU.add))
                    chain.done(v.tensor_tensor(poly[:], poly[:], c["neg_a"][:].unsqueeze(1).to_broadcast([P, U, H]), ALU.mult))
                    v.tensor_scalar(tokv[:, :, 2 * E0 + H:ROWV], poly[:], -1000.0, None, ALU.max)
                    v.tensor_copy(tokv[:, :, 2 * E0:2 * E0 + H], rec[:, :, 0:H])
                    for u in range(U):
                        carry(nc, c)
                        chain.done(v.max(top[:, u], scores[:, u]))
                        carry(nc, c)
                        chain.done(v.max_index(top_i[:, u], top[:, u], scores[:, u]))
                    chain.done(v.tensor_copy(top_f[:], top_i[:]))
                    for u in range(U):
                        chain.done(v.tensor_scalar(sel[:, u], c["row0"][:, 0:E0], top_f[:, u, 0:1], None, ALU.is_equal))
                        chain.done(v.scalar_tensor_tensor(sel[:, u], c["row0"][:, 0:E0], top_f[:, u, 1:2], sel[:, u],
                                                          ALU.is_equal, ALU.add))
                    v.tensor_copy(sel_bf[:, :, 0], sel[:])
                    v.tensor_copy(sel_bf[:, :, 1, 1:2], sel[:, :, 0:1])
                    chain.done(v.tensor_tensor(sel_bf[:, :, 1, 2:3], sel[:, :, 0:1], sel[:, :, 1:2], ALU.add))
                    v.tensor_tensor(sel_bf[:, :, 1, 3:4], sel_bf[:, :, 1, 2:3], sel[:, :, 2:3], ALU.add).then_inc(sel_ready.sem, 1)
                    chain.done(v.tensor_tensor(wun[:], scores[:, :, 0:E0], sel[:], ALU.mult))
                    chain.done(v.tensor_tensor(wsum[:].unsqueeze(2), top[:, :, 0:1], top[:, :, 1:2], ALU.add))
                    chain.done(v.reciprocal(wrec[:], wsum[:]))
                    chain.done(v.tensor_tensor(wun[:], wun[:], wrec[:].unsqueeze(2).to_broadcast([P, U, E0]), ALU.mult))
                    v.tensor_scalar(tokv[:, :, 0:E0], wun[:], 0.5 * DK ** -0.5, None, ALU.mult)
                    chain.done(v.tensor_scalar(tokv[:, :, E0:2 * E0], wun[:], 0.0, None, ALU.is_gt))
                    project(0, 2)
                    dve.wait_ge(place_ps.sem, place_ps.at(it, 1))
                    chain.done(v.tensor_copy(place[:], sm_place))
                    chain.done(v.scalar_tensor_tensor(place1[:], place[:, :, 0], 1.0, sel[:], ALU.add, ALU.mult))
                    for u in range(U):
                        chain.done(v.tensor_scalar(pT[:, u], c["row1"][:], place1[:, u, 0:1], None, ALU.is_equal))
                        for e in range(1, E0):
                            last = v.scalar_tensor_tensor(pT[:, u], c["row1"][:], place1[:, u, e:e + 1], pT[:, u],
                                                          ALU.is_equal, ALU.add)
                            if e < E0 - 1:
                                chain.done(last)
                        last.then_inc(perm_ready.sem, 1)
                    project(2, 4)
                    for u in range(U):
                        dve.wait_ge(sq_ready.sem, sq_ready.at(it, u + 1))
                        chain.done(v.tensor_reduce(ss[:, u], qk_sq[:, u], AX.X, ALU.add))
                    v.tensor_scalar(ss[:], ss[:], 4e-6, None, ALU.add).then_inc(ss_ready.sem, 1)
                    for u in range(U):
                        for t in range(2):
                            v.tensor_scalar(from_e[:, u, t, 0:E0], place[:, u, 1], c["rowid"][:, t:t + 1], None, ALU.is_le)
                        chain.done(v.tensor_scalar(eid[:, u], c["row0"][:], place[:, u, 1, 1:2], None, ALU.is_ge))
                        for e in range(2, E0):
                            chain.done(v.scalar_tensor_tensor(eid[:, u], c["row0"][:], place[:, u, 1, e:e + 1], eid[:, u],
                                                              ALU.is_ge, ALU.add))
                    chain.done(v.tensor_reduce(eid_row[:].rearrange("p u t -> p (u t)"),
                                               from_e[:, :, :, 1:E0].rearrange("p u t e -> p (u t) e"), AX.X, ALU.add))
                    dve.wait_ge(out.sem, out.at(it, 0))
                    for u in range(U):
                        for t in range(2):
                            last = v.scalar_tensor_tensor(mask[:, u, t], eid[:, u, P * t:P * t + P], eid_row[:, u, t:t + 1],
                                                          c["causal"][:], ALU.is_equal, ALU.add)
                        last.then_inc(mask_ready.sem, 1)
                        v.tensor_scalar(straddle[:, u], eid_row[:, u], eid[:, u, P - 1:P], None, ALU.is_equal)
                    for u in range(U):
                        dve.wait_ge(mask_ready.sem, mask_ready.at(it, u + 1))
                        for k in range(NB_):
                            rows = slice(BK * k, BK * k + BK)
                            last = v.tensor_copy(mask_c[rows, u], mask[rows, u, :, rows])
                        last.then_inc(mask_c_ready.sem, 1)
                    dve.wait_ge(rows_ps.sem, rows_ps.at(it, U))
                    v.tensor_copy(rv[:], sm_row)
                    chain.done(v.tensor_tensor(onehot[:], from_e[:, :, :, 0:E0], from_e[:, :, :, 1:E0 + 1], ALU.subtract))
                    for a in range(2):
                        last = v.tensor_tensor(picked[:, :, :, a], rv[:, :, :, E0 * a:E0 * a + E0], onehot[:], ALU.mult)
                    chain.done(last)
                    chain.done(v.tensor_reduce(w_act[:].rearrange("p u t a -> p (u t a)"),
                                               picked[:].rearrange("p u t a e -> p (u t a) e"), AX.X, ALU.add))
                    v.tensor_copy(roww[:], w_act[:, :, :, 0])
                    active = w_act[:, :, :, 1:2].to_broadcast([P, U, 2, H])
                    v.tensor_tensor(rowb[:], rv[:, :, :, 2 * E0:2 * E0 + H], active, ALU.mult)
                    v.tensor_tensor(rowg[:], rv[:, :, :, 2 * E0 + H:ROWV], active, ALU.mult).then_inc(rowv_ready.sem, 1)
                    if following is not None:
                        layernorm(x, following, 0)
                    for u in range(U):
                        dve.wait_ge(decay_ready.sem, decay_ready.at(it, u + 1))
                        v.tensor_tensor(edge[:, u], edge_e[:, u], straddle[:, u].unsqueeze(2).to_broadcast([P, 2, H]), ALU.mult)
                        for odd in range(2):
                            last = v.tensor_tensor(acomp[:, u, :, odd:H:2], ps[:, u, odd, 0:256].rearrange("p (t h i) -> p t h i", t=2, h=4),
                                                   decay[:, u, :, odd:H:2], ALU.mult)
                        last.then_inc(acomp_ready.sem, 1)
                    chain.close()

                layernorm(x, 0, 0)
                with dve.Fori(0, TURNS - 1) as it:
                    turn(it, it + 1)
                turn(TURNS - 1, None)


def phase_invert(nc, c, dram, NB):
    GROUP = P // (2 * H)
    TURNS = NB // GROUP
    SY = 2 * H
    ctx = ExitStack()
    counts = []

    def sb(name, shape, dt=F32):
        return ctx.enter_context(nc.sbuf_tensor(name, shape, dt))

    def count(name, per, unit=1, again=False):
        counts.append(Count(ctx, nc, "b_" + name, per, unit, again))
        return counts[-1]

    with ctx:
        a_in = sb("b_a_in", [P, GROUP, SY, BK])
        beta_in = sb("b_beta_in", [P, GROUP, SY])
        betaT = sb("b_betaT", [P, P])
        a_sys = sb("b_a_sys", [P, BK, NB_, BK])
        x_sys = sb("b_x_sys", [P, BK, NB_, BK])
        eyes = sb("b_eyes", [P, BK, NB_, BK])
        prod_d = sb("b_prod_d", [P, BK * NB_ * BK // 4])
        prod_p = sb("b_prod_p", [P, BK * BK // 4 + BK])
        inv = sb("b_inv", [P, P, BK])
        ps = ctx.enter_context(nc.psum_tensor("b_ps", [P, 4, 4, P], F32))
        ps_beta = ctx.enter_context(nc.psum_tensor("b_ps_beta", [P, P], F32))
        ps_back = ctx.enter_context(nc.psum_tensor("b_ps_back", [P, 3, 4, P], F32))

        zeroed = ctx.enter_context(nc.semaphore("b_zeroed"))
        loaded = count("loaded", 2, 16)
        beta_ps = count("beta_ps", 1)
        beta_sb = count("beta_sb", 1, again=True)
        sys_ps = count("sys_ps", 8, again=True)
        sys_sb = count("sys_sb", 8, again=True)
        eye = count("eye", 1)
        solved = count("solved", 1)
        pool_step = count("pool_step", 2 * (BK - 1))
        dve_step = count("dve_step", 2 * (BK - 1))
        scaled = count("scaled", 1, again=True)
        back_ps = count("back_ps", 8, again=True)
        back_sb = count("back_sb", 8, again=True)
        stored = count("stored", 1, 16, again=True)

        def update(engine, lo, hi, prod, chain, last_sem):
            for s in range(BK - 1):
                rows, cols = BK - 1 - s, s + 1
                p = prod[:, 0:rows * (hi - lo) * cols].rearrange("p (r k c) -> p r k c", r=rows, k=hi - lo)
                factor = a_sys[:, s + 1:BK, lo:hi, s:s + 1].to_broadcast([P, rows, hi - lo, cols])
                row = x_sys[:, s:s + 1, lo:hi, 0:cols].to_broadcast([P, rows, hi - lo, cols])
                below = x_sys[:, s + 1:BK, lo:hi, 0:cols]
                chain.done(engine.tensor_tensor(p, factor, row, ALU.mult))
                last = engine.tensor_tensor(below, below, p, ALU.subtract)
                chain.done(last)
            chain.close()

        with nc.Block() as block:
            @block.sync
            def _(sp):
                start_at_one(sp, counts)
                with sp.Fori(0, TURNS) as it:
                    sp.wait_ge(sys_ps.sem, sys_ps.at(it, 0))
                    hold(sp)
                    sp.dma_start(a_in[:], dram["acomp"][bass.ds(it * GROUP, GROUP)].rearrange("b p t h i -> p b (t h) i")).then_inc(loaded.sem, 16)
                    sp.dma_start(beta_in[:], dram["rowb"][bass.ds(it * GROUP, GROUP)].rearrange("b p t h -> p b (t h)"),
                                 allow_slow_non_contiguous=True).then_inc(loaded.sem, 16)
                    sp.wait_ge(back_sb.sem, back_sb.at(it, 8))
                    hold(sp)
                    sp.dma_start(dram["inv"][bass.ds(it * GROUP, GROUP)].rearrange("b p t h i -> p b (t h i)"),
                                 inv[:].rearrange("p (b s) i -> p b (s i)", b=GROUP)).then_inc(stored.sem, 16)
                sp.wait_ge(stored.sem, stored.at(TURNS, 0))

            @block.tensor
            def _(pe):
                tr = nc.tensor.transpose
                a_flat = a_in[:].rearrange("p b s i -> p (b s) i")
                with pe.Fori(0, TURNS) as it:
                    pe.wait_ge(loaded.sem, loaded.at(it, 2))
                    pe.wait_ge(beta_sb.sem, beta_sb.at(it, 0))
                    tr(ps_beta[:], beta_in[:].rearrange("p b s -> p (b s)"), c["ident"][:]).then_inc(beta_ps.sem, 1)
                    for n in range(8):
                        if n >= 4:
                            pe.wait_ge(sys_sb.sem, sys_sb.at(it, n - 3))
                        else:
                            pe.wait_ge(sys_sb.sem, sys_sb.at(it, 0))
                        for q in range(4):
                            last = tr(ps[:, n % 4, q], a_flat[:, :, 4 * n + q], c["ident"][:])
                        last.then_inc(sys_ps.sem, 1)
                    pe.wait_ge(scaled.sem, scaled.at(it, 1))
                    for n in range(8):
                        if n >= 3:
                            pe.wait_ge(back_sb.sem, back_sb.at(it, n - 2))
                        else:
                            pe.wait_ge(back_sb.sem, back_sb.at(it, 0))
                        for q in range(4):
                            last = tr(ps_back[:, n % 3, q], x_sys[:, 4 * n + q].rearrange("p k c -> p (k c)"), c["ident"][:])
                        last.then_inc(back_ps.sem, 1)

            @block.scalar
            def _(act):
                with act.Fori(0, TURNS) as it:
                    act.wait_ge(beta_ps.sem, beta_ps.at(it, 1))
                    act.wait_ge(scaled.sem, scaled.at(it, 0))
                    nc.scalar.activation(betaT[:], ps_beta[:], ACT.Copy).then_inc(beta_sb.sem, 1)
                    act.wait_ge(stored.sem, stored.at(it, 0))
                    for n in range(8):
                        act.wait_ge(back_ps.sem, back_ps.at(it, n + 1))
                        nc.scalar.activation(inv[:].rearrange("p s i -> p i s")[:, 4 * n:4 * n + 4], ps_back[:, n % 3],
                                             ACT.Copy).then_inc(back_sb.sem, 1)

            @block.gpsimd
            def _(pool):
                g = nc.gpsimd
                g.memset(eyes[:], 0.0).then_inc(zeroed, 1)
                pool.wait_ge(zeroed, 1)
                g.affine_select(out=eyes[:], in_=eyes[:], pattern=[[1, BK], [0, NB_], [-1, BK]],
                                compare_op=ALU.not_equal, fill=1.0, base=0, channel_multiplier=0).then_inc(zeroed, 1)
                pool.wait_ge(zeroed, 2)
                with pool.Fori(0, TURNS) as it:
                    pool.wait_ge(back_ps.sem, back_ps.at(it, 0))
                    g.tensor_tensor(x_sys[:], eyes[:], eyes[:], ALU.mult).then_inc(eye.sem, 1)
                    pool.wait_ge(eye.sem, eye.at(it, 1))
                    pool.wait_ge(sys_sb.sem, sys_sb.at(it, 8))
                    update(g, NB_ - 1, NB_, prod_p, Chain(pool_step, pool, it), None)
                    pool.wait_ge(dve_step.sem, dve_step.at(it, dve_step.per))
                    g.tensor_tensor(x_sys[:], x_sys[:], betaT[:].rearrange("p (k r) -> p r k", k=NB_).unsqueeze(3).to_broadcast([P, BK, NB_, BK]),
                                    ALU.mult).then_inc(scaled.sem, 1)

            @block.vector
            def _(dve):
                v = nc.vector
                with dve.Fori(0, TURNS) as it:
                    dve.wait_ge(beta_sb.sem, beta_sb.at(it, 1))
                    dve.wait_ge(scaled.sem, scaled.at(it, 0))
                    for n in range(8):
                        dve.wait_ge(sys_ps.sem, sys_ps.at(it, n + 1))
                        v.tensor_tensor(a_sys[:, 4 * n:4 * n + 4].rearrange("p i k c -> p i (k c)"), ps[:, n % 4],
                                        betaT[:].unsqueeze(1).to_broadcast([P, 4, P]), ALU.mult).then_inc(sys_sb.sem, 1)
                    dve.wait_ge(eye.sem, eye.at(it, 1))
                    dve.wait_ge(sys_sb.sem, sys_sb.at(it, 8))
                    update(v, 0, NB_ - 1, prod_d, Chain(dve_step, dve, it), None)


def phase_mix(nc, c, dram, NB):
    TURNS = NB // U
    ctx = ExitStack()
    counts = []

    def sb(name, shape, dt=F32):
        return ctx.enter_context(nc.sbuf_tensor(name, shape, dt))

    def count(name, per, unit=1, again=False):
        counts.append(Count(ctx, nc, "c_" + name, per, unit, again))
        return counts[-1]

    DECAYS = [(t, half) for t in range(2) for half in range(2)]
    PRODUCTS = [(t, (h, h + 2)) for t in range(2) for h in (0, 1, 4, 5)]
    ND, NP = len(DECAYS), len(PRODUCTS)

    with ctx:
        wo = sb("c_wo", [P, 4, D])
        kqT = sb("c_kqT", [P, U, 2, 4, R])
        vp = sb("c_vp", [P, U, 2, HD])
        mask = sb("c_mask", [P, U, 2, P], BF16)
        krow = sb("c_krow", [P, U, HD])
        edge = sb("c_edge", [P, U, 2, H])
        krow_edge = sb("c_krow_edge", [P, U, HD])
        edge_w = sb("c_edge_w", [P, U, H])
        state = sb("c_state", [P, U, 4, DK])
        from0 = sb("c_from0", [P, U, HD])
        o_from0 = sb("c_o_from0", [P, U, HD])
        perm = sb("c_perm", [P, U, 2, P])
        inv = sb("c_inv", [P, U, 2, H, BK])
        rowg = sb("c_rowg", [P, U, 2, H])
        roww = sb("c_roww", [P, U, 2])
        gate = sb("c_gate", [P, U, HD])
        x1 = sb("c_x1", [P, U, D])
        gsum = sb("c_gsum", [P, U, 2, H, P])
        decay = sb("c_decay", [P, U, 2, H, P])
        mix = sb("c_mix", [P, U, 2, H, 2, P])
        rest = sb("c_rest", [P, U, HD])
        base1 = sb("c_base1", [P, U, HD])
        uu = sb("c_uu", [P, U, 2, HD])
        oo = sb("c_oo", [P, U, 2, HD])
        core_sq = sb("c_core_sq", [P, U, HD])
        ms = sb("c_ms", [P, U, H])
        rms = sb("c_rms", [P, U, H])
        y = sb("c_y", [P, U, HD])
        yT = sb("c_yT", [P, U, 4, P])
        x2 = sb("c_x2", [P, U, D])
        ps = ctx.enter_context(nc.psum_tensor("c_ps", [P, U, 4, 512], F32))

        w_in = ctx.enter_context(nc.semaphore("c_w_in"))
        g_in = count("g_in", 2 * U, 16)
        kq_in = count("kq_in", U, 16)
        v_in = count("v_in", 5 * U, 16)
        tail_in = count("tail_in", 3 * U, 16)
        gsum_ready = count("gsum_ready", U)
        decay_ps = count("decay_ps", ND * U, again=True)
        decay_sb = count("decay_sb", ND * U)
        prod_ps = count("prod_ps", NP * U)
        mix_ready = count("mix_ready", NP * U, again=True)
        solve_ps = count("solve_ps", 2 * NB_ * U)
        uu_ready = count("uu_ready", 2 * NB_ * U)
        rest_ps = count("rest_ps", 2 * (NB_ - 1) * U)
        rest_ready = count("rest_ready", 2 * (NB_ - 1) * U)
        krow_ready = count("krow_ready", U)
        state_ps = count("state_ps", U, again=True)
        state_ready = count("state_ready", U)
        cross_ps = count("cross_ps", U)
        ocross_ps = count("ocross_ps", U, again=True)
        ocross_sb = count("ocross_sb", U)
        base1_ready = count("base1_ready", U)
        o_ps = count("o_ps", 2 * U)
        oo0_ready = count("oo0_ready", U)
        oo_ready = count("oo_ready", U)
        core_ps = count("core_ps", U, again=True)
        sq_ready = count("sq_ready", U)
        ms_ready = count("ms_ready", 1)
        rms_ready = count("rms_ready", 1)
        y_ready = count("y_ready", U)
        yT_ps = count("yT_ps", U)
        yT_ready = count("yT_ready", U)
        out_ps = count("out_ps", U)
        x2_ready = count("x2_ready", U, again=True)
        stored = count("stored", U, 16, again=True)
        dve_step = count("dve_step", C_DVE_STEPS)

        def head_cols(h):
            return slice(DK * h, DK * h + DK)

        def key_part(h):
            return slice(DK * (h % 2), DK * (h % 2) + DK)

        def by_head(ap):
            return ap.rearrange("p (h d) -> p h d", d=DK)

        with nc.Block() as block:
            @block.sync
            def _(sp):
                start_at_one(sp, counts)
                sp.dma_start(wo[:], dram["L0_ffn_Wo"].rearrange("(k p) f -> p k f", p=P)).then_inc(w_in, 16)

                def load_decays(it):
                    for u in range(U):
                        b = it * U + u
                        sp.wait_ge(decay_ps.sem, decay_ps.at(it, 0))
                        hold(sp)
                        sp.dma_start(rowg[:, u], dram["rowg"][b]).then_inc(g_in.sem, 16)
                        sp.dma_start(mask[:, u], dram["mask"][b]).then_inc(g_in.sem, 16)

                def load_keys(it):
                    for u in range(U):
                        b = it * U + u
                        sp.wait_ge(ocross_ps.sem, ocross_ps.at(it, 0))
                        hold(sp)
                        sp.dma_start(kqT[:, u], dram["kqT"][b]).then_inc(kq_in.sem, 16)

                def load_values(it):
                    for u in range(U):
                        b = it * U + u
                        sp.wait_ge(core_ps.sem, core_ps.at(it, 0))
                        hold(sp)
                        sp.dma_start(vp[:, u], dram["vp"][b]).then_inc(v_in.sem, 16)
                        sp.dma_start(inv[:, u], dram["inv"][b]).then_inc(v_in.sem, 16)
                        sp.dma_start(roww[:, u], dram["roww"][b]).then_inc(v_in.sem, 16)
                        sp.dma_start(krow[:, u], dram["krow"][b]).then_inc(v_in.sem, 16)
                        sp.dma_start(edge[:, u], dram["edge"][b]).then_inc(v_in.sem, 16)

                def load_tail(it):
                    for u in range(U):
                        b = it * U + u
                        sp.wait_ge(x2_ready.sem, x2_ready.at(it, 0))
                        hold(sp)
                        sp.dma_start(perm[:, u], dram["perm"][b]).then_inc(tail_in.sem, 16)
                        sp.dma_start(gate[:, u], dram["gate"][b]).then_inc(tail_in.sem, 16)
                        sp.dma_start(x1[:, u], dram["x1"][b]).then_inc(tail_in.sem, 16)

                def turn(it, following):
                    if following is not None:
                        load_decays(following)
                        load_keys(following)
                        load_values(following)
                    for u in range(U):
                        b = it * U + u
                        sp.wait_ge(x2_ready.sem, x2_ready.at(it, u + 1))
                        hold(sp)
                        sp.dma_start(dram["x2"][b], x2[:, u]).then_inc(stored.sem, 16)
                    if following is not None:
                        load_tail(following)

                load_decays(0)
                load_keys(0)
                load_values(0)
                load_tail(0)
                with sp.Fori(0, TURNS - 1) as it:
                    turn(it, it + 1)
                turn(TURNS - 1, None)
                sp.wait_ge(stored.sem, stored.at(TURNS, 0))

            @block.tensor
            def _(pe):
                mm, tr = nc.tensor.matmul, nc.tensor.transpose

                def carrier(u, bank=1):
                    mm(ps[:, u, bank, 0:1], c["ones_bf"][:], c["ones_bf"][:, 0:1], start=True, stop=True)

                def decays(it, first, last):
                    for n in range(first, last):
                        t, half = DECAYS[n]
                        for u in range(U):
                            if n == 0:
                                pe.wait_ge(g_in.sem, g_in.at(it, 2 * U))
                                pe.wait_ge(gsum_ready.sem, gsum_ready.at(it, u + 1))
                            if n >= 2:
                                pe.wait_ge(decay_sb.sem, decay_sb.at(it, (n - 2) * U + u + 1))
                            dst = ps[:, u, n % 2].rearrange("p (h i) -> p h i", h=4)
                            mm(dst, c["after"][:], gsum[:, u, t, 4 * half:4 * half + 4], start=True, stop=False)
                            mm(dst, c["big_ident"][:], mask[:, u, t].unsqueeze(1).to_broadcast([P, 4, P]),
                               start=False, stop=True).then_inc(decay_ps.sem, 1)

                def turn(it, following):
                    pe.wait_ge(kq_in.sem, kq_in.at(it, U))
                    for n, (t, heads) in enumerate(PRODUCTS):
                        for u in range(U):
                            if n < 2:
                                pe.wait_ge(decay_sb.sem, decay_sb.at(it, (2 + n) * U + u + 1))
                            elif n < 4:
                                pe.wait_ge(x2_ready.sem, x2_ready.at(it, 0))
                            else:
                                pe.wait_ge(mix_ready.sem, mix_ready.at(it, (n - 4) * U + u + 1))
                            for m, h in enumerate(heads):
                                dst = ps[:, u, n % 4, 2 * P * m:2 * P * m + 2 * P].rearrange("p (a i) -> p a i", a=2)
                                last = mm(dst, kqT[key_part(h), u, 0, h // 2, P * t:P * t + P],
                                          kqT[key_part(h), u, :, h // 2, P * t:P * t + P], start=True, stop=True)
                            last.then_inc(prod_ps.sem, 1)
                    pe.wait_ge(mix_ready.sem, mix_ready.at(it, NP * U))
                    pe.wait_ge(v_in.sem, v_in.at(it, 5 * U))
                    for t in range(2):
                        if t == 1:
                            for u in range(U):
                                pe.wait_ge(krow_ready.sem, krow_ready.at(it, u + 1))
                                pe.wait_ge(uu_ready.sem, uu_ready.at(it, (NB_ - 1) * U + u + 1))
                                carrier(u)
                                for h in range(H):
                                    last = mm(ps[key_part(h), u, 2, head_cols(h // 2)], krow_edge[:, u, head_cols(h)],
                                              uu[:, u, 0, head_cols(h)], start=True, stop=True)
                                last.then_inc(state_ps.sem, 1)
                            for u in range(U):
                                pe.wait_ge(state_ready.sem, state_ready.at(it, u + 1))
                                for h in range(H):
                                    last = mm(ps[:, u, 2 + h % 2, head_cols(h // 2)], kqT[key_part(h), u, 0, h // 2, P:R],
                                              state[key_part(h), u, h // 2], start=True, stop=True)
                                last.then_inc(cross_ps.sem, 1)
                            for u in range(U):
                                for h in range(H):
                                    last = mm(ps[:, u, h % 2, head_cols(h // 2)], kqT[key_part(h), u, 1, h // 2, P:R],
                                              state[key_part(h), u, h // 2], start=True, stop=True)
                                last.then_inc(ocross_ps.sem, 1)
                        for k in range(NB_):
                            rows = slice(BK * k, BK * k + BK)
                            if k:
                                for u in range(U):
                                    pe.wait_ge(uu_ready.sem, uu_ready.at(it, (t * NB_ + k - 1) * U + u + 1))
                                    if k < 3:
                                        by_wait(u, t, it)
                                    for h in range(H):
                                        last = mm(ps[rows, u, 2, head_cols(h)], mix[0:BK * k, u, t, h, 0, rows],
                                                  uu[0:BK * k, u, t, head_cols(h)], start=True, stop=True)
                                    last.then_inc(rest_ps.sem, 1)
                            for u in range(U):
                                if k:
                                    pe.wait_ge(rest_ready.sem, rest_ready.at(it, (t * (NB_ - 1) + k - 1) * U + u + 1))
                                    pe.wait_ge(uu_ready.sem, uu_ready.at(it, (t * NB_ + k - 1) * U + u + 1))
                                elif t:
                                    pe.wait_ge(base1_ready.sem, base1_ready.at(it, u + 1))
                                by_wait(u, t, it)
                                src = rest[:, u] if k else (base1[:, u] if t else vp[:, u, 0])
                                for h in range(H):
                                    last = mm(ps[rows, u, 3, head_cols(h)], inv[rows, u, t, h],
                                              src[rows, head_cols(h)], start=True, stop=True)
                                last.then_inc(solve_ps.sem, 1)
                    for t in range(2):
                        for u in range(U):
                            pe.wait_ge(uu_ready.sem, uu_ready.at(it, (2 * NB_ - 1) * U + u + 1))
                            for h in range(H):
                                last = mm(ps[:, u, t, head_cols(h)], mix[:, u, t, h, 1], uu[:, u, t, head_cols(h)],
                                          start=True, stop=True)
                            last.then_inc(o_ps.sem, 1)
                    pe.wait_ge(tail_in.sem, tail_in.at(it, 3 * U))
                    for u in range(U):
                        pe.wait_ge(oo0_ready.sem, oo0_ready.at(it, u + 1))
                        pe.wait_ge(oo_ready.sem, oo_ready.at(it, u + 1))
                        for t in range(2):
                            last = mm(ps[:, u, 2], perm[:, u, t], oo[:, u, t], start=t == 0, stop=t == 1)
                        last.then_inc(core_ps.sem, 1)
                    if following is not None:
                        decays(following, 0, ND)
                    for u in range(U):
                        pe.wait_ge(y_ready.sem, y_ready.at(it, u + 1))
                        for k in range(4):
                            last = tr(ps[:, u, 3, P * k:P * k + P], y[:, u, P * k:P * k + P], c["ident"][:])
                        last.then_inc(yT_ps.sem, 1)
                    for u in range(U):
                        pe.wait_ge(yT_ready.sem, yT_ready.at(it, u + 1))
                        for k in range(4):
                            last = mm(ps[:, u, 2, 0:D], yT[:, u, k], wo[:, k], start=k == 0, stop=k == 3)
                        last.then_inc(out_ps.sem, 1)

                def by_wait(u, t, it):
                    if t:
                        pe.wait_ge(ocross_sb.sem, ocross_sb.at(it, u + 1))
                    carrier(u)

                pe.wait_ge(w_in, 16)
                decays(0, 0, ND)
                with pe.Fori(0, TURNS - 1) as it:
                    turn(it, it + 1)
                turn(TURNS - 1, None)

            @block.scalar
            def _(act):
                a = nc.scalar

                def decays(it):
                    for n, (t, half) in enumerate(DECAYS):
                        for u in range(U):
                            act.wait_ge(decay_ps.sem, decay_ps.at(it, n * U + u + 1))
                            if n == 0:
                                act.wait_ge(mix_ready.sem, mix_ready.at(it, 0))
                            a.activation(decay[:, u, t, 4 * half:4 * half + 4], ps[:, u, n % 2].rearrange("p (h i) -> p h i", h=4),
                                         ACT.Exp).then_inc(decay_sb.sem, 1)

                def turn(it, following):
                    for t in range(2):
                        if t == 1:
                            for u in range(U):
                                act.wait_ge(state_ps.sem, state_ps.at(it, u + 1))
                                a.activation(state[:, u], ps[:, u, 2, 0:4 * DK], ACT.Copy).then_inc(state_ready.sem, 1)
                        for k in range(NB_):
                            rows = slice(BK * k, BK * k + BK)
                            for u in range(U):
                                act.wait_ge(solve_ps.sem, solve_ps.at(it, (t * NB_ + k) * U + u + 1))
                                a.activation(uu[rows, u, t], ps[rows, u, 3], ACT.Copy).then_inc(uu_ready.sem, 1)
                    for u in range(U):
                        act.wait_ge(o_ps.sem, o_ps.at(it, u + 1))
                        a.activation(oo[:, u, 0], ps[:, u, 0], ACT.Copy, scale=roww[:, u, 0:1]).then_inc(oo0_ready.sem, 1)
                    for u in range(U):
                        act.wait_ge(core_ps.sem, core_ps.at(it, u + 1))
                        a.activation(core_sq[:, u], ps[:, u, 2], ACT.Square).then_inc(sq_ready.sem, 1)
                    if following is not None:
                        decays(following)
                    for u in range(U):
                        act.wait_ge(yT_ps.sem, yT_ps.at(it, u + 1))
                        a.activation(yT[:, u], ps[:, u, 3], ACT.Copy).then_inc(yT_ready.sem, 1)

                decays(0)
                with act.Fori(0, TURNS - 1) as it:
                    turn(it, it + 1)
                turn(TURNS - 1, None)

            @block.gpsimd
            def _(pool):
                g = nc.gpsimd

                def sums(it):
                    pool.wait_ge(g_in.sem, g_in.at(it, 2 * U))
                    pool.wait_ge(decay_ps.sem, decay_ps.at(it, 0))
                    for u in range(U):
                        for t in range(2):
                            last = g.tensor_tensor(gsum[:, u, t], c["upto"][:].unsqueeze(1).to_broadcast([P, H, P]),
                                                   rowg[:, u, t].unsqueeze(2).to_broadcast([P, H, P]), ALU.mult)
                        last.then_inc(gsum_ready.sem, 1)

                def turn(it, following):
                    pool.wait_ge(v_in.sem, v_in.at(it, 5 * U))
                    pool.wait_ge(state_ps.sem, state_ps.at(it, 0))
                    for u in range(U):
                        g.tensor_tensor(by_head(krow_edge[:, u]), by_head(krow[:, u]),
                                        edge[:, u, 0].unsqueeze(2).to_broadcast([P, H, DK]), ALU.mult).then_inc(krow_ready.sem, 1)
                    if following is not None:
                        sums(following)
                    pool.wait_ge(ms_ready.sem, ms_ready.at(it, 1))
                    g.tensor_tensor(rms[:].rearrange("p u h -> p (u h)"), ms[:].rearrange("p u h -> p (u h)"),
                                    c["minus_half"][:, 0:U * H], ALU.pow).then_inc(rms_ready.sem, 1)

                sums(0)
                with pool.Fori(0, TURNS - 1) as it:
                    turn(it, it + 1)
                turn(TURNS - 1, None)

            @block.vector
            def _(dve):
                v = nc.vector
                with dve.Fori(0, TURNS) as it:
                    chain = Chain(dve_step, dve, it)
                    dve.wait_ge(decay_sb.sem, decay_sb.at(it, ND * U))
                    for n, (t, heads) in enumerate(PRODUCTS):
                        for u in range(U):
                            dve.wait_ge(prod_ps.sem, prod_ps.at(it, n * U + u + 1))
                            pair = slice(heads[0], heads[1] + 1, 2)
                            v.tensor_tensor(mix[:, u, t, pair], ps[:, u, n % 4].rearrange("p (h a i) -> p h a i", h=2, a=2),
                                            decay[:, u, t, pair].unsqueeze(2).to_broadcast([P, 2, 2, P]), ALU.mult).then_inc(mix_ready.sem, 1)
                    dve.wait_ge(v_in.sem, v_in.at(it, 5 * U))
                    for u in range(U):
                        last = v.tensor_scalar(edge_w[:, u], edge[:, u, 1], roww[:, u, 1:2], None, ALU.mult)
                    chain.done(last)
                    for t in range(2):
                        if t == 1:
                            for u in range(U):
                                dve.wait_ge(cross_ps.sem, cross_ps.at(it, u + 1))
                                for odd in range(2):
                                    last = v.tensor_tensor(by_head(from0[:, u])[:, odd:H:2], by_head(ps[:, u, 2 + odd, 0:4 * DK]),
                                                           edge[:, u, 1, odd:H:2].unsqueeze(2).to_broadcast([P, 4, DK]), ALU.mult)
                                chain.done(last)
                                v.tensor_tensor(base1[:, u], vp[:, u, 1], from0[:, u], ALU.subtract).then_inc(base1_ready.sem, 1)
                            for u in range(U):
                                dve.wait_ge(ocross_ps.sem, ocross_ps.at(it, u + 1))
                                for odd in range(2):
                                    last = v.tensor_tensor(by_head(o_from0[:, u])[:, odd:H:2], by_head(ps[:, u, odd, 0:4 * DK]),
                                                           edge_w[:, u, odd:H:2].unsqueeze(2).to_broadcast([P, 4, DK]), ALU.mult)
                                last.then_inc(ocross_sb.sem, 1)
                            dve.wait_ge(base1_ready.sem, base1_ready.at(it, U))
                        for k in range(1, NB_):
                            rows = slice(BK * k, BK * k + BK)
                            for u in range(U):
                                dve.wait_ge(rest_ps.sem, rest_ps.at(it, (t * (NB_ - 1) + k - 1) * U + u + 1))
                                src = base1[:, u] if t else vp[:, u, 0]
                                v.tensor_tensor(rest[rows, u], src[rows], ps[rows, u, 2], ALU.subtract).then_inc(rest_ready.sem, 1)
                    for u in range(U):
                        dve.wait_ge(ocross_sb.sem, ocross_sb.at(it, u + 1))
                        dve.wait_ge(o_ps.sem, o_ps.at(it, U + u + 1))
                        v.scalar_tensor_tensor(oo[:, u, 1], ps[:, u, 1], roww[:, u, 1:2], o_from0[:, u], ALU.mult,
                                               ALU.add).then_inc(oo_ready.sem, 1)
                    dve.wait_ge(tail_in.sem, tail_in.at(it, 3 * U))
                    for u in range(U):
                        dve.wait_ge(sq_ready.sem, sq_ready.at(it, u + 1))
                        chain.done(v.tensor_reduce(ms[:, u], by_head(core_sq[:, u]), AX.X, ALU.add))
                    v.tensor_scalar(ms[:], ms[:], 1.0 / DK, LN_EPS, ALU.mult, ALU.add).then_inc(ms_ready.sem, 1)
                    dve.wait_ge(rms_ready.sem, rms_ready.at(it, 1))
                    for u in range(U):
                        chain.done(v.tensor_tensor(by_head(y[:, u]), by_head(ps[:, u, 2]),
                                                   rms[:, u].unsqueeze(2).to_broadcast([P, H, DK]), ALU.mult))
                        v.tensor_tensor(y[:, u], y[:, u], gate[:, u], ALU.mult).then_inc(y_ready.sem, 1)
                    dve.wait_ge(stored.sem, stored.at(it, 0))
                    for u in range(U):
                        dve.wait_ge(out_ps.sem, out_ps.at(it, u + 1))
                        v.tensor_tensor(x2[:, u], ps[:, u, 2, 0:D], x1[:, u], ALU.add).then_inc(x2_ready.sem, 1)
                    chain.close()


def phase_experts(nc, c, dram, NB):
    TURNS = NB // U
    G4 = 4
    TOKENS = G4 * P
    SLOTS = 2
    PAIRS, GROUPS = E1 // SLOTS, NB // G4
    SCALE = float(D1) ** -0.5
    ctx = ExitStack()
    counts = []

    def count(name, per, unit=1, again=False):
        counts.append(Count(ctx, nc, "e_" + name, per, unit, again))
        return counts[-1]

    def sb_in(stack):
        return lambda name, shape, dt=F32: stack.enter_context(nc.sbuf_tensor(name, shape, dt))

    with ctx:
        sb = sb_in(ctx)
        acc = sb("e_acc", [P, NB, D])
        xT_all = sb("e_xT_all", [P, 2, NB * P])
        w_all = sb("e_w_all", [P, NB, E1])

        with ExitStack() as attention:
            sb = sb_in(attention)
            wqkv = sb("d_wqkv", [P, 3, 2, D])
            wo = sb("d_wo", [P, 2, D])
            wsel = sb("d_wsel", [P, 2, E1])
            bqk = sb("d_bqk", [P, 2, 2])
            bv = sb("d_bv", [P, D])
            bo = sb("d_bo", [P, D])
            x = sb("d_x", [P, U, D])
            stats = sb("d_stats", [P, U, 6])
            mv = sb("d_mv", [P, U, 2])
            var = sb("d_var", [P, U])
            rstd = sb("d_rstd", [P, U])
            xn = sb("d_xn", [P, U, D])
            xnT = sb("d_xnT", [P, U, 2, P])
            qkT = sb("d_qkT", [P, U, 2, 2, P])
            vals = sb("d_vals", [P, U, D])
            s = sb("d_s", [P, U, H, P])
            neg_max = sb("d_neg_max", [P, U, H])
            probs = sb("d_probs", [P, U, H, P])
            psum = sb("d_psum", [P, U, H])
            prec = sb("d_prec", [P, U, H])
            probsT = sb("d_probsT", [P, U, H, P])
            ao = sb("d_ao", [P, U, D])
            aoT = sb("d_aoT", [P, U, 2, P])
            xb = sb("d_xb", [P, U, D])
            x3 = sb("d_x3", [P, U, D])
            x3nT = sb("d_x3nT", [P, U, 2, P])
            sig_e = sb("d_sig_e", [P, U, E1])
            sig_d = sb("d_sig_d", [P, U, E1])
            sig = sb("d_sig", [P, U, E1])
            top = sb("d_top", [P, U, 8])
            top_i = sb("d_top_i", [P, U, 8], U32)
            top_f = sb("d_top_f", [P, U, 8])
            w1 = sb("d_w1", [P, U, E1])
            w2 = sb("d_w2", [P, U, E1])
            ps = attention.enter_context(nc.psum_tensor("d_ps", [P, U, 4, 512], F32))

            w_in = attention.enter_context(nc.semaphore("d_w_in"))
            x_in = count("x_in", U, 16)
            var_ready = count("var_ready", 2)
            rstd_ready = count("rstd_ready", 2)
            xn_ready = count("xn_ready", 2 * U)
            xnT_ps = count("xnT_ps", U)
            xnT_sb = count("xnT_sb", U)
            qk_ps = count("qk_ps", U)
            v_ps = count("v_ps", U)
            qk_sb = count("qk_sb", U)
            v_sb = count("v_sb", U)
            s_ps = count("s_ps", U)
            s_ready = count("s_ready", U)
            probs_ready = count("probs_ready", U)
            probsT_ps = count("probsT_ps", 2 * U)
            probsT_sb = count("probsT_sb", 2 * U)
            pv_ps = count("pv_ps", U)
            ao_ready = count("ao_ready", U)
            aoT_ps = count("aoT_ps", U)
            aoT_sb = count("aoT_sb", U)
            out_ps = count("out_ps", U, again=True)
            out_added = count("out_added", U, again=True)
            xb_ready = count("xb_ready", U, again=True)
            x3nT_ps = count("x3nT_ps", U, again=True)
            x3nT_sb = count("x3nT_sb", U)
            sel_ps = count("sel_ps", U)
            sig_ready = count("sig_ready", U)
            routed = count("routed", U, again=True)
            ln_first = count("ln_first", 2 * U)
            ln_second = count("ln_second", 2 * U)
            dve_step = count("dve_step", D_DVE_STEPS)

            with nc.Block() as block:
                @block.sync
                def _(sp):
                    start_at_one(sp, counts)
                    for n, name in enumerate(("Wq", "Wk", "Wv")):
                        sp.dma_start(wqkv[:, n], dram["L1_gnn_" + name].rearrange("(k p) f -> p k f", p=P)).then_inc(w_in, 16)
                    sp.dma_start(wo[:], dram["L1_gnn_Wo"].rearrange("(k p) f -> p k f", p=P)).then_inc(w_in, 16)
                    sp.dma_start(wsel[:], dram["L1_ffn_expert_sel"].rearrange("(k p) f -> p k f", p=P),
                                 allow_slow_non_contiguous=True).then_inc(w_in, 16)
                    for n, name in enumerate(("bq", "bk")):
                        sp.dma_start(bqk[:, n], dram["L1_gnn_" + name].rearrange("(k p) -> p k", p=P),
                                     allow_slow_non_contiguous=True).then_inc(w_in, 16)
                    sp.dma_start(bv[:], dram["L1_gnn_bv"].partition_broadcast(P)).then_inc(w_in, 16)
                    sp.dma_start(bo[:], dram["L1_gnn_bo"].partition_broadcast(P)).then_inc(w_in, 16)
                    with sp.Fori(0, TURNS) as it:
                        for u in range(U):
                            sp.wait_ge(xb_ready.sem, xb_ready.at(it, 0))
                            hold(sp)
                            sp.dma_start(x[:, u], dram["x2"][it * U + u]).then_inc(x_in.sem, 16)

                @block.tensor
                def _(pe):
                    mm, tr = nc.tensor.matmul, nc.tensor.transpose
                    pe.wait_ge(w_in, 16 * 9)
                    with pe.Fori(0, TURNS) as it:
                        for u in range(U):
                            pe.wait_ge(routed.sem, routed.at(it, 0))
                            pe.wait_ge(xn_ready.sem, xn_ready.at(it, u + 1))
                            for k in range(2):
                                last = tr(ps[:, u, 0, P * k:P * k + P], xn[:, u, P * k:P * k + P], c["ident"][:])
                            last.then_inc(xnT_ps.sem, 1)
                        for u in range(U):
                            pe.wait_ge(xnT_sb.sem, xnT_sb.at(it, u + 1))
                            for n in range(2):
                                for m in range(2):
                                    for k in range(2):
                                        at = 2 * P * n + P * m
                                        last = mm(ps[:, u, 1, at:at + P], wqkv[:, n, k, P * m:P * m + P], xnT[:, u, k],
                                                  start=k == 0, stop=k == 1)
                            last.then_inc(qk_ps.sem, 1)
                            for k in range(2):
                                last = mm(ps[:, u, 2, 0:D], xnT[:, u, k], wqkv[:, 2, k], start=k == 0, stop=k == 1)
                            last.then_inc(v_ps.sem, 1)
                        for u in range(U):
                            pe.wait_ge(qk_sb.sem, qk_sb.at(it, u + 1))
                            pe.wait_ge(v_sb.sem, v_sb.at(it, u + 1))
                            for h in range(H):
                                part = slice(D1 * (h % 4), D1 * (h % 4) + D1)
                                at = P * (h // 4)
                                last = mm(ps[:, u, h % 4, at:at + P], qkT[part, u, 0, h // 4], qkT[part, u, 1, h // 4],
                                          start=True, stop=True)
                            last.then_inc(s_ps.sem, 1)
                        for u in range(U):
                            pe.wait_ge(probs_ready.sem, probs_ready.at(it, u + 1))
                            for half in range(2):
                                for q in range(4):
                                    last = tr(ps[:, u, half, P * q:P * q + P], probs[:, u, 4 * half + q], c["ident"][:])
                                last.then_inc(probsT_ps.sem, 1)
                        for u in range(U):
                            pe.wait_ge(probsT_sb.sem, probsT_sb.at(it, 2 * u + 2))
                            for h in range(H):
                                cols = slice(D1 * h, D1 * h + D1)
                                last = mm(ps[:, u, 2, cols], probsT[:, u, h], vals[:, u, cols], start=True, stop=True)
                            last.then_inc(pv_ps.sem, 1)
                        for u in range(U):
                            pe.wait_ge(ao_ready.sem, ao_ready.at(it, u + 1))
                            for k in range(2):
                                last = tr(ps[:, u, 3, P * k:P * k + P], ao[:, u, P * k:P * k + P], c["ident"][:])
                            last.then_inc(aoT_ps.sem, 1)
                        for u in range(U):
                            pe.wait_ge(aoT_sb.sem, aoT_sb.at(it, u + 1))
                            for k in range(2):
                                last = mm(ps[:, u, 2, D:2 * D], aoT[:, u, k], wo[:, k], start=k == 0, stop=k == 1)
                            last.then_inc(out_ps.sem, 1)
                        for u in range(U):
                            pe.wait_ge(xn_ready.sem, xn_ready.at(it, U + u + 1))
                            for k in range(2):
                                last = tr(ps[:, u, 0, P * k:P * k + P], xn[:, u, P * k:P * k + P], c["ident"][:])
                            last.then_inc(x3nT_ps.sem, 1)
                        for u in range(U):
                            pe.wait_ge(x3nT_sb.sem, x3nT_sb.at(it, u + 1))
                            for k in range(2):
                                last = mm(ps[:, u, 1, 0:E1], x3nT[:, u, k], wsel[:, k], start=k == 0, stop=k == 1)
                            last.then_inc(sel_ps.sem, 1)

                @block.scalar
                def _(act):
                    a = nc.scalar
                    act.wait_ge(w_in, 16 * 9)
                    with act.Fori(0, TURNS) as it:
                        for u in range(U):
                            act.wait_ge(xnT_ps.sem, xnT_ps.at(it, u + 1))
                            a.activation(xnT[:, u], ps[:, u, 0, 0:2 * P], ACT.Copy).then_inc(xnT_sb.sem, 1)
                        for u in range(U):
                            act.wait_ge(qk_ps.sem, qk_ps.at(it, u + 1))
                            for n in range(2):
                                for m in range(2):
                                    at = 2 * P * n + P * m
                                    last = a.activation(qkT[:, u, n, m], ps[:, u, 1, at:at + P], ACT.Identity,
                                                        bias=bqk[:, n, m:m + 1])
                            last.then_inc(qk_sb.sem, 1)
                        for u in range(U):
                            act.wait_ge(s_ready.sem, s_ready.at(it, u + 1))
                            for h in range(H):
                                last = a.activation(probs[:, u, h], s[:, u, h], ACT.Exp, bias=neg_max[:, u, h:h + 1],
                                                    accum_out=psum[:, u, h:h + 1])
                            last.then_inc(probs_ready.sem, 1)
                        for u in range(U):
                            for half in range(2):
                                act.wait_ge(probsT_ps.sem, probsT_ps.at(it, 2 * u + half + 1))
                                a.activation(probsT[:, u, 4 * half:4 * half + 4], ps[:, u, half], ACT.Copy).then_inc(probsT_sb.sem, 1)
                        for u in range(U):
                            act.wait_ge(aoT_ps.sem, aoT_ps.at(it, u + 1))
                            a.activation(aoT[:, u], ps[:, u, 3, 0:2 * P], ACT.Copy).then_inc(aoT_sb.sem, 1)
                        for u in range(U):
                            act.wait_ge(x3nT_ps.sem, x3nT_ps.at(it, u + 1))
                            src = ps[:, u, 0, 0:2 * P].rearrange("p (k t) -> p k t", k=2)
                            a.activation(xT_all[:, :, bass.ds((it * U + u) * P, P)], src, ACT.Copy)
                            a.activation(x3nT[:, u], src, ACT.Copy).then_inc(x3nT_sb.sem, 1)
                        for u in range(U):
                            act.wait_ge(sel_ps.sem, sel_ps.at(it, u + 1))
                            a.activation(sig_e[:, u], ps[:, u, 1, 0:E1], ACT.Exp, scale=-1.0).then_inc(sig_ready.sem, 1)

                @block.gpsimd
                def _(pool):
                    g = nc.gpsimd
                    pool.wait_ge(w_in, 16 * 9)

                    def deviations(it, n):
                        pool.wait_ge(var_ready.sem, var_ready.at(it, n + 1))
                        g.tensor_tensor(rstd[:], var[:], c["minus_half"][:, 0:U], ALU.pow).then_inc(rstd_ready.sem, 1)

                    def turn(it, following):
                        pool.wait_ge(xn_ready.sem, xn_ready.at(it, U))
                        pool.wait_ge(out_added.sem, out_added.at(it, 0))
                        for u in range(U):
                            g.tensor_tensor(xb[:, u], x[:, u], bo[:], ALU.add).then_inc(xb_ready.sem, 1)
                        deviations(it, 1)
                        if following is not None:
                            deviations(following, 0)

                    deviations(0, 0)
                    with pool.Fori(0, TURNS - 1) as it:
                        turn(it, it + 1)
                    turn(TURNS - 1, None)

                @block.vector
                def _(dve):
                    v = nc.vector
                    dve.wait_ge(w_in, 16 * 9)

                    def layernorm(src, it, n):
                        steps = Chain((ln_first, ln_second)[n], dve, it)
                        for u in range(U):
                            if n == 0:
                                dve.wait_ge(x_in.sem, x_in.at(it, U))
                            steps.done(v.bn_stats(stats[:, u], src[:, u]))
                            carry(nc, c)
                            steps.done(v.bn_aggr(mv[:, u], stats[:, u]))
                        v.tensor_scalar(var[:], mv[:, :, 1], LN_EPS, None, ALU.add).then_inc(var_ready.sem, 1)
                        dve.wait_ge(rstd_ready.sem, rstd_ready.at(it, n + 1))
                        if n == 0:
                            dve.wait_ge(x3nT_ps.sem, x3nT_ps.at(it, 0))
                        for u in range(U):
                            v.tensor_scalar(xn[:, u], src[:, u], mv[:, u, 0:1], rstd[:, u:u + 1],
                                            ALU.subtract, ALU.mult).then_inc(xn_ready.sem, 1)
                        steps.close()

                    def turn(it, following):
                        chain = Chain(dve_step, dve, it)

                        for u in range(U):
                            dve.wait_ge(v_ps.sem, v_ps.at(it, u + 1))
                            v.tensor_tensor(vals[:, u], ps[:, u, 2, 0:D], bv[:], ALU.add).then_inc(v_sb.sem, 1)
                        for u in range(U):
                            dve.wait_ge(s_ps.sem, s_ps.at(it, u + 1))
                            for r in range(4):
                                last = v.scalar_tensor_tensor(s[:, u, r:H:4], ps[:, u, r, 0:2 * P].rearrange("p (h k) -> p h k", h=2),
                                                              SCALE, c["adj_off"][:].unsqueeze(1).to_broadcast([P, 2, P]),
                                                              ALU.mult, ALU.add)
                            chain.done(last)
                            v.tensor_reduce(neg_max[:, u], s[:, u], AX.X, ALU.max, negate=True).then_inc(s_ready.sem, 1)
                        for u in range(U):
                            dve.wait_ge(pv_ps.sem, pv_ps.at(it, u + 1))
                            chain.done(v.reciprocal(prec[:, u], psum[:, u]))
                            v.tensor_tensor(ao[:, u].rearrange("p (h d) -> p h d", d=D1), ps[:, u, 2, 0:D].rearrange("p (h d) -> p h d", d=D1),
                                            prec[:, u].unsqueeze(2).to_broadcast([P, H, D1]), ALU.mult).then_inc(ao_ready.sem, 1)
                        dve.wait_ge(xb_ready.sem, xb_ready.at(it, U))
                        for u in range(U):
                            dve.wait_ge(out_ps.sem, out_ps.at(it, u + 1))
                            v.tensor_tensor(acc[:, bass.ds(it * U + u, 1)].rearrange("p a d -> p (a d)"), ps[:, u, 2, D:2 * D], xb[:, u], ALU.add)
                            v.tensor_tensor(x3[:, u], ps[:, u, 2, D:2 * D], xb[:, u], ALU.add).then_inc(out_added.sem, 1)
                        dve.wait_ge(out_added.sem, out_added.at(it, U))
                        layernorm(x3, it, 1)
                        if following is not None:
                            layernorm(x, following, 0)
                        for u in range(U):
                            dve.wait_ge(sig_ready.sem, sig_ready.at(it, u + 1))
                            chain.done(v.tensor_scalar(sig_d[:, u], sig_e[:, u], 1.0, None, ALU.add))
                            chain.done(v.reciprocal(sig[:, u], sig_d[:, u]))
                            carry(nc, c)
                            chain.done(v.max(top[:, u], sig[:, u]))
                            carry(nc, c)
                            chain.done(v.max_index(top_i[:, u], top[:, u], sig[:, u]))
                            chain.done(v.tensor_copy(top_f[:, u], top_i[:, u]))
                            v.tensor_scalar(w1[:, u], c["row0"][:, 0:E1], top_f[:, u, 0:1], top[:, u, 0:1], ALU.is_equal, ALU.mult)
                            chain.done(v.tensor_scalar(w2[:, u], c["row0"][:, 0:E1], top_f[:, u, 1:2], top[:, u, 1:2],
                                                       ALU.is_equal, ALU.mult))
                            v.tensor_tensor(w_all[:, bass.ds(it * U + u, 1)].rearrange("p a e -> p (a e)"), w1[:, u], w2[:, u],
                                            ALU.add).then_inc(routed.sem, 1)
                        chain.close()

                    layernorm(x, 0, 0)
                    with dve.Fori(0, TURNS - 1) as it:
                        turn(it, it + 1)
                    turn(TURNS - 1, None)
                    dve.wait_ge(routed.sem, routed.at(TURNS, 0))

        sb = sb_in(ctx)
        keys = sb("e_keys", [P, SLOTS * 2, H1])
        values = sb("e_values", [P, SLOTS, D])
        hidden = sb("e_hidden", [P, SLOTS, TOKENS])
        ps_h = ctx.enter_context(nc.psum_tensor("e_ps_h", [P, SLOTS, TOKENS], F32))
        ps_o = ctx.enter_context(nc.psum_tensor("e_ps_o", [P, SLOTS, G4, D], F32))
        attention_counts = len(counts)
        weights_in = count("weights_in", 2, 16)
        hidden_ps = count("hidden_ps", SLOTS)
        hidden_ready = count("hidden_ready", SLOTS, again=True)
        out_ps = count("expert_ps", SLOTS, again=True)
        added = count("added", SLOTS, again=True)
        stored = count("stored", NB, 16)
        expert_counts = counts[attention_counts:]

        with nc.Block() as block:
            @block.sync
            def _(sp):
                start_at_one(sp, expert_counts)
                with sp.Fori(0, PAIRS) as pair:
                    sp.wait_ge(out_ps.sem, out_ps.at(pair * GROUPS, 0))
                    hold(sp)
                    two = bass.ds(pair * SLOTS, SLOTS)
                    sp.dma_start(keys[:], dram["L1_ffn_keys"][two].rearrange("n (k p) f -> p (n k) f", p=P)).then_inc(weights_in.sem, 16)
                    sp.dma_start(values[:], dram["L1_ffn_values"][two].rearrange("n p f -> p n f")).then_inc(weights_in.sem, 16)
                sp.wait_ge(added.sem, added.at(PAIRS * GROUPS, 0))
                with sp.Fori(0, NB) as b:
                    sp.dma_start(dram["out"][b], acc[:, bass.ds(b, 1)].rearrange("p a d -> p (a d)")).then_inc(stored.sem, 16)
                sp.wait_ge(stored.sem, stored.at(1, 0))
                hold(sp)

            @block.tensor
            def _(pe):
                mm = nc.tensor.matmul
                with pe.Fori(0, PAIRS) as pair:
                    with pe.Fori(0, GROUPS) as group:
                        turn = pair * GROUPS + group
                        pe.wait_ge(weights_in.sem, weights_in.at(pair, 2))
                        for n in range(SLOTS):
                            pe.wait_ge(hidden_ready.sem, hidden_ready.at(turn, 0))
                            for k in range(2):
                                last = mm(ps_h[:, n], keys[:, 2 * n + k], xT_all[:, k, bass.ds(group * TOKENS, TOKENS)],
                                          start=k == 0, stop=k == 1)
                            last.then_inc(hidden_ps.sem, 1)
                        for n in range(SLOTS):
                            pe.wait_ge(hidden_ready.sem, hidden_ready.at(turn, n + 1))
                            pe.wait_ge(added.sem, added.at(turn, 0))
                            for q in range(G4):
                                last = mm(ps_o[:, n, q], hidden[:, n, P * q:P * q + P], values[:, n], start=True, stop=True)
                            last.then_inc(out_ps.sem, 1)

            @block.scalar
            def _(act):
                with act.Fori(0, PAIRS * GROUPS) as turn:
                    for n in range(SLOTS):
                        act.wait_ge(out_ps.sem, out_ps.at(turn, 0))
                        act.wait_ge(hidden_ps.sem, hidden_ps.at(turn, n + 1))
                        nc.scalar.activation(hidden[:, n], ps_h[:, n], ACT.Relu).then_inc(hidden_ready.sem, 1)

            @block.vector
            def _(dve):
                v = nc.vector
                with dve.Fori(0, PAIRS) as pair:
                    with dve.Fori(0, GROUPS) as group:
                        turn = pair * GROUPS + group
                        for n in range(SLOTS):
                            dve.wait_ge(out_ps.sem, out_ps.at(turn, n + 1))
                            dve.wait_ge(added.sem, added.at(turn, n))
                            for q in range(G4):
                                b = group * G4 + q
                                y = acc[:, bass.ds(b, 1)].rearrange("p a d -> p (a d)")
                                w = w_all[:, bass.ds(b, 1), bass.ds(pair * SLOTS + n, 1)].rearrange("p a e -> p (a e)")
                                last = v.scalar_tensor_tensor(y, ps_o[:, n, q], w, y, ALU.mult, ALU.add)
                            last.then_inc(added.sem, 1)


def program(nc, ins, out, upto="E"):
    dram = dict(ins)
    NB = ins["x"].shape[0]
    dram["out"] = out

    def scratch(name, shape, dt=F32):
        dram[name] = nc.dram_tensor("scratch_" + name, [NB] + shape, dt, kind="Internal").ap()

    scratch("x1", [P, D])
    scratch("gate", [P, HD])
    scratch("mask", [P, 2, P], BF16)
    scratch("krow", [P, HD])
    scratch("edge", [P, 2, H])
    scratch("perm", [P, 2, P])
    scratch("rowg", [P, 2, H])
    scratch("rowb", [P, 2, H])
    scratch("roww", [P, 2])
    scratch("vp", [P, 2, HD])
    scratch("kqT", [P, 2, 4, R])
    scratch("acomp", [P, 2, H, BK])
    scratch("x2", [P, D])
    scratch("inv", [P, 2, H, BK])
    with ExitStack() as ctx:
        c = constants(nc, ctx, dram)
        phase_rows(nc, c, dram, NB)
        if upto >= "B":
            phase_invert(nc, c, dram, NB)
        if upto >= "C":
            phase_mix(nc, c, dram, NB)
        if upto >= "E":
            phase_experts(nc, c, dram, NB)


TRANSPOSED = ("L1_gnn_Wq", "L1_gnn_Wk", "L1_gnn_Wv", "L1_gnn_Wo", "L1_ffn_expert_sel")


def kernel(**inputs):
    import concourse.bacc as bacc
    from concourse.bass_utils import run_bass_kernel_spmd

    nc = bacc.Bacc("TRN2", target_bir_lowering=False, num_devices=1)
    arrays, ins = {}, {}
    for name, a in inputs.items():
        a = np.asarray(a)
        a = np.ascontiguousarray(a.T if name in TRANSPOSED else a)
        arrays["in_" + name] = a
        ins[name] = nc.dram_tensor("in_" + name, a.shape, mybir.dt.from_np(a.dtype), kind="ExternalInput").ap()
    out = nc.dram_tensor("out", inputs["x"].shape, F32, kind="ExternalOutput").ap()
    program(nc, ins, out)
    r = run_bass_kernel_spmd(nc, [arrays], core_ids=[0])
    return r.results[0]["out"]
```

```python
from contextlib import ExitStack

import numpy as np
import concourse.bass as bass
from concourse import mybir

ALU = mybir.AluOpType
ACT = mybir.ActivationFunctionType
AX = mybir.AxisListType
F32 = mybir.dt.float32
BF16 = mybir.dt.bfloat16
I32 = mybir.dt.int32
U32 = mybir.dt.uint32

P = 128
D = 256
F1 = 128
H = 8
DK = 64
HD = H * DK
E0 = 4
TOPK = 2
R = TOPK * P
BK = 32
NB_ = P // BK
D1 = 32
E1 = 32
H1 = 128
U = 2
SMALL = E0 + 2 * H
ROWV = 2 * H + 2 * E0
LN_EPS = 1e-5
BIG = 32768.0
NEG = -1.0e9
OFF = -1.0e30


class Count:

    def __init__(self, ctx, nc, name, per, unit=1, again=False):
        self.sem = ctx.enter_context(nc.semaphore(name))
        self.per, self.unit, self.first = per, unit, int(again)

    def at(self, turn, k):
        assert k or self.first or (isinstance(turn, int) and turn)
        return turn * (self.per * self.unit) + (k * self.unit + self.first)


def start_at_one(engine, counts):
    for count in counts:
        if count.first:
            engine.sem_inc(count.sem, 1)


class Chain:

    def __init__(self, count, engine, turn):
        self.count, self.engine, self.turn, self.k = count, engine, turn, 0

    def done(self, instruction):
        self.k += 1
        instruction.then_inc(self.count.sem, 1)
        self.engine.wait_ge(self.count.sem, self.count.at(self.turn, self.k))

    def close(self):
        assert self.k == self.count.per, (self.k, self.count.per)


def carry(nc, c):
    nc.vector.memset(c["pad"][:], 0.0)


def hold(engine):
    engine.nop(nofuse=True)


def constants(nc, ctx, dram):
    def sb(name, shape, dt=F32):
        return ctx.enter_context(nc.sbuf_tensor(name, shape, dt))

    c = {
        "ident": sb("ident", [P, P]),
        "big_ident": sb("big_ident", [P, P], BF16),
        "before": sb("before", [P, P], BF16),
        "ones_bf": sb("ones_bf", [P, P], BF16),
        "ones": sb("ones", [P, P]),
        "after": sb("after", [P, P]),
        "after_block": sb("after_block", [P, P]),
        "upto": sb("upto", [P, P]),
        "upto_block": sb("upto_block", [P, BK]),
        "col_block": sb("col_block", [P, P]),
        "my_block": sb("my_block", [P, 1]),
        "in_block": sb("in_block", [P, 1]),
        "causal": sb("causal", [P, P]),
        "row1": sb("row1", [P, R]),
        "row0": sb("row0", [P, R]),
        "rowid": sb("rowid", [P, 2]),
        "adj_neg": sb("adj_neg", [P, P]),
        "adj_off": sb("adj_off", [P, P]),
        "adj_i": sb("adj_i", [P, P], I32),
        "adj_f": sb("adj_f", [P, P]),
        "dt_bias": sb("dt_bias", [P, H]),
        "neg_a": sb("neg_a", [P, H]),
        "a_log": sb("a_log", [P, H]),
        "norm_w": sb("norm_w", [P, DK]),
        "norm_w0": sb("norm_w0", [P, DK]),
        "pad": sb("pad", [P, 1]),
        "minus_half": sb("minus_half", [P, 2 * U * 2 * H]),
    }
    made = c["made"] = ctx.enter_context(nc.semaphore("const_made"))
    zeroed = ctx.enter_context(nc.semaphore("const_zeroed"))
    params = ctx.enter_context(nc.semaphore("params_loaded"))
    steps = ctx.enter_context(nc.semaphore("const_steps"))
    acted = ctx.enter_context(nc.semaphore("const_exp"))

    with nc.Block() as block:
        @block.sync
        def _(sp):
            sp.dma_start(c["adj_i"][:], dram["adj"]).then_inc(params, 16)
            sp.dma_start(c["dt_bias"][:], dram["L0_ffn_dt_bias"].partition_broadcast(P)).then_inc(params, 16)
            sp.dma_start(c["a_log"][:], dram["L0_ffn_A_log"].partition_broadcast(P)).then_inc(params, 16)
            sp.dma_start(c["norm_w0"][:], dram["L0_ffn_o_norm_weight"].partition_broadcast(P)).then_inc(params, 16)

        @block.gpsimd
        def _(pool):
            g = nc.gpsimd
            for name, value in (("ident", 0.0), ("big_ident", 0.0), ("before", 1.0), ("ones_bf", 1.0), ("ones", 1.0),
                                ("after", 1.0), ("upto", 1.0),
                                ("causal", -1.0), ("minus_half", -0.5)):
                last = g.memset(c[name][:], value)
            last.then_inc(zeroed, 1)
            pool.wait_ge(zeroed, 1)

            def keep(ap, pattern, base, cm, fill, op=ALU.is_ge):
                return g.affine_select(out=ap, in_=ap, pattern=pattern, compare_op=op, fill=fill,
                                       base=base, channel_multiplier=cm)

            keep(c["ident"][:], [[-1, P]], 0, 1, 1.0, ALU.not_equal)
            keep(c["big_ident"][:], [[-1, P]], 0, 1, BIG, ALU.not_equal)
            keep(c["before"][:], [[1, P]], -1, -1, 0.0)
            keep(c["after"][:], [[-1, P]], -1, 1, 0.0)
            keep(c["upto"][:], [[1, P]], 0, -1, 0.0)
            g.iota(c["col_block"][:].rearrange("p (k i) -> p k i", i=BK), [[1, NB_], [0, BK]], base=0, channel_multiplier=0,
                   allow_small_or_imprecise_dtypes=True)
            keep(c["causal"][:], [[1, P]], 0, -1, -2.0)
            g.iota(c["row1"][:], [[1, R]], base=1, channel_multiplier=0, allow_small_or_imprecise_dtypes=True)
            g.iota(c["row0"][:], [[1, R]], base=0, channel_multiplier=0, allow_small_or_imprecise_dtypes=True)
            g.iota(c["rowid"][:], [[P, 2]], base=0, channel_multiplier=1,
                   allow_small_or_imprecise_dtypes=True).then_inc(made, 1)

        @block.scalar
        def _(act):
            act.wait_ge(params, 64)
            nc.scalar.activation(c["neg_a"][:], c["a_log"][:], ACT.Exp).then_inc(acted, 1)

        @block.vector
        def _(dve):
            v = nc.vector
            dve.wait_ge(params, 64)
            v.tensor_scalar(c["norm_w"][:], c["norm_w0"][:], 0.5, None, ALU.mult)
            v.tensor_copy(c["adj_f"][:], c["adj_i"][:]).then_inc(steps, 1)
            dve.wait_ge(steps, 1)
            v.tensor_scalar(c["adj_neg"][:], c["adj_f"][:], -NEG, NEG, ALU.mult, ALU.add)
            v.tensor_scalar(c["adj_off"][:], c["adj_f"][:], 0.0, OFF, ALU.is_equal, ALU.mult)
            dve.wait_ge(acted, 1)
            v.tensor_scalar(c["neg_a"][:], c["neg_a"][:], -1.0, None, ALU.mult).then_inc(steps, 1)
            dve.wait_ge(steps, 2)
            dve.wait_ge(made, 1)
            v.tensor_scalar(c["my_block"][:], c["rowid"][:, 0:1], float(BK), None, ALU.is_ge).then_inc(steps, 1)
            for k in range(2, NB_):
                dve.wait_ge(steps, k + 1)
                v.scalar_tensor_tensor(c["my_block"][:], c["rowid"][:, 0:1], float(BK * k), c["my_block"][:],
                                       ALU.is_ge, ALU.add).then_inc(steps, 1)
            dve.wait_ge(steps, 5)
            v.scalar_tensor_tensor(c["in_block"][:], c["my_block"][:], -float(BK), c["rowid"][:, 0:1], ALU.mult, ALU.add)
            v.scalar_tensor_tensor(c["after_block"][:], c["col_block"][:], c["my_block"][:], c["after"][:],
                                   ALU.is_equal, ALU.mult).then_inc(steps, 1)
            dve.wait_ge(steps, 6)
            v.tensor_scalar(c["upto_block"][:], c["row0"][:, 0:BK], c["in_block"][:], None, ALU.is_ge).then_inc(steps, 1)
            dve.wait_ge(steps, 7)
    return c

A_DVE_STEPS = 56
A_POOL_STEPS = 2
C_DVE_STEPS = 7
D_DVE_STEPS = 10
R_DVE_STEPS = 12


def phase_rows(nc, c, dram, NB):
    TURNS = NB // U
    ctx = ExitStack()
    counts = []

    def sb(name, shape, dt=F32):
        return ctx.enter_context(nc.sbuf_tensor(name, shape, dt))

    def count(name, per, unit=1, again=False):
        counts.append(Count(ctx, nc, "a_" + name, per, unit, again))
        return counts[-1]

    with ctx:
        w0 = sb("a_w0", [P, 2, F1])
        att = sb("a_att", [P, 2])
        att_b = sb("a_att_b", [P, 2, P])
        wqkvg = sb("a_wqkvg", [P, 4, 2, HD])
        wsmall = sb("a_wsmall", [P, 2, SMALL])
        x = sb("a_x", [P, U, D])
        stats = sb("a_stats", [P, U, 6])
        mv = sb("a_mv", [P, U, 2])
        var = sb("a_var", [P, U])
        rstd = sb("a_rstd", [P, U])
        xn = sb("a_xn", [P, U, D])
        xnT = sb("a_xnT", [P, U, 2, P])
        hh = sb("a_hh", [P, U, 2, P])
        e_low = sb("a_e_low", [P, U, P])
        e_high = sb("a_e_high", [P, U, P])
        e_masked = sb("a_e_masked", [P, U, P])
        e_neg_max = sb("a_e_neg_max", [P, U])
        probs = sb("a_probs", [P, U, P])
        probsT = sb("a_probsT", [P, U, P])
        p_sum = sb("a_p_sum", [P, U])
        p_rec = sb("a_p_rec", [P, U])
        x1 = sb("a_x1", [P, U, D])
        x1nT = sb("a_x1nT", [P, U, 2, P])
        tanh = sb("a_tanh", [P, U, 4, HD])
        qk = sb("a_qk", [P, U, 2, HD])
        qk_sq = sb("a_qk_sq", [P, U, 2 * H, DK])
        ss = sb("a_ss", [P, U, 2 * H])
        rnorm = sb("a_rnorm", [P, U, 2 * H])
        vv = sb("a_vv", [P, U, HD])
        gg = sb("a_gg", [P, U, HD])
        gate = sb("a_gate", [P, U, HD])
        lmax = sb("a_lmax", [P, U])
        ez = sb("a_ez", [P, U, SMALL])
        zz = sb("a_zz", [P, U, H])
        ex = sb("a_ex", [P, U, SMALL])
        den = sb("a_den", [P, U, 2 * H + 1])
        rec = sb("a_rec", [P, U, 2 * H + 1])
        s1 = sb("a_s1", [P, U, H])
        s2 = sb("a_s2", [P, U, H])
        poly = sb("a_poly", [P, U, H])
        scores = sb("a_scores", [P, U, 8])
        top = sb("a_top", [P, U, 8])
        top_i = sb("a_top_i", [P, U, 8], U32)
        top_f = sb("a_top_f", [P, U, 8])
        sel = sb("a_sel", [P, U, E0])
        sel_bf = sb("a_sel_bf", [P, U, 2, E0], BF16)
        wun = sb("a_wun", [P, U, E0])
        wsum = sb("a_wsum", [P, U])
        wrec = sb("a_wrec", [P, U])
        tokv = sb("a_tokv", [P, U, ROWV])
        place = sb("a_place", [P, U, 2, E0])
        place1 = sb("a_place1", [P, U, E0])
        pT = sb("a_pT", [P, U, R])
        pP = sb("a_pP", [P, U, 2, P])
        eid = sb("a_eid", [P, U, R])
        from_e = sb("a_from_e", [P, U, 2, E0 + 1])
        eid_row = sb("a_eid_row", [P, U, 2])
        onehot = sb("a_onehot", [P, U, 2, E0])
        rv = sb("a_rv", [P, U, 2, ROWV])
        picked = sb("a_picked", [P, U, 2, 2, E0])
        w_act = sb("a_w_act", [P, U, 2, 2])
        rowg = sb("a_rowg", [P, U, 2, H])
        rowb = sb("a_rowb", [P, U, 2, H])
        roww = sb("a_roww", [P, U, 2])
        mask = sb("a_mask", [P, U, 2, P], BF16)
        mask_c = sb("a_mask_c", [P, U, 2, BK], BF16)
        straddle = sb("a_straddle", [P, U, 2])
        edge_e = sb("a_edge_e", [P, U, 2, H])
        edge = sb("a_edge", [P, U, 2, H])
        kqT = sb("a_kqT", [P, U, 2, 4, R])
        krow = sb("a_krow", [P, U, HD])
        vp = sb("a_vp", [P, U, 2, HD])
        gdecay = sb("a_gdecay", [P, U, 2, H, BK])
        decay = sb("a_decay", [P, U, 2, H, BK])
        acomp = sb("a_acomp", [P, U, 2, H, BK])

        ps = ctx.enter_context(nc.psum_tensor("a_ps", [P, U, 3, 512], F32))
        ps_small = ctx.enter_context(nc.psum_tensor("a_ps_small", [P, 512], F32))
        ps_perm = ctx.enter_context(nc.psum_tensor("a_ps_perm", [P, U, 2, P], F32))
        sm_proj = ps_small[:, 0:U * SMALL].rearrange("p (u s) -> p u s", u=U)
        sm_place = ps_small[:, 64:64 + U * 2 * E0].rearrange("p (u a e) -> p u a e", u=U, a=2)
        sm_row = ps_small[:, 128:128 + U * 2 * ROWV].rearrange("p (u t s) -> p u t s", u=U, t=2)

        sm_edge = ps[:, :, 0, 256:256 + 2 * H].rearrange("p u (t h) -> p u t h", t=2)

        w_in = ctx.enter_context(nc.semaphore("a_w_in"))
        att_ready = ctx.enter_context(nc.semaphore("a_att_ready"))
        x_in = count("x_in", U, 16)
        xn_ready = count("xn_ready", 2 * U)
        var_ready = count("var_ready", 2)
        rstd_ready = count("rstd_ready", 2)
        xnT_ps = count("xnT_ps", U)
        xnT_sb = count("xnT_sb", U)
        h_ps = count("h_ps", U)
        h_sb = count("h_sb", U)
        e_ps = count("e_ps", U)
        e_ready = count("e_ready", U)
        probs_ready = count("probs_ready", U)
        pT_ps = count("probsT_ps", U)
        pT_sb = count("probsT_sb", U)
        o_ps = count("o_ps", U)
        x1_ready = count("x1_ready", U, again=True)
        x1nT_ps = count("x1nT_ps", U, again=True)
        x1nT_sb = count("x1nT_sb", U)
        small_ps = count("small_ps", U)
        ez_ready = count("ez_ready", 1)
        ex_ready = count("ex_ready", 1)
        proj_ps = count("proj_ps", 4 * U)
        tanh_ready = count("tanh_ready", 4 * U)
        proj_sb = count("proj_sb", 4 * U)
        sq_ready = count("sq_ready", U)
        ss_ready = count("ss_ready", U)
        rnorm_ready = count("rnorm_ready", 1)
        qk_ready = count("qk_ready", U)
        gate_ready = count("gate_ready", U)
        sel_ready = count("sel_ready", 1)
        place_ps = count("place_ps", 1)
        perm_ready = count("perm_ready", U)
        rows_ps = count("rows_ps", U)
        P_sb = count("P_sb", 1)
        mask_ready = count("mask_ready", U)
        mask_c_ready = count("mask_c_ready", U)
        rowv_ready = count("rowv_ready", 1)
        perm_ps = count("perm_ps", 7 * U)
        perm_sb = count("perm_sb", 7 * U)
        gdecay_ready = count("gdecay_ready", U)
        compact_ps = count("compact_ps", U)
        decay_ready = count("decay_ready", U)
        acomp_ready = count("acomp_ready", U, again=True)
        x1_out = count("x1_out", U, 16, again=True)
        out = count("out", 11 * U, 16, again=True)
        ln_first = count("ln_first", 2 * U)
        ln_second = count("ln_second", 2 * U)
        dve_step = count("dve_step", A_DVE_STEPS)
        pool_step = count("pool_step", A_POOL_STEPS)

        PERMUTED = [(n, u) for n in range(2) for u in range(U)] + [(n, u) for u in range(U) for n in range(2, 7)]

        with nc.Block() as block:
            @block.sync
            def _(sp):
                start_at_one(sp, counts)
                sp.dma_start(w0[:], dram["L0_gnn_W"].rearrange("(k p) f -> p k f", p=P)).then_inc(w_in, 16)
                sp.dma_start(att[:], dram["L0_gnn_a"].rearrange("a o d -> o (a d)"),
                             allow_slow_non_contiguous=True).then_inc(w_in, 16)
                for n, name in enumerate(("Wq", "Wk", "Wv", "Wg")):
                    sp.dma_start(wqkvg[:, n], dram["L0_ffn_" + name].rearrange("(k p) f -> p k f", p=P)).then_inc(w_in, 16)
                at = 0
                for name, width in (("Wgate", E0), ("Wb", H), ("Wa", H)):
                    sp.dma_start(wsmall[:, :, at:at + width],
                                 dram["L0_ffn_" + name].rearrange("(k p) f -> p k f", p=P),
                                 allow_slow_non_contiguous=True).then_inc(w_in, 16)
                    at += width

                def load(it):
                    for u in range(U):
                        b = it * U + u
                        sp.wait_ge(x1_ready.sem, x1_ready.at(it, 0))
                        hold(sp)
                        sp.dma_start(x[:, u], dram["x"][b]).then_inc(x_in.sem, 16)

                def turn(it, following):
                    for u in range(U):
                        b = it * U + u
                        sp.wait_ge(x1_ready.sem, x1_ready.at(it, u + 1))
                        hold(sp)
                        sp.dma_start(dram["x1"][b], x1[:, u]).then_inc(x1_out.sem, 16)
                    if following is not None:
                        load(following)
                    for u in range(U):
                        b = it * U + u
                        sp.wait_ge(gate_ready.sem, gate_ready.at(it, u + 1))
                        hold(sp)
                        sp.dma_start(dram["gate"][b], gate[:, u]).then_inc(out.sem, 16)
                        sp.wait_ge(mask_ready.sem, mask_ready.at(it, u + 1))
                        hold(sp)
                        sp.dma_start(dram["mask"][b], mask[:, u]).then_inc(out.sem, 16)
                    sp.wait_ge(P_sb.sem, P_sb.at(it, 1))
                    hold(sp)
                    sp.wait_ge(rowv_ready.sem, rowv_ready.at(it, 1))
                    hold(sp)
                    for u in range(U):
                        b = it * U + u
                        sp.dma_start(dram["perm"][b], pP[:, u]).then_inc(out.sem, 16)
                        sp.dma_start(dram["rowg"][b], rowg[:, u]).then_inc(out.sem, 16)
                        sp.dma_start(dram["rowb"][b], rowb[:, u]).then_inc(out.sem, 16)
                        sp.dma_start(dram["roww"][b], roww[:, u]).then_inc(out.sem, 16)
                    sp.wait_ge(perm_sb.sem, perm_sb.at(it, 7 * U))
                    hold(sp)
                    for u in range(U):
                        b = it * U + u
                        sp.dma_start(dram["vp"][b], vp[:, u]).then_inc(out.sem, 16)
                        sp.dma_start(dram["krow"][b], krow[:, u]).then_inc(out.sem, 16)
                        sp.dma_start(dram["kqT"][b], kqT[:, u]).then_inc(out.sem, 16)
                    for u in range(U):
                        b = it * U + u
                        sp.wait_ge(acomp_ready.sem, acomp_ready.at(it, u + 1))
                        hold(sp)
                        sp.dma_start(dram["acomp"][b], acomp[:, u]).then_inc(out.sem, 16)
                        sp.dma_start(dram["edge"][b], edge[:, u]).then_inc(out.sem, 16)

                load(0)
                with sp.Fori(0, TURNS - 1) as it:
                    turn(it, it + 1)
                turn(TURNS - 1, None)
                sp.wait_ge(x1_out.sem, x1_out.at(TURNS, 0))
                sp.wait_ge(out.sem, out.at(TURNS, 0))

            @block.tensor
            def _(pe):
                mm, tr = nc.tensor.matmul, nc.tensor.transpose

                def places(it):
                    pe.wait_ge(sel_ready.sem, sel_ready.at(it, 1))
                    for u in range(U):
                        mm(sm_place[:, u, 0], c["before"][:], sel_bf[:, u, 0], start=True, stop=False)
                        mm(sm_place[:, u, 0], c["ones_bf"][:], sel_bf[:, u, 1], start=False, stop=True)
                        last = mm(sm_place[:, u, 1], c["ones_bf"][:], sel_bf[:, u, 1], start=True, stop=True)
                    last.then_inc(place_ps.sem, 1)

                pe.wait_ge(w_in, 16 * 9)
                pe.wait_ge(att_ready, 1)
                with pe.Fori(0, TURNS) as it:
                    for u in range(U):
                        pe.wait_ge(acomp_ready.sem, acomp_ready.at(it, 0))
                        pe.wait_ge(xn_ready.sem, xn_ready.at(it, u + 1))
                        for k in range(2):
                            last = tr(ps[:, u, 0, P * k:P * k + P], xn[:, u, P * k:P * k + P], c["ident"][:])
                        last.then_inc(xnT_ps.sem, 1)
                    for u in range(U):
                        pe.wait_ge(xnT_sb.sem, xnT_sb.at(it, u + 1))
                        for k in range(2):
                            mm(ps[:, u, 1, 0:P], xnT[:, u, k], w0[:, k], start=k == 0, stop=k == 1)
                        for k in range(2):
                            last = mm(ps[:, u, 1, P:2 * P], w0[:, k], xnT[:, u, k], start=k == 0, stop=k == 1)
                        last.then_inc(h_ps.sem, 1)
                    for u in range(U):
                        pe.wait_ge(h_sb.sem, h_sb.at(it, u + 1))
                        mm(ps[:, u, 2, 0:P], hh[:, u, 1], att_b[:, 0], start=True, stop=False)
                        mm(ps[:, u, 2, 0:P], att_b[:, 1], hh[:, u, 1], start=False, stop=True).then_inc(e_ps.sem, 1)
                    for u in range(U):
                        pe.wait_ge(probs_ready.sem, probs_ready.at(it, u + 1))
                        tr(ps[:, u, 2, P:2 * P], probs[:, u], c["ident"][:]).then_inc(pT_ps.sem, 1)
                    for u in range(U):
                        pe.wait_ge(pT_sb.sem, pT_sb.at(it, u + 1))
                        mm(ps[:, u, 2, 2 * P:3 * P], probsT[:, u], hh[:, u, 0], start=True, stop=True).then_inc(o_ps.sem, 1)
                    for u in range(U):
                        pe.wait_ge(xn_ready.sem, xn_ready.at(it, U + u + 1))
                        for k in range(2):
                            last = tr(ps[:, u, 0, 2 * P + P * k:3 * P + P * k], xn[:, u, P * k:P * k + P], c["ident"][:])
                        last.then_inc(x1nT_ps.sem, 1)
                    for u in range(U):
                        pe.wait_ge(x1nT_sb.sem, x1nT_sb.at(it, u + 1))
                        for k in range(2):
                            last = mm(sm_proj[:, u], x1nT[:, u, k], wsmall[:, k], start=k == 0, stop=k == 1)
                        last.then_inc(small_ps.sem, 1)
                    for n, bank in enumerate((1, 2, 0, 1)):
                        if n == 2:
                            places(it)
                        for u in range(U):
                            if n == 3:
                                pe.wait_ge(proj_sb.sem, proj_sb.at(it, u + 1))
                            for k in range(2):
                                last = mm(ps[:, u, bank], x1nT[:, u, k], wqkvg[:, n, k], start=k == 0, stop=k == 1)
                            last.then_inc(proj_ps.sem, 1)
                    for u in range(U):
                        pe.wait_ge(perm_ready.sem, perm_ready.at(it, u + 1))
                        for t in range(2):
                            rows = slice(P * t, P * t + P)
                            tr(ps_perm[:, u, t], pT[:, u, rows], c["ident"][:])
                            last = mm(sm_row[:, u, t], pT[:, u, rows], tokv[:, u], start=True, stop=True)
                        last.then_inc(rows_ps.sem, 1)
                    for n, u in PERMUTED:
                        if n < 2:
                            pe.wait_ge(proj_sb.sem, proj_sb.at(it, (2 + n) * U + u + 1))
                        if n == 2:
                            pe.wait_ge(qk_ready.sem, qk_ready.at(it, u + 1))
                        if n >= 3:
                            pe.wait_ge(perm_sb.sem, perm_sb.at(it, PERMUTED.index((n - 3, u)) + 1))
                        if n < 2:
                            last = mm(ps[:, u, n], pT[:, u, P * n:P * n + P], vv[:, u], start=True, stop=True)
                        elif n == 6:
                            last = mm(ps[:, u, 0], pT[:, u, 0:P], qk[:, u, 1], start=True, stop=True)
                        else:
                            which, half = (1, n - 2) if n < 4 else (0, n - 4)
                            for q in range(2):
                                pair = 2 * half + q
                                last = mm(ps[:, u, n % 3, R * q:R * q + R], qk[:, u, which, P * pair:P * pair + P],
                                          pT[:, u], start=True, stop=True)
                        last.then_inc(perm_ps.sem, 1)
                    for u in range(U):
                        pe.wait_ge(perm_sb.sem, perm_sb.at(it, PERMUTED.index((6, u)) + 1))
                        pe.wait_ge(gdecay_ready.sem, gdecay_ready.at(it, u + 1))
                        pe.wait_ge(mask_c_ready.sem, mask_c_ready.at(it, u + 1))
                        mm(sm_edge[:, u, 0], c["after"][:], rowg[:, u, 0], start=True, stop=True)
                        mm(sm_edge[:, u, 1], c["upto"][:], rowg[:, u, 1], start=True, stop=True)
                        for t in range(2):
                            dst = ps[:, u, 2, H * BK * t:H * BK * (t + 1)].rearrange("p (h i) -> p h i", h=H)
                            mm(dst, c["after_block"][:], gdecay[:, u, t], start=True, stop=False)
                            mm(dst, c["big_ident"][:], mask_c[:, u, t].unsqueeze(1).to_broadcast([P, H, BK]),
                               start=False, stop=True)
                        for t in range(2):
                            for h in range(H):
                                part = slice(DK * (h % 2), DK * (h % 2) + DK)
                                for k in range(NB_):
                                    kT = kqT[part, u, 0, h // 2, P * t + BK * k:P * t + BK * k + BK]
                                    at = (t * 4 + h // 2) * BK
                                    last = mm(ps[BK * k:BK * k + BK, u, h % 2, at:at + BK], kT, kT, start=True, stop=True)
                        last.then_inc(compact_ps.sem, 1)

            @block.scalar
            def _(act):
                a = nc.scalar
                with act.Fori(0, TURNS) as it:
                    for u in range(U):
                        act.wait_ge(xnT_ps.sem, xnT_ps.at(it, u + 1))
                        a.activation(xnT[:, u], ps[:, u, 0, 0:2 * P], ACT.Copy).then_inc(xnT_sb.sem, 1)
                    for u in range(U):
                        act.wait_ge(h_ps.sem, h_ps.at(it, u + 1))
                        a.activation(hh[:, u], ps[:, u, 1, 0:2 * P], ACT.Copy).then_inc(h_sb.sem, 1)
                    for u in range(U):
                        act.wait_ge(e_ready.sem, e_ready.at(it, u + 1))
                        a.activation(probs[:, u], e_masked[:, u], ACT.Exp, bias=e_neg_max[:, u:u + 1],
                                     accum_out=p_sum[:, u:u + 1]).then_inc(probs_ready.sem, 1)
                    for u in range(U):
                        act.wait_ge(pT_ps.sem, pT_ps.at(it, u + 1))
                        a.activation(probsT[:, u], ps[:, u, 2, P:2 * P], ACT.Copy).then_inc(pT_sb.sem, 1)
                    for u in range(U):
                        act.wait_ge(x1nT_ps.sem, x1nT_ps.at(it, u + 1))
                        a.activation(x1nT[:, u], ps[:, u, 0, 2 * P:4 * P], ACT.Copy).then_inc(x1nT_sb.sem, 1)
                    act.wait_ge(ez_ready.sem, ez_ready.at(it, 1))
                    a.activation(ex[:], ez[:], ACT.Exp).then_inc(ex_ready.sem, 1)
                    for n, bank in enumerate((1, 2, 0, 1)):
                        for u in range(U):
                            act.wait_ge(proj_ps.sem, proj_ps.at(it, n * U + u + 1))
                            a.activation(tanh[:, u, n], ps[:, u, bank], ACT.Tanh, scale=0.5).then_inc(tanh_ready.sem, 1)
                        if n == 1:
                            for u in range(U):
                                act.wait_ge(proj_sb.sem, proj_sb.at(it, U + u + 1))
                                a.activation(qk_sq[:, u], qk[:, u].rearrange("p a (h d) -> p (a h) d", d=DK), ACT.Square).then_inc(sq_ready.sem, 1)
                    act.wait_ge(out.sem, out.at(it, 0))
                    act.wait_ge(rows_ps.sem, rows_ps.at(it, U))
                    a.activation(pP[:], ps_perm[:], ACT.Copy).then_inc(P_sb.sem, 1)
                    for n, u in PERMUTED:
                        act.wait_ge(perm_ps.sem, perm_ps.at(it, PERMUTED.index((n, u)) + 1))
                        if n < 2:
                            dst = vp[:, u, n]
                        elif n == 6:
                            dst = krow[:, u]
                        else:
                            which, half = (0, n - 2) if n < 4 else (1, n - 4)
                            dst = kqT[:, u, which, 2 * half:2 * half + 2]
                        a.activation(dst, ps[:, u, n % 3], ACT.Copy).then_inc(perm_sb.sem, 1)
                    for u in range(U):
                        act.wait_ge(compact_ps.sem, compact_ps.at(it, u + 1))
                        a.activation(edge_e[:, u], sm_edge[:, u], ACT.Exp)
                        a.activation(decay[:, u], ps[:, u, 2], ACT.Exp).then_inc(decay_ready.sem, 1)

            @block.gpsimd
            def _(pool):
                g = nc.gpsimd

                def deviations(it, n):
                    pool.wait_ge(var_ready.sem, var_ready.at(it, n + 1))
                    g.tensor_tensor(rstd[:], var[:], c["minus_half"][:, 0:U], ALU.pow).then_inc(rstd_ready.sem, 1)

                def turn(it, following):
                    chain = Chain(pool_step, pool, it)
                    deviations(it, 1)
                    for u in range(U):
                        pool.wait_ge(ss_ready.sem, ss_ready.at(it, u + 1))
                        chain.done(g.tensor_tensor(rnorm[:, u], ss[:, u], c["minus_half"][:, 0:2 * H], ALU.pow))
                        y = qk[:, u].rearrange("p a (h d) -> p (a h) d", d=DK)
                        g.tensor_tensor(y, y, rnorm[:, u].unsqueeze(2).to_broadcast([P, 2 * H, DK]),
                                        ALU.mult).then_inc(qk_ready.sem, 1)
                    pool.wait_ge(out.sem, out.at(it, 0))
                    for u in range(U):
                        pool.wait_ge(proj_sb.sem, proj_sb.at(it, 3 * U + u + 1))
                        g.tensor_tensor(gate[:, u].rearrange("p (h d) -> p h d", d=DK), gg[:, u].rearrange("p (h d) -> p h d", d=DK),
                                        c["norm_w"][:].unsqueeze(1).to_broadcast([P, H, DK]), ALU.mult).then_inc(gate_ready.sem, 1)
                    pool.wait_ge(rowv_ready.sem, rowv_ready.at(it, 1))
                    for u in range(U):
                        for t in range(2):
                            last = g.tensor_tensor(gdecay[:, u, t], c["upto_block"][:].unsqueeze(1).to_broadcast([P, H, BK]),
                                                   rowg[:, u, t].unsqueeze(2).to_broadcast([P, H, BK]), ALU.mult)
                        last.then_inc(gdecay_ready.sem, 1)
                    chain.close()
                    if following is not None:
                        deviations(following, 0)

                deviations(0, 0)
                with pool.Fori(0, TURNS - 1) as it:
                    turn(it, it + 1)
                turn(TURNS - 1, None)

            @block.vector
            def _(dve):
                v = nc.vector
                dve.wait_ge(w_in, 16 * 9)
                v.tensor_scalar(att_b[:, 0], c["ones"][:], att[:, 0:1], None, ALU.mult)
                v.memset(scores[:], -1.0)
                v.memset(from_e[:], 0.0)
                v.memset(sel_bf[:], 0.0)
                v.tensor_scalar(att_b[:, 1], c["ones"][:], att[:, 1:2], None, ALU.mult).then_inc(att_ready, 1)
                dve.wait_ge(att_ready, 1)
                def layernorm(src, it, n):
                    steps = Chain((ln_first, ln_second)[n], dve, it)
                    for u in range(U):
                        if n == 0:
                            dve.wait_ge(x_in.sem, x_in.at(it, U))
                        steps.done(v.bn_stats(stats[:, u], src[:, u]))
                        carry(nc, c)
                        steps.done(v.bn_aggr(mv[:, u], stats[:, u]))
                    v.tensor_scalar(var[:], mv[:, :, 1], LN_EPS, None, ALU.add).then_inc(var_ready.sem, 1)
                    dve.wait_ge(rstd_ready.sem, rstd_ready.at(it, n + 1))
                    if n == 0:
                        dve.wait_ge(x1nT_ps.sem, x1nT_ps.at(it, 0))
                    for u in range(U):
                        v.tensor_scalar(xn[:, u], src[:, u], mv[:, u, 0:1], rstd[:, u:u + 1],
                                        ALU.subtract, ALU.mult).then_inc(xn_ready.sem, 1)
                    steps.close()

                def turn(it, following):
                    chain = Chain(dve_step, dve, it)

                    def project(first, last):
                        for n in range(first, last):
                            for u in range(U):
                                dve.wait_ge(tanh_ready.sem, tanh_ready.at(it, n * U + u + 1))
                                dst = (qk[:, u, 0], qk[:, u, 1], vv[:, u], gg[:, u])[n]
                                v.scalar_tensor_tensor(dst, tanh[:, u, n], 1.0, ps[:, u, (1, 2, 0, 1)[n]], ALU.add,
                                                       ALU.mult).then_inc(proj_sb.sem, 1)


                    for u in range(U):
                        dve.wait_ge(e_ps.sem, e_ps.at(it, u + 1))
                        v.scalar_tensor_tensor(e_low[:, u], ps[:, u, 2, 0:P], 0.2, c["adj_neg"][:], ALU.mult, ALU.add)
                        chain.done(v.tensor_tensor(e_high[:, u], ps[:, u, 2, 0:P], c["adj_neg"][:], ALU.add))
                        chain.done(v.tensor_tensor(e_masked[:, u], e_low[:, u], e_high[:, u], ALU.max))
                        v.tensor_reduce(e_neg_max[:, u:u + 1], e_masked[:, u], AX.X, ALU.max, negate=True).then_inc(e_ready.sem, 1)
                    dve.wait_ge(x1_out.sem, x1_out.at(it, 0))
                    for u in range(U):
                        v.tensor_tensor(x1[:, u, F1:D], hh[:, u, 0], x[:, u, F1:D], ALU.add)
                    for u in range(U):
                        dve.wait_ge(probs_ready.sem, probs_ready.at(it, u + 1))
                        last = v.reciprocal(p_rec[:, u:u + 1], p_sum[:, u:u + 1])
                    chain.done(last)
                    for u in range(U):
                        dve.wait_ge(o_ps.sem, o_ps.at(it, u + 1))
                        v.scalar_tensor_tensor(x1[:, u, 0:F1], ps[:, u, 2, 2 * P:3 * P], p_rec[:, u:u + 1], x[:, u, 0:F1],
                                               ALU.mult, ALU.add).then_inc(x1_ready.sem, 1)
                        dve.wait_ge(x1_ready.sem, x1_ready.at(it, u + 1))
                    layernorm(x1, it, 1)
                    dve.wait_ge(small_ps.sem, small_ps.at(it, U))
                    v.tensor_reduce(lmax[:], sm_proj[:, :, 0:E0], AX.X, ALU.max)
                    v.tensor_scalar(ez[:, :, E0:E0 + H], sm_proj[:, :, E0:E0 + H], -1.0, None, ALU.mult)
                    chain.done(v.tensor_tensor(zz[:], sm_proj[:, :, E0 + H:SMALL],
                                               c["dt_bias"][:].unsqueeze(1).to_broadcast([P, U, H]), ALU.add))
                    v.tensor_tensor(ez[:, :, 0:E0], sm_proj[:, :, 0:E0], lmax[:].unsqueeze(2).to_broadcast([P, U, E0]),
                                    ALU.subtract)
                    v.scalar_tensor_tensor(ez[:, :, E0 + H:SMALL], zz[:], -1.0, zz[:], ALU.mult, ALU.min).then_inc(ez_ready.sem, 1)
                    dve.wait_ge(ex_ready.sem, ex_ready.at(it, 1))
                    v.tensor_scalar(den[:, :, 0:H], ex[:, :, E0:E0 + H], 1.0, None, ALU.add)
                    v.tensor_scalar(den[:, :, H:2 * H], ex[:, :, E0 + H:SMALL], 2.0, None, ALU.add)
                    chain.done(v.tensor_reduce(den[:, :, 2 * H:2 * H + 1], ex[:, :, 0:E0], AX.X, ALU.add))
                    chain.done(v.reciprocal(rec[:], den[:]))
                    v.tensor_tensor(scores[:, :, 0:E0], ex[:, :, 0:E0], rec[:, :, 2 * H:2 * H + 1].to_broadcast([P, U, E0]), ALU.mult)
                    chain.done(v.tensor_tensor(s1[:], ex[:, :, E0 + H:SMALL], rec[:, :, H:2 * H], ALU.mult))
                    chain.done(v.tensor_tensor(s2[:], s1[:], s1[:], ALU.mult))
                    chain.done(v.tensor_scalar(poly[:], s2[:], 2.0 / 17.0, None, ALU.mult))
                    for m in range(7, 0, -1):
                        chain.done(v.scalar_tensor_tensor(poly[:], poly[:], 2.0 / (2 * m + 1), s2[:], ALU.add, ALU.mult))
                    chain.done(v.scalar_tensor_tensor(poly[:], poly[:], 2.0, s1[:], ALU.add, ALU.mult))
                    chain.done(v.scalar_tensor_tensor(poly[:], zz[:], 0.0, poly[:], ALU.max, ALU.add))
                    chain.done(v.tensor_tensor(poly[:], poly[:], c["neg_a"][:].unsqueeze(1).to_broadcast([P, U, H]), ALU.mult))
                    v.tensor_scalar(tokv[:, :, 2 * E0 + H:ROWV], poly[:], -1000.0, None, ALU.max)
                    v.tensor_copy(tokv[:, :, 2 * E0:2 * E0 + H], rec[:, :, 0:H])
                    for u in range(U):
                        carry(nc, c)
                        chain.done(v.max(top[:, u], scores[:, u]))
                        carry(nc, c)
                        chain.done(v.max_index(top_i[:, u], top[:, u], scores[:, u]))
                    chain.done(v.tensor_copy(top_f[:], top_i[:]))
                    for u in range(U):
                        chain.done(v.tensor_scalar(sel[:, u], c["row0"][:, 0:E0], top_f[:, u, 0:1], None, ALU.is_equal))
                        chain.done(v.scalar_tensor_tensor(sel[:, u], c["row0"][:, 0:E0], top_f[:, u, 1:2], sel[:, u],
                                                          ALU.is_equal, ALU.add))
                    v.tensor_copy(sel_bf[:, :, 0], sel[:])
                    v.tensor_copy(sel_bf[:, :, 1, 1:2], sel[:, :, 0:1])
                    chain.done(v.tensor_tensor(sel_bf[:, :, 1, 2:3], sel[:, :, 0:1], sel[:, :, 1:2], ALU.add))
                    v.tensor_tensor(sel_bf[:, :, 1, 3:4], sel_bf[:, :, 1, 2:3], sel[:, :, 2:3], ALU.add).then_inc(sel_ready.sem, 1)
                    chain.done(v.tensor_tensor(wun[:], scores[:, :, 0:E0], sel[:], ALU.mult))
                    chain.done(v.tensor_tensor(wsum[:].unsqueeze(2), top[:, :, 0:1], top[:, :, 1:2], ALU.add))
                    chain.done(v.reciprocal(wrec[:], wsum[:]))
                    chain.done(v.tensor_tensor(wun[:], wun[:], wrec[:].unsqueeze(2).to_broadcast([P, U, E0]), ALU.mult))
                    v.tensor_scalar(tokv[:, :, 0:E0], wun[:], 0.5 * DK ** -0.5, None, ALU.mult)
                    chain.done(v.tensor_scalar(tokv[:, :, E0:2 * E0], wun[:], 0.0, None, ALU.is_gt))
                    project(0, 2)
                    dve.wait_ge(place_ps.sem, place_ps.at(it, 1))
                    chain.done(v.tensor_copy(place[:], sm_place))
                    chain.done(v.scalar_tensor_tensor(place1[:], place[:, :, 0], 1.0, sel[:], ALU.add, ALU.mult))
                    for u in range(U):
                        chain.done(v.tensor_scalar(pT[:, u], c["row1"][:], place1[:, u, 0:1], None, ALU.is_equal))
                        for e in range(1, E0):
                            last = v.scalar_tensor_tensor(pT[:, u], c["row1"][:], place1[:, u, e:e + 1], pT[:, u],
                                                          ALU.is_equal, ALU.add)
                            if e < E0 - 1:
                                chain.done(last)
                        last.then_inc(perm_ready.sem, 1)
                    for u in range(U):
                        dve.wait_ge(sq_ready.sem, sq_ready.at(it, u + 1))
                        chain.done(v.tensor_reduce(ss[:, u], qk_sq[:, u], AX.X, ALU.add))
                        v.tensor_scalar(ss[:, u], ss[:, u], 4e-6, None, ALU.add).then_inc(ss_ready.sem, 1)
                    project(2, 4)
                    for u in range(U):
                        for t in range(2):
                            v.tensor_scalar(from_e[:, u, t, 0:E0], place[:, u, 1], c["rowid"][:, t:t + 1], None, ALU.is_le)
                        chain.done(v.tensor_scalar(eid[:, u], c["row0"][:], place[:, u, 1, 1:2], None, ALU.is_ge))
                        for e in range(2, E0):
                            chain.done(v.scalar_tensor_tensor(eid[:, u], c["row0"][:], place[:, u, 1, e:e + 1], eid[:, u],
                                                              ALU.is_ge, ALU.add))
                    chain.done(v.tensor_reduce(eid_row[:].rearrange("p u t -> p (u t)"),
                                               from_e[:, :, :, 1:E0].rearrange("p u t e -> p (u t) e"), AX.X, ALU.add))
                    dve.wait_ge(out.sem, out.at(it, 0))
                    for u in range(U):
                        for t in range(2):
                            last = v.scalar_tensor_tensor(mask[:, u, t], eid[:, u, P * t:P * t + P], eid_row[:, u, t:t + 1],
                                                          c["causal"][:], ALU.is_equal, ALU.add)
                        last.then_inc(mask_ready.sem, 1)
                        v.tensor_scalar(straddle[:, u], eid_row[:, u], eid[:, u, P - 1:P], None, ALU.is_equal)
                    for u in range(U):
                        dve.wait_ge(mask_ready.sem, mask_ready.at(it, u + 1))
                        for k in range(NB_):
                            rows = slice(BK * k, BK * k + BK)
                            last = v.tensor_copy(mask_c[rows, u], mask[rows, u, :, rows])
                        last.then_inc(mask_c_ready.sem, 1)
                    dve.wait_ge(rows_ps.sem, rows_ps.at(it, U))
                    v.tensor_copy(rv[:], sm_row)
                    chain.done(v.tensor_tensor(onehot[:], from_e[:, :, :, 0:E0], from_e[:, :, :, 1:E0 + 1], ALU.subtract))
                    for a in range(2):
                        last = v.tensor_tensor(picked[:, :, :, a], rv[:, :, :, E0 * a:E0 * a + E0], onehot[:], ALU.mult)
                    chain.done(last)
                    chain.done(v.tensor_reduce(w_act[:].rearrange("p u t a -> p (u t a)"),
                                               picked[:].rearrange("p u t a e -> p (u t a) e"), AX.X, ALU.add))
                    v.tensor_copy(roww[:], w_act[:, :, :, 0])
                    active = w_act[:, :, :, 1:2].to_broadcast([P, U, 2, H])
                    v.tensor_tensor(rowb[:], rv[:, :, :, 2 * E0:2 * E0 + H], active, ALU.mult)
                    v.tensor_tensor(rowg[:], rv[:, :, :, 2 * E0 + H:ROWV], active, ALU.mult).then_inc(rowv_ready.sem, 1)
                    if following is not None:
                        layernorm(x, following, 0)
                    for u in range(U):
                        dve.wait_ge(decay_ready.sem, decay_ready.at(it, u + 1))
                        v.tensor_tensor(edge[:, u], edge_e[:, u], straddle[:, u].unsqueeze(2).to_broadcast([P, 2, H]), ALU.mult)
                        for odd in range(2):
                            last = v.tensor_tensor(acomp[:, u, :, odd:H:2], ps[:, u, odd, 0:256].rearrange("p (t h i) -> p t h i", t=2, h=4),
                                                   decay[:, u, :, odd:H:2], ALU.mult)
                        last.then_inc(acomp_ready.sem, 1)
                    chain.close()

                layernorm(x, 0, 0)
                with dve.Fori(0, TURNS - 1) as it:
                    turn(it, it + 1)
                turn(TURNS - 1, None)

        with nc.Block() as block:
            @block.gpsimd
            def _(pool):
                for semaphore in [w_in, att_ready] + [each.sem for each in counts]:
                    pool.sem_clear(semaphore)


def phase_invert(nc, c, dram, NB):
    GROUP = P // (2 * H)
    TURNS = NB // GROUP
    SY = 2 * H
    MIDDLE = BK // 2
    ctx = ExitStack()
    counts = []

    def sb(name, shape, dt=F32):
        return ctx.enter_context(nc.sbuf_tensor(name, shape, dt))

    def count(name, per, unit=1, again=False):
        counts.append(Count(ctx, nc, "b_" + name, per, unit, again))
        return counts[-1]

    with ctx:
        a_in = sb("b_a_in", [P, GROUP, SY, BK])
        beta_in = sb("b_beta_in", [P, GROUP, SY])
        betaT = sb("b_betaT", [P, 2, P])
        a_sys = sb("b_a_sys", [P, 2, BK, NB_, BK])
        x_sys = sb("b_x_sys", [P, 2, BK, NB_, BK])
        eyes = sb("b_eyes", [P, BK, NB_, BK])
        prod_d = sb("b_prod_d", [P, BK * NB_ * BK // 4])
        prod_p = sb("b_prod_p", [P, BK * BK // 4 + BK])
        inv = sb("b_inv", [P, P, BK])
        ps = ctx.enter_context(nc.psum_tensor("b_ps", [P, 4, 4, P], F32))
        ps_beta = ctx.enter_context(nc.psum_tensor("b_ps_beta", [P, P], F32))
        ps_back = ctx.enter_context(nc.psum_tensor("b_ps_back", [P, 3, 4, P], F32))

        zeroed = ctx.enter_context(nc.semaphore("b_zeroed"))
        loaded = count("loaded", 2, 16)
        beta_ps = count("beta_ps", 1)
        beta_sb = count("beta_sb", 1, again=True)
        sys_ps = count("sys_ps", 8, again=True)
        sys_sb = count("sys_sb", 8, again=True)
        eye = count("eye", 1)
        pool_step = count("pool_step", 2 * (BK - 1), again=True)
        dve_step = count("dve_step", 2 * (BK - 1))
        scaled = count("scaled", 1, again=True)
        back_ps = count("back_ps", 8, again=True)
        back_sb = count("back_sb", 8, again=True)
        stored = count("stored", 1, 16, again=True)

        def update(engine, side, lo, hi, prod, chain, steps):
            for s in steps:
                rows, cols = BK - 1 - s, s + 1
                p = prod[:, 0:rows * (hi - lo) * cols].rearrange("p (r k c) -> p r k c", r=rows, k=hi - lo)
                factor = a_sys[:, side, s + 1:BK, lo:hi, s:s + 1].to_broadcast([P, rows, hi - lo, cols])
                row = x_sys[:, side, s:s + 1, lo:hi, 0:cols].to_broadcast([P, rows, hi - lo, cols])
                below = x_sys[:, side, s + 1:BK, lo:hi, 0:cols]
                chain.done(engine.tensor_tensor(p, factor, row, ALU.mult))
                chain.done(engine.tensor_tensor(below, below, p, ALU.subtract))

        def turns(engine, turn):
            with engine.Fori(0, TURNS // 2 - 1) as two:
                for side in range(2):
                    turn(two * 2 + side, side, two * 2 + (side + 1))
            turn(TURNS - 2, 0, TURNS - 1)
            turn(TURNS - 1, 1, None)

        with nc.Block() as block:
            @block.sync
            def _(sp):
                start_at_one(sp, counts)

                def load(it):
                    if not isinstance(it, int):
                        sp.wait_ge(sys_ps.sem, sys_ps.at(it, 0))
                        hold(sp)
                    sp.dma_start(a_in[:], dram["acomp"][bass.ds(it * GROUP, GROUP)].rearrange("b p t h i -> p b (t h) i")).then_inc(loaded.sem, 16)
                    sp.dma_start(beta_in[:], dram["rowb"][bass.ds(it * GROUP, GROUP)].rearrange("b p t h -> p b (t h)"),
                                 allow_slow_non_contiguous=True).then_inc(loaded.sem, 16)

                def store(it):
                    sp.wait_ge(back_sb.sem, back_sb.at(it, 8))
                    hold(sp)
                    sp.dma_start(dram["inv"][bass.ds(it * GROUP, GROUP)].rearrange("b p t h i -> p b (t h i)"),
                                 inv[:].rearrange("p (b s) i -> p b (s i)", b=GROUP)).then_inc(stored.sem, 16)

                load(0)
                with sp.Fori(0, TURNS - 1) as it:
                    load(it + 1)
                    store(it)
                store(TURNS - 1)
                sp.wait_ge(stored.sem, stored.at(TURNS, 0))

            @block.tensor
            def _(pe):
                tr = nc.tensor.transpose
                a_flat = a_in[:].rearrange("p b s i -> p (b s) i")

                def to_systems(it):
                    pe.wait_ge(loaded.sem, loaded.at(it, 2))
                    pe.wait_ge(beta_sb.sem, beta_sb.at(it, 0))
                    tr(ps_beta[:], beta_in[:].rearrange("p b s -> p (b s)"), c["ident"][:]).then_inc(beta_ps.sem, 1)
                    for n in range(8):
                        if n >= 4:
                            pe.wait_ge(sys_sb.sem, sys_sb.at(it, n - 3))
                        else:
                            pe.wait_ge(sys_sb.sem, sys_sb.at(it, 0))
                        for q in range(4):
                            last = tr(ps[:, n % 4, q], a_flat[:, :, 4 * n + q], c["ident"][:])
                        last.then_inc(sys_ps.sem, 1)

                def turn(it, side, following):
                    if following is not None:
                        to_systems(following)
                    pe.wait_ge(scaled.sem, scaled.at(it, 1))
                    for n in range(8):
                        if n >= 3:
                            pe.wait_ge(back_sb.sem, back_sb.at(it, n - 2))
                        else:
                            pe.wait_ge(back_sb.sem, back_sb.at(it, 0))
                        for q in range(4):
                            last = tr(ps_back[:, n % 3, q], x_sys[:, side, 4 * n + q].rearrange("p k c -> p (k c)"), c["ident"][:])
                        last.then_inc(back_ps.sem, 1)

                to_systems(0)
                turns(pe, turn)

            @block.scalar
            def _(act):
                def betas(it, side):
                    act.wait_ge(beta_ps.sem, beta_ps.at(it, 1))
                    nc.scalar.activation(betaT[:, side], ps_beta[:], ACT.Copy).then_inc(beta_sb.sem, 1)

                def turn(it, side, following):
                    if following is not None:
                        act.wait_ge(scaled.sem, scaled.at(it, 0))
                        betas(following, 1 - side)
                    act.wait_ge(stored.sem, stored.at(it, 0))
                    for n in range(8):
                        act.wait_ge(back_ps.sem, back_ps.at(it, n + 1))
                        nc.scalar.activation(inv[:].rearrange("p s i -> p i s")[:, 4 * n:4 * n + 4], ps_back[:, n % 3],
                                             ACT.Copy).then_inc(back_sb.sem, 1)

                betas(0, 0)
                turns(act, turn)

            @block.gpsimd
            def _(pool):
                g = nc.gpsimd
                g.memset(eyes[:], 0.0).then_inc(zeroed, 1)
                pool.wait_ge(zeroed, 1)
                g.affine_select(out=eyes[:], in_=eyes[:], pattern=[[1, BK], [0, NB_], [-1, BK]],
                                compare_op=ALU.not_equal, fill=1.0, base=0, channel_multiplier=0).then_inc(zeroed, 1)
                pool.wait_ge(zeroed, 2)

                def start(side):
                    g.tensor_tensor(x_sys[:, side], eyes[:], eyes[:], ALU.mult).then_inc(eye.sem, 1)

                def turn(it, side, following):
                    pool.wait_ge(eye.sem, eye.at(it, 1))
                    pool.wait_ge(sys_sb.sem, sys_sb.at(it, 8))
                    chain = Chain(pool_step, pool, it)
                    update(g, side, NB_ - 1, NB_, prod_p, chain, range(BK - 1))
                    chain.close()
                    if following is not None:
                        pool.wait_ge(back_ps.sem, back_ps.at(it, 0))
                        start(1 - side)
                    pool.wait_ge(dve_step.sem, dve_step.at(it, dve_step.per))
                    g.tensor_tensor(x_sys[:, side], x_sys[:, side],
                                    betaT[:, side].rearrange("p (k r) -> p r k", k=NB_).unsqueeze(3).to_broadcast([P, BK, NB_, BK]),
                                    ALU.mult).then_inc(scaled.sem, 1)

                start(0)
                turns(pool, turn)

            @block.vector
            def _(dve):
                v = nc.vector

                def take(it, side):
                    dve.wait_ge(beta_sb.sem, beta_sb.at(it, 1))
                    for n in range(8):
                        dve.wait_ge(sys_ps.sem, sys_ps.at(it, n + 1))
                        v.tensor_tensor(a_sys[:, side, 4 * n:4 * n + 4].rearrange("p i k c -> p i (k c)"), ps[:, n % 4],
                                        betaT[:, side].unsqueeze(1).to_broadcast([P, 4, P]), ALU.mult).then_inc(sys_sb.sem, 1)

                def turn(it, side, following):
                    dve.wait_ge(eye.sem, eye.at(it, 1))
                    dve.wait_ge(sys_sb.sem, sys_sb.at(it, 8))
                    chain = Chain(dve_step, dve, it)
                    update(v, side, 0, NB_ - 1, prod_d, chain, range(MIDDLE))
                    if following is not None:
                        dve.wait_ge(pool_step.sem, pool_step.at(it, 0))
                        take(following, 1 - side)
                    update(v, side, 0, NB_ - 1, prod_d, chain, range(MIDDLE, BK - 1))
                    chain.close()

                take(0, 0)
                turns(dve, turn)


def phase_mix(nc, c, dram, NB):
    TURNS = NB // U
    ctx = ExitStack()
    counts = []

    def sb(name, shape, dt=F32):
        return ctx.enter_context(nc.sbuf_tensor(name, shape, dt))

    def count(name, per, unit=1, again=False):
        counts.append(Count(ctx, nc, "c_" + name, per, unit, again))
        return counts[-1]

    DECAYS = [(t, half) for t in range(2) for half in range(2)]
    PRODUCTS = [(t, (h, h + 2)) for t in range(2) for h in (0, 1, 4, 5)]
    ND, NP = len(DECAYS), len(PRODUCTS)

    with ctx:
        wo = sb("c_wo", [P, 4, D])
        kqT = sb("c_kqT", [P, U, 2, 4, R])
        vp = sb("c_vp", [P, U, 2, HD])
        mask = sb("c_mask", [P, U, 2, P], BF16)
        krow = sb("c_krow", [P, U, HD])
        edge = sb("c_edge", [P, U, 2, H])
        krow_edge = sb("c_krow_edge", [P, U, HD])
        edge_w = sb("c_edge_w", [P, U, H])
        state = sb("c_state", [P, U, 4, 2 * DK])
        from0 = sb("c_from0", [P, U, HD])
        o_from0 = sb("c_o_from0", [P, U, HD])
        perm = sb("c_perm", [P, U, 2, P])
        inv = sb("c_inv", [P, U, 2, H, BK])
        rowg = sb("c_rowg", [P, U, 2, H])
        roww = sb("c_roww", [P, U, 2])
        gate = sb("c_gate", [P, U, HD])
        x1 = sb("c_x1", [P, U, D])
        gsum = sb("c_gsum", [P, U, 2, H, P])
        decay = sb("c_decay", [P, U, 2, H, P])
        mix = sb("c_mix", [P, U, 2, H, 2, P])
        rest = sb("c_rest", [P, U, HD])
        base1 = sb("c_base1", [P, U, HD])
        uu = sb("c_uu", [P, U, 2, HD])
        oo = sb("c_oo", [P, U, 2, HD])
        core_sq = sb("c_core_sq", [P, U, HD])
        ms = sb("c_ms", [P, U, H])
        rms = sb("c_rms", [P, U, H])
        y = sb("c_y", [P, U, HD])
        yT = sb("c_yT", [P, U, 4, P])
        x2 = sb("c_x2", [P, U, D])
        ps = ctx.enter_context(nc.psum_tensor("c_ps", [P, U, 4, 512], F32))

        w_in = ctx.enter_context(nc.semaphore("c_w_in"))
        zeroed = ctx.enter_context(nc.semaphore("c_zeroed"))
        g_in = count("g_in", 2 * U, 16)
        kq_in = count("kq_in", U, 16)
        v_in = count("v_in", 5 * U, 16)
        tail_in = count("tail_in", 3 * U, 16)
        gsum_ready = count("gsum_ready", U)
        decay_ps = count("decay_ps", ND * U, again=True)
        decay_sb = count("decay_sb", ND * U)
        prod_ps = count("prod_ps", NP * U)
        mix_ready = count("mix_ready", NP * U, again=True)
        solve_ps = count("solve_ps", 2 * NB_ * U)
        uu_ready = count("uu_ready", 2 * NB_ * U)
        rest_ps = count("rest_ps", 2 * (NB_ - 1) * U)
        rest_ready = count("rest_ready", 2 * (NB_ - 1) * U)
        krow_ready = count("krow_ready", U)
        state_ps = count("state_ps", U, again=True)
        state_ready = count("state_ready", U)
        cross_ps = count("cross_ps", U)
        ocross_ps = count("ocross_ps", U, again=True)
        ocross_sb = count("ocross_sb", U)
        base1_ready = count("base1_ready", U)
        o_ps = count("o_ps", 2 * U)
        oo0_ready = count("oo0_ready", U)
        oo_ready = count("oo_ready", U)
        core_ps = count("core_ps", U, again=True)
        sq_ready = count("sq_ready", U)
        ms_ready = count("ms_ready", 1)
        rms_ready = count("rms_ready", 1)
        y_ready = count("y_ready", U)
        yT_ps = count("yT_ps", U)
        yT_ready = count("yT_ready", U)
        out_ps = count("out_ps", U)
        x2_ready = count("x2_ready", U, again=True)
        stored = count("stored", U, 16, again=True)
        dve_step = count("dve_step", C_DVE_STEPS)

        def head_cols(h):
            return slice(DK * h, DK * h + DK)

        def key_part(h):
            return slice(DK * (h % 2), DK * (h % 2) + DK)

        def by_head(ap):
            return ap.rearrange("p (h d) -> p h d", d=DK)

        with nc.Block() as block:
            @block.sync
            def _(sp):
                start_at_one(sp, counts)

                def load_decays(it):
                    for u in range(U):
                        b = it * U + u
                        sp.wait_ge(decay_ps.sem, decay_ps.at(it, 0))
                        hold(sp)
                        sp.dma_start(rowg[:, u], dram["rowg"][b]).then_inc(g_in.sem, 16)
                        sp.dma_start(mask[:, u], dram["mask"][b]).then_inc(g_in.sem, 16)

                def load_keys(it):
                    for u in range(U):
                        b = it * U + u
                        sp.wait_ge(ocross_ps.sem, ocross_ps.at(it, 0))
                        hold(sp)
                        sp.dma_start(kqT[:, u], dram["kqT"][b]).then_inc(kq_in.sem, 16)

                def load_values(it):
                    for u in range(U):
                        b = it * U + u
                        sp.wait_ge(core_ps.sem, core_ps.at(it, 0))
                        hold(sp)
                        sp.dma_start(vp[:, u], dram["vp"][b]).then_inc(v_in.sem, 16)
                        sp.dma_start(inv[:, u], dram["inv"][b]).then_inc(v_in.sem, 16)
                        sp.dma_start(roww[:, u], dram["roww"][b]).then_inc(v_in.sem, 16)
                        sp.dma_start(krow[:, u], dram["krow"][b]).then_inc(v_in.sem, 16)
                        sp.dma_start(edge[:, u], dram["edge"][b]).then_inc(v_in.sem, 16)

                def load_tail(it):
                    for u in range(U):
                        b = it * U + u
                        sp.wait_ge(x2_ready.sem, x2_ready.at(it, 0))
                        hold(sp)
                        sp.dma_start(perm[:, u], dram["perm"][b]).then_inc(tail_in.sem, 16)
                        sp.dma_start(gate[:, u], dram["gate"][b]).then_inc(tail_in.sem, 16)
                        sp.dma_start(x1[:, u], dram["x1"][b]).then_inc(tail_in.sem, 16)

                def turn(it, following):
                    if following is not None:
                        load_decays(following)
                        load_keys(following)
                        load_values(following)
                    for u in range(U):
                        b = it * U + u
                        sp.wait_ge(x2_ready.sem, x2_ready.at(it, u + 1))
                        hold(sp)
                        sp.dma_start(dram["x2"][b], x2[:, u]).then_inc(stored.sem, 16)
                    if following is not None:
                        load_tail(following)

                load_decays(0)
                load_keys(0)
                load_values(0)
                load_tail(0)
                sp.dma_start(wo[:], dram["L0_ffn_Wo"].rearrange("(k p) f -> p k f", p=P)).then_inc(w_in, 16)
                with sp.Fori(0, TURNS - 1) as it:
                    turn(it, it + 1)
                turn(TURNS - 1, None)
                sp.wait_ge(stored.sem, stored.at(TURNS, 0))

            @block.tensor
            def _(pe):
                mm, tr = nc.tensor.matmul, nc.tensor.transpose

                def decays(it, first, last):
                    for n in range(first, last):
                        t, half = DECAYS[n]
                        for u in range(U):
                            if n == 0:
                                pe.wait_ge(g_in.sem, g_in.at(it, 2 * U))
                                pe.wait_ge(gsum_ready.sem, gsum_ready.at(it, u + 1))
                            if n >= 2:
                                pe.wait_ge(decay_sb.sem, decay_sb.at(it, (n - 2) * U + u + 1))
                            dst = ps[:, u, n % 2].rearrange("p (h i) -> p h i", h=4)
                            mm(dst, c["after"][:], gsum[:, u, t, 4 * half:4 * half + 4], start=True, stop=False)
                            mm(dst, c["big_ident"][:], mask[:, u, t].unsqueeze(1).to_broadcast([P, 4, P]),
                               start=False, stop=True).then_inc(decay_ps.sem, 1)

                def turn(it, following):
                    pe.wait_ge(kq_in.sem, kq_in.at(it, U))
                    for n, (t, heads) in enumerate(PRODUCTS):
                        for u in range(U):
                            if n < 2:
                                pe.wait_ge(decay_sb.sem, decay_sb.at(it, (2 + n) * U + u + 1))
                            elif n < 4:
                                pe.wait_ge(x2_ready.sem, x2_ready.at(it, 0))
                            else:
                                pe.wait_ge(mix_ready.sem, mix_ready.at(it, (n - 4) * U + u + 1))
                            for m, h in enumerate(heads):
                                dst = ps[:, u, n % 4, 2 * P * m:2 * P * m + 2 * P].rearrange("p (a i) -> p a i", a=2)
                                last = mm(dst, kqT[key_part(h), u, 0, h // 2, P * t:P * t + P],
                                          kqT[key_part(h), u, :, h // 2, P * t:P * t + P], start=True, stop=True)
                            last.then_inc(prod_ps.sem, 1)
                    pe.wait_ge(mix_ready.sem, mix_ready.at(it, NP * U))
                    pe.wait_ge(v_in.sem, v_in.at(it, 5 * U))
                    for t in range(2):
                        if t == 1:
                            for u in range(U):
                                pe.wait_ge(krow_ready.sem, krow_ready.at(it, u + 1))
                                pe.wait_ge(uu_ready.sem, uu_ready.at(it, (NB_ - 1) * U + u + 1))
                                for pair in range(4):
                                    cols = slice(2 * DK * pair, 2 * DK * pair + 2 * DK)
                                    last = mm(ps[:, u, 2, cols], krow_edge[:, u, cols], uu[:, u, 0, cols], start=True, stop=True)
                                last.then_inc(state_ps.sem, 1)
                            for u in range(U):
                                pe.wait_ge(state_ready.sem, state_ready.at(it, u + 1))
                                for pair in range(4):
                                    last = mm(ps[:, u, 3, 2 * DK * pair:2 * DK * pair + 2 * DK], kqT[:, u, 0, pair, P:R],
                                              state[:, u, pair], start=True, stop=True)
                                last.then_inc(cross_ps.sem, 1)
                            for u in range(U):
                                for pair in range(4):
                                    last = mm(ps[:, u, 0, 2 * DK * pair:2 * DK * pair + 2 * DK], kqT[:, u, 1, pair, P:R],
                                              state[:, u, pair], start=True, stop=True)
                                last.then_inc(ocross_ps.sem, 1)
                        for k in range(NB_):
                            rows = slice(BK * k, BK * k + BK)
                            if k:
                                for u in range(U):
                                    pe.wait_ge(uu_ready.sem, uu_ready.at(it, (t * NB_ + k - 1) * U + u + 1))
                                    if k < 3:
                                        hold(pe)
                                    for h in range(H):
                                        last = mm(ps[rows, u, 2, head_cols(h)], mix[0:BK * k, u, t, h, 0, rows],
                                                  uu[0:BK * k, u, t, head_cols(h)], start=True, stop=True)
                                    last.then_inc(rest_ps.sem, 1)
                            for u in range(U):
                                if k:
                                    pe.wait_ge(rest_ready.sem, rest_ready.at(it, (t * (NB_ - 1) + k - 1) * U + u + 1))
                                    pe.wait_ge(uu_ready.sem, uu_ready.at(it, (t * NB_ + k - 1) * U + u + 1))
                                elif t:
                                    pe.wait_ge(base1_ready.sem, base1_ready.at(it, u + 1))
                                hold(pe)
                                src = rest[:, u] if k else (base1[:, u] if t else vp[:, u, 0])
                                for h in range(H):
                                    last = mm(ps[rows, u, 3, head_cols(h)], inv[rows, u, t, h],
                                              src[rows, head_cols(h)], start=True, stop=True)
                                last.then_inc(solve_ps.sem, 1)
                    for t in range(2):
                        for u in range(U):
                            pe.wait_ge(uu_ready.sem, uu_ready.at(it, (2 * NB_ - 1) * U + u + 1))
                            for h in range(H):
                                last = mm(ps[:, u, t, head_cols(h)], mix[:, u, t, h, 1], uu[:, u, t, head_cols(h)],
                                          start=True, stop=True)
                            last.then_inc(o_ps.sem, 1)
                    pe.wait_ge(tail_in.sem, tail_in.at(it, 3 * U))
                    for u in range(U):
                        pe.wait_ge(oo0_ready.sem, oo0_ready.at(it, u + 1))
                        pe.wait_ge(oo_ready.sem, oo_ready.at(it, u + 1))
                        for t in range(2):
                            last = mm(ps[:, u, 2], perm[:, u, t], oo[:, u, t], start=t == 0, stop=t == 1)
                        last.then_inc(core_ps.sem, 1)
                    if following is not None:
                        decays(following, 0, ND)
                    for u in range(U):
                        pe.wait_ge(y_ready.sem, y_ready.at(it, u + 1))
                        for k in range(4):
                            last = tr(ps[:, u, 3, P * k:P * k + P], y[:, u, P * k:P * k + P], c["ident"][:])
                        last.then_inc(yT_ps.sem, 1)
                    pe.wait_ge(w_in, 16)
                    for u in range(U):
                        pe.wait_ge(yT_ready.sem, yT_ready.at(it, u + 1))
                        for k in range(4):
                            last = mm(ps[:, u, 2, 0:D], yT[:, u, k], wo[:, k], start=k == 0, stop=k == 3)
                        last.then_inc(out_ps.sem, 1)

                decays(0, 0, ND)
                with pe.Fori(0, TURNS - 1) as it:
                    turn(it, it + 1)
                turn(TURNS - 1, None)

            @block.scalar
            def _(act):
                a = nc.scalar

                def decays(it):
                    for n, (t, half) in enumerate(DECAYS):
                        for u in range(U):
                            act.wait_ge(decay_ps.sem, decay_ps.at(it, n * U + u + 1))
                            if n == 0:
                                act.wait_ge(mix_ready.sem, mix_ready.at(it, 0))
                            a.activation(decay[:, u, t, 4 * half:4 * half + 4], ps[:, u, n % 2].rearrange("p (h i) -> p h i", h=4),
                                         ACT.Exp).then_inc(decay_sb.sem, 1)

                def turn(it, following):
                    for t in range(2):
                        if t == 1:
                            for u in range(U):
                                act.wait_ge(state_ps.sem, state_ps.at(it, u + 1))
                                for odd in range(2):
                                    part = slice(DK * odd, DK * odd + DK)
                                    last = a.activation(state[part, u, :, part], ps[part, u, 2].rearrange("p (h d) -> p h d", d=2 * DK)[:, :, part],
                                                        ACT.Copy)
                                last.then_inc(state_ready.sem, 1)
                        for k in range(NB_):
                            rows = slice(BK * k, BK * k + BK)
                            for u in range(U):
                                act.wait_ge(solve_ps.sem, solve_ps.at(it, (t * NB_ + k) * U + u + 1))
                                a.activation(uu[rows, u, t], ps[rows, u, 3], ACT.Copy).then_inc(uu_ready.sem, 1)
                    for u in range(U):
                        act.wait_ge(o_ps.sem, o_ps.at(it, u + 1))
                        a.activation(oo[:, u, 0], ps[:, u, 0], ACT.Copy, scale=roww[:, u, 0:1]).then_inc(oo0_ready.sem, 1)
                    for u in range(U):
                        act.wait_ge(core_ps.sem, core_ps.at(it, u + 1))
                        a.activation(core_sq[:, u], ps[:, u, 2], ACT.Square).then_inc(sq_ready.sem, 1)
                    if following is not None:
                        decays(following)
                    for u in range(U):
                        act.wait_ge(yT_ps.sem, yT_ps.at(it, u + 1))
                        a.activation(yT[:, u], ps[:, u, 3], ACT.Copy).then_inc(yT_ready.sem, 1)

                act.wait_ge(zeroed, 1)
                decays(0)
                with act.Fori(0, TURNS - 1) as it:
                    turn(it, it + 1)
                turn(TURNS - 1, None)

            @block.gpsimd
            def _(pool):
                g = nc.gpsimd

                def sums(it):
                    pool.wait_ge(g_in.sem, g_in.at(it, 2 * U))
                    pool.wait_ge(decay_ps.sem, decay_ps.at(it, 0))
                    for u in range(U):
                        for t in range(2):
                            last = g.tensor_tensor(gsum[:, u, t], c["upto"][:].unsqueeze(1).to_broadcast([P, H, P]),
                                                   rowg[:, u, t].unsqueeze(2).to_broadcast([P, H, P]), ALU.mult)
                        last.then_inc(gsum_ready.sem, 1)

                def turn(it, following):
                    pool.wait_ge(v_in.sem, v_in.at(it, 5 * U))
                    pool.wait_ge(state_ps.sem, state_ps.at(it, 0))
                    for u in range(U):
                        g.tensor_tensor(by_head(krow_edge[:, u]), by_head(krow[:, u]),
                                        edge[:, u, 0].unsqueeze(2).to_broadcast([P, H, DK]), ALU.mult).then_inc(krow_ready.sem, 1)
                    if following is not None:
                        sums(following)
                    pool.wait_ge(ms_ready.sem, ms_ready.at(it, 1))
                    g.tensor_tensor(rms[:].rearrange("p u h -> p (u h)"), ms[:].rearrange("p u h -> p (u h)"),
                                    c["minus_half"][:, 0:U * H], ALU.pow).then_inc(rms_ready.sem, 1)

                sums(0)
                with pool.Fori(0, TURNS - 1) as it:
                    turn(it, it + 1)
                turn(TURNS - 1, None)

            @block.vector
            def _(dve):
                v = nc.vector
                v.memset(state[:], 0.0).then_inc(zeroed, 1)
                with dve.Fori(0, TURNS) as it:
                    chain = Chain(dve_step, dve, it)
                    dve.wait_ge(decay_sb.sem, decay_sb.at(it, ND * U))
                    for n, (t, heads) in enumerate(PRODUCTS):
                        for u in range(U):
                            dve.wait_ge(prod_ps.sem, prod_ps.at(it, n * U + u + 1))
                            pair = slice(heads[0], heads[1] + 1, 2)
                            v.tensor_tensor(mix[:, u, t, pair], ps[:, u, n % 4].rearrange("p (h a i) -> p h a i", h=2, a=2),
                                            decay[:, u, t, pair].unsqueeze(2).to_broadcast([P, 2, 2, P]), ALU.mult).then_inc(mix_ready.sem, 1)
                    dve.wait_ge(v_in.sem, v_in.at(it, 5 * U))
                    for u in range(U):
                        last = v.tensor_scalar(edge_w[:, u], edge[:, u, 1], roww[:, u, 1:2], None, ALU.mult)
                    chain.done(last)
                    for t in range(2):
                        if t == 1:
                            for u in range(U):
                                dve.wait_ge(cross_ps.sem, cross_ps.at(it, u + 1))
                                chain.done(v.tensor_tensor(by_head(from0[:, u]), by_head(ps[:, u, 3]),
                                                           edge[:, u, 1].unsqueeze(2).to_broadcast([P, H, DK]), ALU.mult))
                                v.tensor_tensor(base1[:, u], vp[:, u, 1], from0[:, u], ALU.subtract).then_inc(base1_ready.sem, 1)
                            for u in range(U):
                                dve.wait_ge(ocross_ps.sem, ocross_ps.at(it, u + 1))
                                v.tensor_tensor(by_head(o_from0[:, u]), by_head(ps[:, u, 0]),
                                                edge_w[:, u].unsqueeze(2).to_broadcast([P, H, DK]), ALU.mult).then_inc(ocross_sb.sem, 1)
                            dve.wait_ge(base1_ready.sem, base1_ready.at(it, U))
                        for k in range(1, NB_):
                            rows = slice(BK * k, BK * k + BK)
                            for u in range(U):
                                dve.wait_ge(rest_ps.sem, rest_ps.at(it, (t * (NB_ - 1) + k - 1) * U + u + 1))
                                src = base1[:, u] if t else vp[:, u, 0]
                                v.tensor_tensor(rest[rows, u], src[rows], ps[rows, u, 2], ALU.subtract).then_inc(rest_ready.sem, 1)
                    for u in range(U):
                        dve.wait_ge(ocross_sb.sem, ocross_sb.at(it, u + 1))
                        dve.wait_ge(o_ps.sem, o_ps.at(it, U + u + 1))
                        v.scalar_tensor_tensor(oo[:, u, 1], ps[:, u, 1], roww[:, u, 1:2], o_from0[:, u], ALU.mult,
                                               ALU.add).then_inc(oo_ready.sem, 1)
                    dve.wait_ge(tail_in.sem, tail_in.at(it, 3 * U))
                    for u in range(U):
                        dve.wait_ge(sq_ready.sem, sq_ready.at(it, u + 1))
                        chain.done(v.tensor_reduce(ms[:, u], by_head(core_sq[:, u]), AX.X, ALU.add))
                    v.tensor_scalar(ms[:], ms[:], 1.0 / DK, LN_EPS, ALU.mult, ALU.add).then_inc(ms_ready.sem, 1)
                    dve.wait_ge(rms_ready.sem, rms_ready.at(it, 1))
                    for u in range(U):
                        chain.done(v.tensor_tensor(by_head(y[:, u]), by_head(ps[:, u, 2]),
                                                   rms[:, u].unsqueeze(2).to_broadcast([P, H, DK]), ALU.mult))
                        v.tensor_tensor(y[:, u], y[:, u], gate[:, u], ALU.mult).then_inc(y_ready.sem, 1)
                    dve.wait_ge(stored.sem, stored.at(it, 0))
                    for u in range(U):
                        dve.wait_ge(out_ps.sem, out_ps.at(it, u + 1))
                        v.tensor_tensor(x2[:, u], ps[:, u, 2, 0:D], x1[:, u], ALU.add).then_inc(x2_ready.sem, 1)
                    chain.close()


def phase_experts(nc, c, dram, NB):
    TURNS = NB // U
    TILES = 2 * NB + E1
    CLEAR = TILES // TURNS
    assert CLEAR * TURNS == TILES
    SCALE = float(D1) ** -0.5
    ctx = ExitStack()
    counts = []

    def count(name, per, unit=1, again=False):
        counts.append(Count(ctx, nc, "e_" + name, per, unit, again))
        return counts[-1]

    def sb_in(stack):
        return lambda name, shape, dt=F32: stack.enter_context(nc.sbuf_tensor(name, shape, dt))

    with ctx:
        sb = sb_in(ctx)
        acc = sb("e_acc", [P, NB, D])
        mean_all = sb("e_mean_all", [P, NB])
        rstd_all = sb("e_rstd_all", [P, NB])
        weights = sb("e_weights", [P, NB, 2])
        chosen = sb("e_chosen", [P, NB, 2])
        xs_rows = dram["sorted_x"].rearrange("t p d -> (t p) d")
        ys_rows = dram["sorted_y"].rearrange("t p d -> (t p) d")

        with ExitStack() as attention:
            sb = sb_in(attention)
            wqkv = sb("d_wqkv", [P, 3, 2, D])
            wo = sb("d_wo", [P, 2, D])
            wsel = sb("d_wsel", [P, 2, E1])
            bqk = sb("d_bqk", [P, 2, 2])
            bv = sb("d_bv", [P, D])
            bo = sb("d_bo", [P, D])
            x = sb("d_x", [P, U, D])
            stats = sb("d_stats", [P, U, 6])
            mv = sb("d_mv", [P, U, 2])
            var = sb("d_var", [P, U])
            rstd = sb("d_rstd", [P, U])
            xn = sb("d_xn", [P, U, D])
            x3n = sb("d_x3n", [P, U, D])
            xnT = sb("d_xnT", [P, U, 2, P])
            qkT = sb("d_qkT", [P, U, 2, 2, P])
            vals = sb("d_vals", [P, U, D])
            s = sb("d_s", [P, U, H, P])
            neg_max = sb("d_neg_max", [P, U, H])
            probs = sb("d_probs", [P, U, H, P])
            psum = sb("d_psum", [P, U, H])
            prec = sb("d_prec", [P, U, H])
            probsT = sb("d_probsT", [P, U, H, P])
            ao = sb("d_ao", [P, U, D])
            aoT = sb("d_aoT", [P, U, 2, P])
            xb = sb("d_xb", [P, U, D])
            x3 = sb("d_x3", [P, U, D])
            x3nT = sb("d_x3nT", [P, U, 2, P])
            sig_e = sb("d_sig_e", [P, U, E1])
            sig_d = sb("d_sig_d", [P, U, E1])
            sig = sb("d_sig", [P, U, E1])
            top = sb("d_top", [P, U, 8])
            top_i = sb("d_top_i", [P, U, 8], U32)
            zeros = sb("d_zeros", [P, CLEAR * D])
            ps = attention.enter_context(nc.psum_tensor("d_ps", [P, U, 4, 512], F32))

            w_in = attention.enter_context(nc.semaphore("d_w_in"))
            zeros_made = attention.enter_context(nc.semaphore("d_zeros_made"))
            x_in = count("x_in", U, 16)
            cleared = count("cleared", 1, 16)
            var_ready = [count("var_ready%d" % n, 1) for n in range(2)]
            rstd_ready = [count("rstd_ready%d" % n, 1) for n in range(2)]
            xn_ready = [count("xn_ready%d" % n, U) for n in range(2)]
            xnT_ps = count("xnT_ps", U)
            xnT_sb = count("xnT_sb", U)
            qk_ps = count("qk_ps", U)
            v_ps = count("v_ps", U)
            qk_sb = count("qk_sb", U)
            v_sb = count("v_sb", U)
            s_ps = count("s_ps", U)
            s_ready = count("s_ready", U)
            probs_ready = count("probs_ready", U)
            probsT_ps = count("probsT_ps", 2 * U)
            probsT_sb = count("probsT_sb", 2 * U)
            pv_ps = count("pv_ps", U)
            ao_ready = count("ao_ready", U)
            aoT_ps = count("aoT_ps", U)
            aoT_sb = count("aoT_sb", U)
            out_ps = count("out_ps", U)
            out_added = count("out_added", U, again=True)
            xb_ready = count("xb_ready", U, again=True)
            x3nT_ps = count("x3nT_ps", U)
            x3nT_sb = count("x3nT_sb", U)
            sel_ps = count("sel_ps", U)
            sig_ready = count("sig_ready", U)
            routed = count("routed", U)
            ln_first = count("ln_first", 2 * U)
            ln_second = count("ln_second", 2 * U)
            score_step = count("score_step", U)
            dve_step = count("dve_step", D_DVE_STEPS)

            with nc.Block() as block:
                @block.sync
                def _(sp):
                    start_at_one(sp, counts)

                    def turn(it):
                        for u in range(U):
                            sp.wait_ge(xb_ready.sem, xb_ready.at(it, 0))
                            hold(sp)
                            sp.dma_start(x[:, u], dram["x2"][it * U + u]).then_inc(x_in.sem, 16)
                        if isinstance(it, int):
                            load_weights()
                        sp.wait_ge(zeros_made, 1)
                        sp.dma_start(xs_rows[bass.ds(it * (CLEAR * P), CLEAR * P)].rearrange("(p r) d -> p (r d)", p=P),
                                     zeros[:]).then_inc(cleared.sem, 16)

                    def load_weights():
                        for n, name in enumerate(("Wq", "Wk", "Wv")):
                            sp.dma_start(wqkv[:, n], dram["L1_gnn_" + name].rearrange("(k p) f -> p k f", p=P)).then_inc(w_in, 16)
                        sp.dma_start(wo[:], dram["L1_gnn_Wo"].rearrange("(k p) f -> p k f", p=P)).then_inc(w_in, 16)
                        sp.dma_start(wsel[:], dram["L1_ffn_expert_sel"].rearrange("(k p) f -> p k f", p=P),
                                     allow_slow_non_contiguous=True).then_inc(w_in, 16)
                        for n, name in enumerate(("bq", "bk")):
                            sp.dma_start(bqk[:, n], dram["L1_gnn_" + name].rearrange("(k p) -> p k", p=P),
                                         allow_slow_non_contiguous=True).then_inc(w_in, 16)
                        sp.dma_start(bv[:], dram["L1_gnn_bv"].partition_broadcast(P)).then_inc(w_in, 16)
                        sp.dma_start(bo[:], dram["L1_gnn_bo"].partition_broadcast(P)).then_inc(w_in, 16)

                    turn(0)
                    with sp.Fori(1, TURNS) as it:
                        turn(it)
                    sp.wait_ge(cleared.sem, cleared.at(TURNS, 0))

                @block.tensor
                def _(pe):
                    mm, tr = nc.tensor.matmul, nc.tensor.transpose
                    pe.wait_ge(w_in, 16 * 9)

                    def front(it, before):
                        for u in range(U):
                            pe.wait_ge(xn_ready[0].sem, xn_ready[0].at(it, u + 1))
                            for k in range(2):
                                last = tr(ps[:, u, 0, P * k:P * k + P], xn[:, u, P * k:P * k + P], c["ident"][:])
                            last.then_inc(xnT_ps.sem, 1)

                        def project(u):
                            pe.wait_ge(xnT_sb.sem, xnT_sb.at(it, u + 1))
                            for n in range(2):
                                for m in range(2):
                                    for k in range(2):
                                        at = 2 * P * n + P * m
                                        last = mm(ps[:, u, 1, at:at + P], wqkv[:, n, k, P * m:P * m + P], xnT[:, u, k],
                                                  start=k == 0, stop=k == 1)
                            last.then_inc(qk_ps.sem, 1)
                            for k in range(2):
                                last = mm(ps[:, u, 0, D:2 * D], xnT[:, u, k], wqkv[:, 2, k], start=k == 0, stop=k == 1)
                            last.then_inc(v_ps.sem, 1)

                        def score(u):
                            pe.wait_ge(qk_sb.sem, qk_sb.at(it, u + 1))
                            pe.wait_ge(v_sb.sem, v_sb.at(it, u + 1))
                            if before is not None:
                                pe.wait_ge(sig_ready.sem, sig_ready.at(before, u + 1))
                            for h in range(H):
                                part = slice(D1 * (h % 4), D1 * (h % 4) + D1)
                                at = P * (h // 4)
                                last = mm(ps[:, u, h % 4, at:at + P], qkT[part, u, 0, h // 4], qkT[part, u, 1, h // 4],
                                          start=True, stop=True)
                            last.then_inc(s_ps.sem, 1)

                        project(0)
                        if before is not None:
                            select(before)
                        for u in range(U):
                            score(u)
                            if u + 1 < U:
                                project(u + 1)

                    def attend(it):
                        for u in range(U):
                            pe.wait_ge(probs_ready.sem, probs_ready.at(it, u + 1))
                            for half in range(2):
                                for q in range(4):
                                    last = tr(ps[:, u, half, P * q:P * q + P], probs[:, u, 4 * half + q], c["ident"][:])
                                last.then_inc(probsT_ps.sem, 1)
                            pe.wait_ge(probsT_sb.sem, probsT_sb.at(it, 2 * u + 2))
                            for h in range(H):
                                cols = slice(D1 * h, D1 * h + D1)
                                last = mm(ps[:, u, 2, cols], probsT[:, u, h], vals[:, u, cols], start=True, stop=True)
                            last.then_inc(pv_ps.sem, 1)
                        for u in range(U):
                            pe.wait_ge(ao_ready.sem, ao_ready.at(it, u + 1))
                            for k in range(2):
                                last = tr(ps[:, u, 3, P * k:P * k + P], ao[:, u, P * k:P * k + P], c["ident"][:])
                            last.then_inc(aoT_ps.sem, 1)
                        for u in range(U):
                            pe.wait_ge(aoT_sb.sem, aoT_sb.at(it, u + 1))
                            for k in range(2):
                                last = mm(ps[:, u, 2, D:2 * D], aoT[:, u, k], wo[:, k], start=k == 0, stop=k == 1)
                            last.then_inc(out_ps.sem, 1)

                    def select(it):
                        for u in range(U):
                            pe.wait_ge(xn_ready[1].sem, xn_ready[1].at(it, u + 1))
                            for k in range(2):
                                last = tr(ps[:, u, 3, P * k:P * k + P], x3n[:, u, P * k:P * k + P], c["ident"][:])
                            last.then_inc(x3nT_ps.sem, 1)
                        for u in range(U):
                            pe.wait_ge(x3nT_sb.sem, x3nT_sb.at(it, u + 1))
                            for k in range(2):
                                last = mm(ps[:, u, 3, 2 * P:2 * P + E1], x3nT[:, u, k], wsel[:, k], start=k == 0, stop=k == 1)
                            last.then_inc(sel_ps.sem, 1)

                    front(0, None)
                    with pe.Fori(0, TURNS - 1) as it:
                        attend(it)
                        front(it + 1, it)
                    attend(TURNS - 1)
                    select(TURNS - 1)

                @block.scalar
                def _(act):
                    a = nc.scalar
                    act.wait_ge(w_in, 16 * 9)

                    def front(it):
                        for u in range(U):
                            act.wait_ge(xnT_ps.sem, xnT_ps.at(it, u + 1))
                            a.activation(xnT[:, u], ps[:, u, 0, 0:2 * P], ACT.Copy).then_inc(xnT_sb.sem, 1)
                        take_projections(it, 0)

                    def take_projections(it, u):
                        act.wait_ge(qk_ps.sem, qk_ps.at(it, u + 1))
                        for n in range(2):
                            for m in range(2):
                                at = 2 * P * n + P * m
                                last = a.activation(qkT[:, u, n, m], ps[:, u, 1, at:at + P], ACT.Identity,
                                                    bias=bqk[:, n, m:m + 1])
                        last.then_inc(qk_sb.sem, 1)

                    def turn(it, following):
                        for u in range(1, U):
                            take_projections(it, u)
                        for u in range(U):
                            act.wait_ge(s_ready.sem, s_ready.at(it, u + 1))
                            for h in range(H):
                                last = a.activation(probs[:, u, h], s[:, u, h], ACT.Exp, bias=neg_max[:, u, h:h + 1],
                                                    accum_out=psum[:, u, h:h + 1])
                            last.then_inc(probs_ready.sem, 1)
                            for half in range(2):
                                act.wait_ge(probsT_ps.sem, probsT_ps.at(it, 2 * u + half + 1))
                                a.activation(probsT[:, u, 4 * half:4 * half + 4], ps[:, u, half], ACT.Copy).then_inc(probsT_sb.sem, 1)
                        for u in range(U):
                            act.wait_ge(aoT_ps.sem, aoT_ps.at(it, u + 1))
                            a.activation(aoT[:, u], ps[:, u, 3, 0:2 * P], ACT.Copy).then_inc(aoT_sb.sem, 1)
                        if following is not None:
                            front(following)
                        for u in range(U):
                            act.wait_ge(x3nT_ps.sem, x3nT_ps.at(it, u + 1))
                            a.activation(x3nT[:, u], ps[:, u, 3, 0:2 * P].rearrange("p (k t) -> p k t", k=2), ACT.Copy).then_inc(x3nT_sb.sem, 1)
                        for u in range(U):
                            act.wait_ge(sel_ps.sem, sel_ps.at(it, u + 1))
                            a.activation(sig_e[:, u], ps[:, u, 3, 2 * P:2 * P + E1], ACT.Exp, scale=-1.0).then_inc(sig_ready.sem, 1)

                    front(0)
                    with act.Fori(0, TURNS - 1) as it:
                        turn(it, it + 1)
                    turn(TURNS - 1, None)

                @block.gpsimd
                def _(pool):
                    g = nc.gpsimd
                    g.memset(zeros[:], 0.0).then_inc(zeros_made, 1)

                    def deviations(it, n):
                        pool.wait_ge(var_ready[n].sem, var_ready[n].at(it, 1))
                        g.tensor_tensor(rstd[:], var[:], c["minus_half"][:, 0:U], ALU.pow).then_inc(rstd_ready[n].sem, 1)

                    def turn(it, following):
                        pool.wait_ge(xn_ready[0].sem, xn_ready[0].at(it, U))
                        pool.wait_ge(out_added.sem, out_added.at(it, 0))
                        for u in range(U):
                            g.tensor_tensor(xb[:, u], x[:, u], bo[:], ALU.add).then_inc(xb_ready.sem, 1)
                        if following is not None:
                            deviations(following, 0)
                        deviations(it, 1)

                    deviations(0, 0)
                    pool.wait_ge(w_in, 16 * 9)
                    with pool.Fori(0, TURNS - 1) as it:
                        turn(it, it + 1)
                    turn(TURNS - 1, None)

                @block.vector
                def _(dve):
                    v = nc.vector

                    def layernorm(src, out, it, n):
                        steps = Chain((ln_first, ln_second)[n], dve, it)
                        for u in range(U):
                            if n == 0:
                                dve.wait_ge(x_in.sem, x_in.at(it, U))
                            steps.done(v.bn_stats(stats[:, u], src[:, u]))
                            carry(nc, c)
                            steps.done(v.bn_aggr(mv[:, u], stats[:, u]))
                        v.tensor_scalar(var[:], mv[:, :, 1], LN_EPS, None, ALU.add).then_inc(var_ready[n].sem, 1)
                        dve.wait_ge(rstd_ready[n].sem, rstd_ready[n].at(it, 1))
                        for u in range(U):
                            v.tensor_scalar(out[:, u], src[:, u], mv[:, u, 0:1], rstd[:, u:u + 1],
                                            ALU.subtract, ALU.mult).then_inc(xn_ready[n].sem, 1)
                        if n == 1:
                            v.tensor_copy(mean_all[:, bass.ds(it * U, U)], mv[:, :, 0])
                            v.tensor_copy(rstd_all[:, bass.ds(it * U, U)], rstd[:])
                        steps.close()

                    def add_bias(it, u):
                        dve.wait_ge(v_ps.sem, v_ps.at(it, u + 1))
                        v.tensor_tensor(vals[:, u], ps[:, u, 0, D:2 * D], bv[:], ALU.add).then_inc(v_sb.sem, 1)

                    def mask_scores(it):
                        chain = Chain(score_step, dve, it)
                        for u in range(U):
                            dve.wait_ge(s_ps.sem, s_ps.at(it, u + 1))
                            for r in range(4):
                                last = v.scalar_tensor_tensor(s[:, u, r:H:4], ps[:, u, r, 0:2 * P].rearrange("p (h k) -> p h k", h=2),
                                                              SCALE, c["adj_off"][:].unsqueeze(1).to_broadcast([P, 2, P]),
                                                              ALU.mult, ALU.add)
                            chain.done(last)
                            v.tensor_reduce(neg_max[:, u], s[:, u], AX.X, ALU.max, negate=True).then_inc(s_ready.sem, 1)
                            if u + 1 < U:
                                add_bias(it, u + 1)
                        chain.close()

                    def turn(it, following):
                        chain = Chain(dve_step, dve, it)
                        if following is not None:
                            layernorm(x, xn, following, 0)
                        for u in range(U):
                            dve.wait_ge(pv_ps.sem, pv_ps.at(it, u + 1))
                            chain.done(v.reciprocal(prec[:, u], psum[:, u]))
                            v.tensor_tensor(ao[:, u].rearrange("p (h d) -> p h d", d=D1), ps[:, u, 2, 0:D].rearrange("p (h d) -> p h d", d=D1),
                                            prec[:, u].unsqueeze(2).to_broadcast([P, H, D1]), ALU.mult).then_inc(ao_ready.sem, 1)
                        dve.wait_ge(xb_ready.sem, xb_ready.at(it, U))
                        for u in range(U):
                            dve.wait_ge(out_ps.sem, out_ps.at(it, u + 1))
                            v.tensor_tensor(acc[:, bass.ds(it * U + u, 1)].rearrange("p a d -> p (a d)"), ps[:, u, 2, D:2 * D], xb[:, u], ALU.add)
                            v.tensor_tensor(x3[:, u], ps[:, u, 2, D:2 * D], xb[:, u], ALU.add).then_inc(out_added.sem, 1)
                        dve.wait_ge(out_added.sem, out_added.at(it, U))
                        layernorm(x3, x3n, it, 1)
                        if following is not None:
                            add_bias(following, 0)
                            mask_scores(following)
                        for u in range(U):
                            dve.wait_ge(sig_ready.sem, sig_ready.at(it, u + 1))
                            chain.done(v.tensor_scalar(sig_d[:, u], sig_e[:, u], 1.0, None, ALU.add))
                            chain.done(v.reciprocal(sig[:, u], sig_d[:, u]))
                            carry(nc, c)
                            chain.done(v.max(top[:, u], sig[:, u]))
                            carry(nc, c)
                            chain.done(v.max_index(top_i[:, u], top[:, u], sig[:, u]))
                            v.tensor_copy(weights[:, bass.ds(it * U + u, 1)].rearrange("p a c -> p (a c)"), top[:, u, 0:2])
                            v.tensor_copy(chosen[:, bass.ds(it * U + u, 1)].rearrange("p a c -> p (a c)"), top_i[:, u, 0:2]).then_inc(routed.sem, 1)
                        chain.close()

                    layernorm(x, xn, 0, 0)
                    dve.wait_ge(w_in, 16 * 9)
                    add_bias(0, 0)
                    mask_scores(0)
                    with dve.Fori(0, TURNS - 1) as it:
                        turn(it, it + 1)
                    turn(TURNS - 1, None)
                    dve.wait_ge(routed.sem, routed.at(TURNS, 0))

        sb = sb_in(ctx)
        SLOTS = 4
        SIDES = 2
        STEP = SLOTS * SIDES
        keys = sb("e_keys", [P, 2, E1, H1])
        values = sb("e_values", [P, E1, D])
        end = sb("e_end", [P, E1])
        row_of = sb("e_row_of", [P, NB, 2], U32)
        ps = ctx.enter_context(nc.psum_tensor("e_ps", [P, SIDES, 4, 512], F32))
        values_in = ctx.enter_context(nc.semaphore("e_values_in"))

        with ExitStack() as ranking:
            sb = sb_in(ranking)
            WIDE = min(512, NB * E1)
            onehot = sb("e_onehot", [P, 2, NB, E1])
            picked = sb("e_picked", [P, NB * E1], BF16)
            sums = sb("e_sums", [P, 2, NB, E1])
            rank = sb("e_rank", [P, NB, E1])
            more = sb("e_more", [P, E1, NB])
            tiles = sb("e_tiles", [P, E1])
            earlier = sb("e_earlier", [P, E1, E1])
            start = sb("e_start", [P, E1])
            row_f = sb("e_row_f", [P, 2, NB])
            picked_ready = count("picked_ready", 1)
            ranks_ps = count("ranks_ps", 1)
            ranked = count("ranked", R_DVE_STEPS + (NB - 1).bit_length())

            with nc.Block() as block:
                @block.sync
                def _(sp):
                    for k in range(2):
                        for e in range(0, E1, 8):
                            sp.dma_start(keys[:, k, e:e + 8],
                                         dram["L1_ffn_keys"][e:e + 8, P * k:P * k + P].rearrange("n p f -> p n f")).then_inc(values_in, 16)
                    sp.dma_start(values[:], dram["L1_ffn_values"].rearrange("n p f -> p n f")).then_inc(values_in, 16)

                @block.tensor
                def _(pe):
                    mm = nc.tensor.matmul
                    pe.wait_ge(picked_ready.sem, picked_ready.at(0, 1))
                    for n, lhs in enumerate((c["before"], c["ones_bf"])):
                        for q in range(NB * E1 // WIDE):
                            last = mm(ps[:, n, q, 0:WIDE], lhs[:], picked[:, WIDE * q:WIDE * q + WIDE], start=True, stop=True)
                    last.then_inc(ranks_ps.sem, 1)

                @block.vector
                def _(dve):
                    v = nc.vector
                    steps = Chain(ranked, dve, 0)
                    numbers = c["row0"][:, 0:E1]
                    for n in range(2):
                        last = v.tensor_tensor(onehot[:, n], numbers.unsqueeze(1).to_broadcast([P, NB, E1]),
                                               chosen[:, :, n:n + 1].to_broadcast([P, NB, E1]), ALU.is_equal)
                    steps.done(last)
                    v.tensor_tensor(picked[:].rearrange("p (b e) -> p b e", e=E1), onehot[:, 0], onehot[:, 1], ALU.add).then_inc(picked_ready.sem, 1)
                    v.tensor_tensor(earlier[:], numbers.unsqueeze(2).to_broadcast([P, E1, E1]), numbers.unsqueeze(1).to_broadcast([P, E1, E1]), ALU.is_gt)
                    dve.wait_ge(ranks_ps.sem, ranks_ps.at(0, 1))
    
                    def counted(n):
                        return ps[:, n].rearrange("p c f -> p (c f)")[:, 0:NB * E1]
    
                    flat = "p b e -> p (b e)"
                    steps.done(v.tensor_copy(sums[:, 0].rearrange(flat), counted(1)))
                    steps.done(v.tensor_tensor(rank[:].rearrange(flat), counted(0), sums[:, 0].rearrange(flat), ALU.subtract))
                    reach, at = 1, 0
                    while reach < NB:
                        v.tensor_copy(sums[:, 1 - at, 0:reach], sums[:, at, 0:reach])
                        steps.done(v.tensor_tensor(sums[:, 1 - at, reach:NB], sums[:, at, reach:NB], sums[:, at, 0:NB - reach], ALU.add))
                        reach, at = 2 * reach, 1 - at
                    steps.done(v.scalar_tensor_tensor(more[:], c["row0"][:, 0:NB].unsqueeze(1).to_broadcast([P, E1, NB]), float(P),
                                                      sums[:, at, NB - 1].unsqueeze(2).to_broadcast([P, E1, NB]), ALU.mult, ALU.is_lt))
                    steps.done(v.tensor_reduce(tiles[:], more[:], AX.X, ALU.add))
                    steps.done(v.tensor_tensor(earlier[:], earlier[:], tiles[:].unsqueeze(1).to_broadcast([P, E1, E1]), ALU.mult))
                    steps.done(v.tensor_reduce(start[:], earlier[:], AX.X, ALU.add))
                    v.tensor_tensor(end[:], start[:], tiles[:], ALU.add)
                    steps.done(v.tensor_tensor(rank[:], rank[:], sums[:, at], ALU.add))
                    steps.done(v.scalar_tensor_tensor(rank[:], start[:].unsqueeze(1).to_broadcast([P, NB, E1]), float(P), rank[:], ALU.mult, ALU.add))
                    for n in range(2):
                        last = v.tensor_tensor(onehot[:, n], onehot[:, n], rank[:], ALU.mult)
                    steps.done(last)
                    steps.done(v.tensor_reduce(row_f[:], onehot[:], AX.X, ALU.add))
                    steps.done(v.tensor_copy(row_of[:], row_f[:].rearrange("p n b -> p b n")))
                    steps.close()

        sb = sb_in(ctx)
        passed = sb("e_passed", [1, TILES, E1])
        expert_f = sb("e_expert_f", [1, TILES])
        expert_of = sb("e_expert_of", [1, TILES], I32)
        now = sb("e_now", [P, SIDES, SLOTS, 2], U32)
        tile_x = sb("e_tile_x", [P, SIDES, SLOTS, D])
        tile_xT = sb("e_tile_xT", [P, SIDES, SLOTS, 2, P])
        hidden = sb("e_hidden", [P, SIDES, SLOTS, H1])
        hiddenT = sb("e_hiddenT", [P, SIDES, SLOTS, P])
        tile_y = sb("e_tile_y", [P, SIDES, SLOTS, D])
        got = [tile_x, tile_y]
        before_experts = len(counts)
        numbered = count("numbered", 2)
        expert_ready = count("expert_ready", 1)
        staged = count("staged", SIDES)
        scattered = [count("scattered%d" % n, 2 * SLOTS, 16) for n in range(SIDES)]
        tiles_in = [count("tiles_in%d" % n, 1, 16) for n in range(SIDES)]
        xT_ps = count("xT_ps", SIDES)
        xT_sb = count("xT_sb", SIDES)
        hidden_ps = count("hidden_ps", SIDES)
        hidden_sb = count("hidden_sb", SIDES)
        hiddenT_ps = count("hiddenT_ps", SIDES)
        hiddenT_sb = count("hiddenT_sb", SIDES)
        y_ps = count("y_ps", SIDES)
        y_sb = [count("y_sb%d" % n, 1, again=True) for n in range(SIDES)]
        y_out = [count("y_out%d" % n, 1, 16) for n in range(SIDES)]
        addressed = count("addressed", SIDES)
        gathered = [count("gathered%d" % n, 2 * SLOTS, 16) for n in range(SIDES)]
        half_added = count("half_added", SIDES)
        added = count("added", SIDES)
        stored = count("stored", SIDES, 16)
        expert_counts = counts[before_experts:]
        SORT_TURNS, TILE_TURNS = NB // STEP, TILES // STEP

        with nc.Block() as block:
            @block.sync
            def _(sp):
                start_at_one(sp, expert_counts)

                def load(it):
                    for side in range(SIDES):
                        if not isinstance(it, int):
                            sp.wait_ge(xT_ps.sem, xT_ps.at(it - 1, side + 1))
                            hold(sp)
                        sp.dma_start(tile_x[:, side], dram["sorted_x"][bass.ds(it * STEP + side * SLOTS, SLOTS)].rearrange("q p d -> p q d")).then_inc(tiles_in[side].sem, 16)

                def turn(it, following):
                    if following is not None:
                        load(following)
                    for side in range(SIDES):
                        sp.wait_ge(y_sb[side].sem, y_sb[side].at(it, 1))
                        hold(sp)
                        sp.dma_start(dram["sorted_y"][bass.ds(it * STEP + side * SLOTS, SLOTS)].rearrange("q p d -> p q d"),
                                     tile_y[:, side]).then_inc(y_out[side].sem, 16)

                for side in range(SIDES):
                    sp.wait_ge(scattered[side].sem, scattered[side].at(SORT_TURNS, 0))
                load(0)
                with sp.Fori(0, TILE_TURNS - 1) as it:
                    turn(it, it + 1)
                turn(TILE_TURNS - 1, None)
                with sp.Fori(0, SORT_TURNS) as it:
                    for side in range(SIDES):
                        sp.wait_ge(added.sem, added.at(it, side + 1))
                        hold(sp)
                        b = bass.ds(it * STEP + side * SLOTS, SLOTS)
                        sp.dma_start(dram["out"][b].rearrange("b p d -> p b d"), acc[:, b]).then_inc(stored.sem, 16)
                sp.wait_ge(stored.sem, stored.at(SORT_TURNS, 0))

            @block.tensor
            def _(pe):
                mm, tr = nc.tensor.matmul, nc.tensor.transpose
                pe.wait_ge(values_in, 16 * (2 * E1 // 8 + 1))
                pe.wait_ge(expert_ready.sem, expert_ready.at(0, 1))
                with pe.Fori(0, TILE_TURNS) as it:
                    _, expert = nc.values_load_multi_w_load_instructions(
                        expert_of[0:1, bass.ds(it * STEP, STEP)], engines=[pe.engine], min_val=0, max_val=E1 - 1,
                        skip_runtime_bounds_check_because="expert_of is at most E1 - 1")
                    for side in range(SIDES):
                        pe.wait_ge(tiles_in[side].sem, tiles_in[side].at(it, 1))
                        pe.wait_ge(y_sb[side].sem, y_sb[side].at(it, 0))
                        for q in range(SLOTS):
                            for k in range(2):
                                last = tr(ps[:, side, q // 2, 2 * P * (q % 2) + P * k:2 * P * (q % 2) + P * k + P],
                                          tile_x[:, side, q, P * k:P * k + P], c["ident"][:])
                        last.then_inc(xT_ps.sem, 1)
                    for side in range(SIDES):
                        pe.wait_ge(xT_sb.sem, xT_sb.at(it, side + 1))
                        for q in range(SLOTS):
                            e = expert[side * SLOTS + q]
                            for k in range(2):
                                last = mm(ps[:, side, 2, H1 * q:H1 * q + H1], tile_xT[:, side, q, k],
                                          keys[:, k, bass.ds(e, 1)].rearrange("p a f -> p (a f)"), start=k == 0, stop=k == 1)
                        last.then_inc(hidden_ps.sem, 1)
                    for side in range(SIDES):
                        pe.wait_ge(hidden_sb.sem, hidden_sb.at(it, side + 1))
                        for q in range(SLOTS):
                            last = tr(ps[:, side, 3, P * q:P * q + P], hidden[:, side, q], c["ident"][:])
                        last.then_inc(hiddenT_ps.sem, 1)
                    for side in range(SIDES):
                        pe.wait_ge(hiddenT_sb.sem, hiddenT_sb.at(it, side + 1))
                        for q in range(SLOTS):
                            e = expert[side * SLOTS + q]
                            last = mm(ps[:, side, q // 2, D * (q % 2):D * (q % 2) + D], hiddenT[:, side, q],
                                      values[:, bass.ds(e, 1)].rearrange("p a f -> p (a f)"), start=True, stop=True)
                        last.then_inc(y_ps.sem, 1)

            @block.scalar
            def _(act):
                a = nc.scalar
                with act.Fori(0, TILE_TURNS) as it:
                    for side in range(SIDES):
                        act.wait_ge(xT_ps.sem, xT_ps.at(it, side + 1))
                        a.activation(tile_xT[:, side].rearrange("p q k t -> p (q k t)"), ps[:, side, 0:2].rearrange("p b f -> p (b f)"), ACT.Copy).then_inc(xT_sb.sem, 1)
                    for side in range(SIDES):
                        act.wait_ge(hiddenT_ps.sem, hiddenT_ps.at(it, side + 1))
                        a.activation(hiddenT[:, side].rearrange("p q t -> p (q t)"), ps[:, side, 3], ACT.Copy).then_inc(hiddenT_sb.sem, 1)

            @block.gpsimd
            def _(pool):
                g = nc.gpsimd
                with pool.Fori(0, SORT_TURNS) as it:
                    for side in range(SIDES):
                        pool.wait_ge(staged.sem, staged.at(it, side + 1))
                        hold(pool)
                        for q in range(SLOTS):
                            for n in range(2):
                                g.indirect_dma_start(xs_rows, bass.IndirectOffsetOnAxis(ap=now[:, side, q, n:n + 1], axis=0),
                                                     tile_x[:, side, q], None).then_inc(scattered[side].sem, 16)
                for side in range(SIDES):
                    pool.wait_ge(y_out[side].sem, y_out[side].at(TILE_TURNS, 0))
                with pool.Fori(0, SORT_TURNS) as it:
                    for side in range(SIDES):
                        pool.wait_ge(addressed.sem, addressed.at(it, side + 1))
                        hold(pool)
                        for q in range(SLOTS):
                            for n in range(2):
                                g.indirect_dma_start(got[n][:, side, q], None, ys_rows,
                                                     bass.IndirectOffsetOnAxis(ap=now[:, side, q, n:n + 1], axis=0)).then_inc(gathered[side].sem, 16)

            @block.vector
            def _(dve):
                v = nc.vector
                def stage(it, before):
                    for side in range(SIDES):
                        if before is not None:
                            dve.wait_ge(scattered[side].sem, scattered[side].at(before, 2 * SLOTS))
                        for q in range(SLOTS):
                            b = bass.ds(it * STEP + side * SLOTS + q, 1)
                            v.tensor_scalar(tile_x[:, side, q], acc[:, b].rearrange("p a d -> p (a d)"), mean_all[:, b], rstd_all[:, b],
                                            ALU.subtract, ALU.mult)
                        v.tensor_copy(now[:, side], row_of[:, bass.ds(it * STEP + side * SLOTS, SLOTS)]).then_inc(staged.sem, 1)

                stage(0, None)
                with dve.Fori(1, SORT_TURNS) as it:
                    stage(it, it - 1)

                steps = Chain(numbered, dve, 0)
                steps.done(v.tensor_tensor(passed[:], c["row0"][0:1, 0:TILES].unsqueeze(2).to_broadcast([1, TILES, E1]),
                                           end[0:1].unsqueeze(1).to_broadcast([1, TILES, E1]), ALU.is_ge))
                steps.done(v.tensor_reduce(expert_f[:], passed[:], AX.X, ALU.add))
                v.tensor_scalar(expert_of[:], expert_f[:], float(E1 - 1), None, ALU.min).then_inc(expert_ready.sem, 1)
                steps.close()

                def leave(it, before):
                    for side in range(SIDES):
                        dve.wait_ge(hidden_ps.sem, hidden_ps.at(it, side + 1))
                        v.tensor_scalar(hidden[:, side].rearrange("p q f -> p (q f)"), ps[:, side, 2], 0.0, None, ALU.max).then_inc(hidden_sb.sem, 1)
                    for side in range(SIDES):
                        if before is not None:
                            dve.wait_ge(y_out[side].sem, y_out[side].at(before, 1))
                        dve.wait_ge(y_ps.sem, y_ps.at(it, side + 1))
                        v.tensor_copy(tile_y[:, side].rearrange("p q f -> p (q f)"), ps[:, side, 0:2].rearrange("p b f -> p (b f)")).then_inc(y_sb[side].sem, 1)

                leave(0, None)
                with dve.Fori(1, TILE_TURNS) as it:
                    leave(it, it - 1)

                def address(it, side):
                    v.tensor_copy(now[:, side], row_of[:, bass.ds(it * STEP + side * SLOTS, SLOTS)]).then_inc(addressed.sem, 1)

                def add(it, side, following):
                    dve.wait_ge(gathered[side].sem, gathered[side].at(it, 2 * SLOTS))
                    for n, semaphore in enumerate((half_added, added)):
                        for q in range(SLOTS):
                            b = bass.ds(it * STEP + side * SLOTS + q, 1)
                            y = acc[:, b].rearrange("p a d -> p (a d)")
                            w = weights[:, b, n:n + 1].rearrange("p a c -> p (a c)")
                            last = v.scalar_tensor_tensor(y, got[n][:, side, q], w, y, ALU.mult, ALU.add)
                        last.then_inc(semaphore.sem, 1)
                        if n == 0:
                            dve.wait_ge(half_added.sem, half_added.at(it, side + 1))
                    if following is not None:
                        address(following, side)

                for side in range(SIDES):
                    dve.wait_ge(y_out[side].sem, y_out[side].at(TILE_TURNS, 0))
                for side in range(SIDES):
                    address(0, side)
                with dve.Fori(0, SORT_TURNS - 1) as it:
                    for side in range(SIDES):
                        add(it, side, it + 1)
                for side in range(SIDES):
                    add(SORT_TURNS - 1, side, None)


def program(nc, ins, out):
    dram = dict(ins)
    NB = ins["x"].shape[0]
    dram["out"] = out

    def scratch(name, shape, dt=F32):
        dram[name] = nc.dram_tensor("scratch_" + name, shape, dt, kind="Internal").ap()

    scratch("x1", [NB, P, D])
    scratch("gate", [NB, P, HD])
    scratch("mask", [NB, P, 2, P], BF16)
    scratch("krow", [NB, P, HD])
    scratch("edge", [NB, P, 2, H])
    scratch("perm", [NB, P, 2, P])
    scratch("rowg", [NB, P, 2, H])
    scratch("rowb", [NB, P, 2, H])
    scratch("roww", [NB, P, 2])
    scratch("vp", [NB, P, 2, HD])
    scratch("kqT", [NB, P, 2, 4, R])
    scratch("acomp", [NB, P, 2, H, BK])
    scratch("x2", [NB, P, D])
    scratch("inv", [NB, P, 2, H, BK])
    scratch("sorted_x", [2 * NB + E1, P, D])
    scratch("sorted_y", [2 * NB + E1, P, D])
    with ExitStack() as ctx:
        c = constants(nc, ctx, dram)
        phase_rows(nc, c, dram, NB)
        phase_invert(nc, c, dram, NB)
        phase_mix(nc, c, dram, NB)
        phase_experts(nc, c, dram, NB)


TRANSPOSED = ("L1_gnn_Wq", "L1_gnn_Wk", "L1_gnn_Wv", "L1_gnn_Wo", "L1_ffn_expert_sel")


def kernel(**inputs):
    import concourse.bacc as bacc
    from concourse.bass_utils import run_bass_kernel_spmd

    nc = bacc.Bacc("TRN2", target_bir_lowering=False, num_devices=1)
    arrays, ins = {}, {}
    for name, a in inputs.items():
        a = np.asarray(a)
        a = np.ascontiguousarray(a.T if name in TRANSPOSED else a)
        arrays["in_" + name] = a
        ins[name] = nc.dram_tensor("in_" + name, a.shape, mybir.dt.from_np(a.dtype), kind="ExternalInput").ap()
    out = nc.dram_tensor("out", inputs["x"].shape, F32, kind="ExternalOutput").ap()
    program(nc, ins, out)
    r = run_bass_kernel_spmd(nc, [arrays], core_ids=[0])
    return r.results[0]["out"]
```
